# Optimizing a Trainium2 kernel written in Bass

```python
import numpy as np
import jax
import jax.numpy as jnp

def _softmax(x, axis=-1):
    return jax.nn.softmax(x, axis=axis)

def _gelu(x):
    return jax.nn.gelu(x, approximate=True)

def _silu(x):
    return jax.nn.silu(x)

def _sigmoid(x):
    return jax.nn.sigmoid(x)

def _layernorm(x, axis=-1, eps=1e-05):
    m = jnp.mean(x, axis=axis, keepdims=True)
    v = jnp.var(x, axis=axis, keepdims=True)
    return (x - m) / jnp.sqrt(v + eps)

def _scatter_add(tgt, idx, src, axis=0):
    return tgt.at[idx].add(src)

def _segment_sum(src, seg, n):
    return jax.ops.segment_sum(src, seg, n)
kernel_name = 'mk_gnn_resnorm_d4_gnn_r8_bff6a4'

def setup_inputs(seed: int=0):
    np.random.seed(seed)
    _w = jnp.asarray

    def _rec_inputs():
        import jax
        import jax.numpy as jnp
        _gk = jax.random.key(seed)
        x = -0.000202 + 1 * jax.random.normal(jax.random.fold_in(_gk, 1), (6250, 128), jnp.float32)
        _s = jax.random.randint(jax.random.fold_in(_gk, 2), (50000,), 0, 6250, jnp.int32)
        _d = jax.random.randint(jax.random.fold_in(_gk, 3), (50000,), 0, 6250, jnp.int32)
        _loop = jnp.arange(6250, dtype=jnp.int32)
        src = jnp.concatenate([_s, _d, _loop])
        dst = jnp.concatenate([_d, _s, _loop])
        _o = jnp.argsort(dst, stable=True)
        src = src[_o]
        dst = dst[_o]
        edge_weight1 = jax.random.uniform(jax.random.fold_in(_gk, 13), (106250, 1), jnp.float32, 0.0, 1)
        return (x, src, dst, edge_weight1)
    x, src, dst, edge_weight1 = _rec_inputs()

    def _L0_gnn_setup():
        import jax, jax.numpy as jnp
        import numpy as np
        N_NODES = 6250

        def _gin_conv(x, src, dst, W_a, b_a, W_b, b_b):
            agg = jax.ops.segment_sum(x[src], dst, num_segments=N_NODES)
            h = x + agg
            h = jax.nn.relu(h @ W_a + b_a)
            return h @ W_b + b_b
        key = jax.random.key(seed)
        ks = jax.random.split(key, 6)
        d = 128
        E = 100000
        s = 1.0 / np.sqrt(d)
        return {'x': jax.random.normal(ks[0], (N_NODES, d), dtype=jnp.float32), 'edge_index': jax.random.randint(ks[1], (2, E), 0, N_NODES, dtype=jnp.int64), 'W1': jax.random.normal(ks[2], (d, d), dtype=jnp.float32) * s, 'b1': jnp.zeros((d,), dtype=jnp.float32), 'W2': jax.random.normal(ks[3], (d, d), dtype=jnp.float32) * s, 'b2': jnp.zeros((d,), dtype=jnp.float32), 'W3': jax.random.normal(ks[4], (d, d), dtype=jnp.float32) * s, 'b3': jnp.zeros((d,), dtype=jnp.float32), 'W4': jax.random.normal(ks[5], (d, d), dtype=jnp.float32) * s, 'b4': jnp.zeros((d,), dtype=jnp.float32)}
    _L0_gnn_all = _L0_gnn_setup()
    _L0_gnn_in = {k: v for k, v in _L0_gnn_all.items() if k in ('W1', 'b1', 'W2', 'b2', 'W3', 'b3', 'W4', 'b4')}
    del _L0_gnn_all

    def _L1_gnn_setup():
        import jax, jax.numpy as jnp
        import numpy as np
        N_NODES = 12500
        N_EDGES = 78125
        D_FEAT = 128
        OUT_DIM = 128
        key = jax.random.key(seed)
        k1, k2, k3, k4 = jax.random.split(key, 4)
        feature = jax.random.normal(k1, (N_NODES, D_FEAT), dtype=jnp.float32)
        relation_weight = jax.random.uniform(k2, (N_EDGES, 1), dtype=jnp.float32)
        relation_indices = jax.random.randint(k3, (2, N_EDGES), 0, N_NODES, dtype=jnp.int32)
        W = jax.random.normal(k4, (2 * D_FEAT, OUT_DIM), dtype=jnp.float32) * 0.05
        b = jnp.zeros((OUT_DIM,), dtype=jnp.float32)
        return {'feature': feature, 'relation_weight': relation_weight, 'W': W, 'b': b, 'relation_indices': relation_indices}
    _L1_gnn_all = _L1_gnn_setup()
    _L1_gnn_in = {k: v for k, v in _L1_gnn_all.items() if k in ('W', 'b')}
    del _L1_gnn_all

    def _L2_gnn_setup():
        import jax, jax.numpy as jnp
        import numpy as np
        N = 12500
        E = 125000
        D = 128
        OUT = 128
        key = jax.random.key(seed)
        k1, k2, k3, k4, k5 = jax.random.split(key, 5)
        feats = jax.random.normal(k1, (N, D), dtype=jnp.float32)
        src = jax.random.randint(k2, (E,), 0, N, dtype=jnp.int32)
        dst = jax.random.randint(k3, (E,), 0, N, dtype=jnp.int32)
        W = jax.random.normal(k4, (OUT, 3 * D), dtype=jnp.float32) * np.float32(1.0 / np.sqrt(3 * D))
        b = jax.random.normal(k5, (OUT,), dtype=jnp.float32) * np.float32(0.01)
        return {'feats': feats, 'W': W, 'b': b, 'src': src, 'dst': dst}
    _L2_gnn_all = _L2_gnn_setup()
    _L2_gnn_in = {k: v for k, v in _L2_gnn_all.items() if k in ('W', 'b')}
    del _L2_gnn_all

    def _L3_gnn_setup():
        import jax, jax.numpy as jnp
        import numpy as np
        N, E, C = (12500, 200000, 128)
        EPS = 1e-05

        def _bn(x, g, b):
            mu = jnp.mean(x, axis=0)
            var = jnp.mean((x - mu) ** 2, axis=0)
            return g * (x - mu) * jax.lax.rsqrt(var + EPS) + b
        key = jax.random.key(seed)
        ks = jax.random.split(key, 8)
        s = 1.0 / np.sqrt(C)
        return {'h': jax.random.normal(ks[0], (N, C), jnp.float32), 'src': jax.random.randint(ks[1], (E,), 0, N, jnp.int32), 'dst': jax.random.randint(ks[2], (E,), 0, N, jnp.int32), 'theta_w': jax.random.normal(ks[3], (C, C), jnp.float32) * s, 'phi_w': jax.random.normal(ks[4], (C, C), jnp.float32) * s, 'fc1_w': jax.random.normal(ks[5], (C, C), jnp.float32) * s, 'bn0_g': jnp.ones((C,), jnp.float32), 'bn0_b': jnp.zeros((C,), jnp.float32), 'bn1_g': jnp.ones((C,), jnp.float32), 'bn1_b': jnp.zeros((C,), jnp.float32)}
    _L3_gnn_all = _L3_gnn_setup()
    _L3_gnn_in = {k: v for k, v in _L3_gnn_all.items() if k in ('theta_w', 'phi_w', 'fc1_w', 'bn0_g', 'bn0_b', 'bn1_g', 'bn1_b')}
    del _L3_gnn_all
    return {'x': x, 'src': src, 'dst': dst, 'edge_weight1': edge_weight1, 'L0_gnn_W1': _L0_gnn_in['W1'], 'L0_gnn_b1': _L0_gnn_in['b1'], 'L0_gnn_W2': _L0_gnn_in['W2'], 'L0_gnn_b2': _L0_gnn_in['b2'], 'L0_gnn_W3': _L0_gnn_in['W3'], 'L0_gnn_b3': _L0_gnn_in['b3'], 'L0_gnn_W4': _L0_gnn_in['W4'], 'L0_gnn_b4': _L0_gnn_in['b4'], 'L1_gnn_W': _L1_gnn_in['W'], 'L1_gnn_b': _L1_gnn_in['b'], 'L2_gnn_W': _L2_gnn_in['W'], 'L2_gnn_b': _L2_gnn_in['b'], 'L3_gnn_theta_w': _L3_gnn_in['theta_w'], 'L3_gnn_phi_w': _L3_gnn_in['phi_w'], 'L3_gnn_fc1_w': _L3_gnn_in['fc1_w'], 'L3_gnn_bn0_g': _L3_gnn_in['bn0_g'], 'L3_gnn_bn0_b': _L3_gnn_in['bn0_b'], 'L3_gnn_bn1_g': _L3_gnn_in['bn1_g'], 'L3_gnn_bn1_b': _L3_gnn_in['bn1_b']}

def reference(x, src, dst, edge_weight1, L0_gnn_W1, L0_gnn_b1, L0_gnn_W2, L0_gnn_b2, L0_gnn_W3, L0_gnn_b3, L0_gnn_W4, L0_gnn_b4, L1_gnn_W, L1_gnn_b, L2_gnn_W, L2_gnn_b, L3_gnn_theta_w, L3_gnn_phi_w, L3_gnn_fc1_w, L3_gnn_bn0_g, L3_gnn_bn0_b, L3_gnn_bn1_g, L3_gnn_bn1_b):
    import jax
    import jax.numpy as jnp

    def _L0_gnn_ref(x, edge_index, W1, b1, W2, b2, W3, b3, W4, b4):
        import jax, jax.numpy as jnp
        import numpy as np
        N_NODES = 6250

        def _gin_conv(x, src, dst, W_a, b_a, W_b, b_b):
            agg = jax.ops.segment_sum(x[src], dst, num_segments=N_NODES)
            h = x + agg
            h = jax.nn.relu(h @ W_a + b_a)
            return h @ W_b + b_b
        src, dst = (edge_index[0], edge_index[1])
        h = jax.nn.relu(_gin_conv(x, src, dst, W1, b1, W2, b2))
        out = _gin_conv(h, src, dst, W3, b3, W4, b4)
        return out

    def _L1_gnn_ref(feature, relation_weight, W, b, relation_indices):
        import jax, jax.numpy as jnp
        import numpy as np
        N_NODES = 12500
        N_EDGES = 78125
        D_FEAT = 128
        OUT_DIM = 128
        dst = relation_indices[0]
        src = relation_indices[1]
        n = feature.shape[0]
        feat_n = feature[src] * relation_weight
        seg_sum = jax.ops.segment_sum(feat_n, dst, num_segments=n)
        seg_cnt = jax.ops.segment_sum(jnp.ones((src.shape[0], 1), feat_n.dtype), dst, num_segments=n)
        neigh_mean = seg_sum / jnp.maximum(seg_cnt, 1.0)
        h = jnp.concatenate([feature, neigh_mean], axis=-1)
        return h @ W + b

    def _L2_gnn_ref(feats, W, b, src, dst):
        import jax, jax.numpy as jnp
        import numpy as np
        N = 12500
        E = 125000
        D = 128
        OUT = 128
        n = feats.shape[0]
        msg_sum = jax.ops.segment_sum(feats[src], dst, num_segments=n)
        deg = jax.ops.segment_sum(jnp.ones(src.shape, feats.dtype), dst, num_segments=n)
        h = msg_sum / jnp.maximum(deg, 1.0)[:, None]
        concat_ftrs = jnp.concatenate([feats, h, feats], axis=1)
        ftrs = jnp.tanh(concat_ftrs @ W.T + b)
        ftrs = ftrs / jnp.linalg.norm(ftrs)
        return ftrs

    def _L3_gnn_ref(h, src, dst, theta_w, phi_w, fc1_w, bn0_g, bn0_b, bn1_g, bn1_b):
        import jax, jax.numpy as jnp
        import numpy as np
        N, E, C = (12500, 200000, 128)
        EPS = 1e-05

        def _bn(x, g, b):
            mu = jnp.mean(x, axis=0)
            var = jnp.mean((x - mu) ** 2, axis=0)
            return g * (x - mu) * jax.lax.rsqrt(var + EPS) + b
        n = h.shape[0]
        x_src = h[src]
        x_dst = h[dst]
        e = (x_dst - x_src) @ theta_w.T + x_src @ phi_w.T
        e = jax.nn.relu(_bn(e, bn0_g, bn0_b))
        e = e @ fc1_w.T
        e = jax.nn.relu(_bn(e, bn1_g, bn1_b))
        agg = jax.ops.segment_sum(e, dst, num_segments=n)
        cnt = jax.ops.segment_sum(jnp.ones((e.shape[0],), e.dtype), dst, num_segments=n)
        x = agg / jnp.maximum(cnt, 1.0)[:, None]
        return jax.nn.relu(x + h)
    edge_index = jnp.stack([src, dst])
    x = _layernorm(x + _L0_gnn_ref(x, edge_index, L0_gnn_W1, L0_gnn_b1, L0_gnn_W2, L0_gnn_b2, L0_gnn_W3, L0_gnn_b3, L0_gnn_W4, L0_gnn_b4), axis=-1)
    x = _layernorm(x + _L1_gnn_ref(x, edge_weight1, L1_gnn_W, L1_gnn_b, edge_index), axis=-1)
    x = _layernorm(x + _L2_gnn_ref(x, L2_gnn_W, L2_gnn_b, src, dst), axis=-1)
    x = _layernorm(x + _L3_gnn_ref(x, src, dst, L3_gnn_theta_w, L3_gnn_phi_w, L3_gnn_fc1_w, L3_gnn_bn0_g, L3_gnn_bn0_b, L3_gnn_bn1_g, L3_gnn_bn1_b), axis=-1)
    return x

_drawn_inputs = setup_inputs


def setup_inputs(seed=0):
    import zlib

    import numpy as np

    out = dict(_drawn_inputs(seed))
    spreads = {'L0_gnn_b1': (0.0, 0.5),
     'L0_gnn_b2': (0.0, 0.1),
     'L0_gnn_b3': (0.0, 2.0),
     'L0_gnn_b4': (0.0, 0.8),
     'L1_gnn_b': (0.0, 0.1),
     'L3_gnn_bn0_g': (1.0, 0.6),
     'L3_gnn_bn0_b': (0.0, 0.709),
     'L3_gnn_bn1_g': (1.0, 0.2),
     'L3_gnn_bn1_b': (0.0, 0.306)}
    factors = {'L2_gnn_W': 64.0, 'L2_gnn_b': 64.0}
    for name, (base, spread) in spreads.items():
        noise = np.random.default_rng([zlib.crc32(name.encode()), seed]).standard_normal(out[name].shape)
        drawn = base * np.exp(spread * noise) if base else spread * noise
        out[name] = jnp.asarray(drawn.astype(out[name].dtype))
    for name, factor in factors.items():
        out[name] = (out[name] * factor).astype(out[name].dtype)
    return out
```

```python
from contextlib import ExitStack

import concourse.bass as bass
from concourse import mybir

F32 = mybir.dt.float32
I32 = mybir.dt.int32
ALU = mybir.AluOpType
ACT = mybir.ActivationFunctionType
AX = mybir.AxisListType

P = 128


class Count:

    def __init__(self, eng, sem, K=0, i=0):
        self.eng, self.sem, self.K, self.i, self.n = eng, sem, K, i, 0

    def inc(self, ins):
        ins.then_inc(self.sem, 1)
        self.n += 1
        return self.n

    def wait(self, n=None):
        self.eng.wait_ge(self.sem, self.i * self.K + (self.n if n is None else n))

    def link(self, ins):
        self.inc(ins)
        self.wait()

    def turn(self, i):
        assert self.n in (0, self.K)
        self.i, self.n = i, 0


def gnn_kernel(nc, x, src, dst, edge_weight1, W1, b1, W2, b2, W3, b3, W4, b4, L1W, L1b, L2W, L2b,
               theta_w, phi_w, fc1_w, bn0_g, bn0_b, bn1_g, bn1_b, out):
    N, D = x.shape
    E = src.shape[0]
    NW = -(-N // P)
    NP = NW * P
    ZROW = NP
    EC = 2 * 8 * (-(-E // (P * 16)))
    EP = E // EC
    ER = E - EP * EC
    assert D == P and EP == P - 1 and 0 < ER < EC
    U = 8
    T = (E + NW * (P - 1)) // P
    T = -(-T // (2 * U)) * 2 * U
    TT = T + 2 * U
    assert EC * P - E <= (TT - T) * P
    ITERS = T // (2 * U)
    SLOTS = T * P
    EPS = 1e-5
    CW = 7
    NCH = NW // CW
    assert NCH * CW == NW
    TAIL = N - (NW - 1) * P
    C = CW * P
    LN = 3 * CW + 1
    KB, LNB = 3 + LN, 3 + 2 * CW
    KC, LNC = 4 + LN, 4 + 2 * CW
    KD2, LND2 = 1 + LN, 1 + 2 * CW
    KF, LNF = 3 + LN, 3 + 2 * CW
    BNV = 16
    D1 = D + 1

    table = nc.dram_tensor("node_table", (NP + P, D), F32).ap()
    rec_dst = nc.dram_tensor("rec_dst", (P * TT, 2), F32).ap()
    rec_src = nc.dram_tensor("rec_src", (P * TT, 4), F32).ap()
    e_store = nc.dram_tensor("e_store", (ITERS * 2, P, U * P), F32).ap()
    table_w = table[0:NP, :].rearrange("(w p) f -> p w f", p=P)

    ctx = ExitStack()
    with ctx:
        def sb(name, shape, dt=F32):
            return ctx.enter_context(nc.sbuf_tensor(name, shape, dt))

        def sem(name):
            return ctx.enter_context(nc.semaphore(name))

        x0 = sb("x0", [P, NW, D])
        cur = sb("cur", [P, NW, D])
        acc = sb("acc", [P, NW, D1])
        deg_dst = sb("deg_dst", [P, NW])
        deg_src = sb("deg_src", [P, NW])
        rdeg = sb("rdeg", [P, NW])
        accf = acc[:, :, :].rearrange("p a b -> p (a b)")
        key_i = accf[:, 0:2 * EC].bitcast(I32).rearrange("p (k c) -> p k c", k=2)
        raw = sb("raw", [P, EC, 3])
        raw_s = sb("raw_s", [P, EC, 3])
        wgt = accf[:, 2 * EC:3 * EC]
        pos = sb("pos", [P, 2, EC], I32)
        rec = [sb("rec_d_sb", [P, TT, 2]), sb("rec_s_sb", [P, TT, 4])]
        gidx = [sb("gidx_d", [P, TT], I32), sb("gidx_s", [P, TT], I32)]
        wtile = [sb("wtile_d", [1, T], I32), sb("wtile_s", [1, T], I32)]
        winf = accf[:, 3 * EC:4 * EC]
        scratch = sb("scratch", [P, 4, C])
        mask = scratch[:, 0:2, 0:EC].bitcast(I32)
        scan = scratch[:, 2:4, 0:EC]
        posf = accf[:, 4 * EC:5 * EC]
        zeros_e = accf[:, 5 * EC:6 * EC]
        cnt = sb("cnt", [P, NW + 1])
        tot = sb("tot", [P, NW + 1])
        tiles_i = sb("tiles_i", [P, NW + 1], I32)
        tiles_f = sb("tiles_f", [P, NW + 1])
        tend = sb("tend", [P, NW + 1])
        off = sb("off", [P, NW + 1])
        wnum = sb("wnum", [P, NW + 1])
        tnum = accf[:, 6 * EC:6 * EC + T]
        wtf = sb("wtf", [P, 1, T])
        posr = sb("posr", [P, 2, U], I32)
        recr = [sb("recr_d", [P, 2, U, 2]), sb("recr_s", [P, 2, U, 4])]
        idxr = sb("idxr", [P, 2, U], I32)
        msg = sb("msg", [P, 2, U, D1])
        oh = sb("oh", [P, 2, U, P])
        ohT = sb("ohT", [P, 2, U, P])
        abuf = sb("abuf", [P, 2, U, D])
        el = raw[:, :, :].rearrange("p a b -> p (a b)")[:, 0:2 * U * P].rearrange("p (h c) -> p h c", h=2)
        rT = raw_s[:, :, :].rearrange("p a b -> p (a b)")[:, 0:2 * U * P].rearrange("p (h c) -> p h c", h=2)
        s_ring, n_ring, sT, nT = (scratch[:, n, :] for n in range(4))
        s2a = n_ring
        y = sb("y", [P, CW, D])
        lnst = sb("lnst", [P, CW, 6])
        lnmv = sb("lnmv", [P, CW, 2])
        lnsd = sb("lnsd", [P, CW])
        lnrs = sb("lnrs", [P, CW])
        ident = sb("ident", [P, P])
        upper = sb("upper", [P, P])
        ones = sb("ones", [P, P])
        col = sb("col", [P, P])
        epsc = sb("epsc", [P, 1])
        wA = [sb(f"w_{n}", [P, D]) for n in range(4)]
        bcol = [sb(f"bcol_{n}", [P, 1]) for n in (0, 2)]
        brow = [sb(f"brow_{n}", [P, D]) for n in (1, 3)]
        wL1 = sb("wL1", [P, 2, D])
        bL1 = sb("bL1", [P, D])
        wL2 = sb("wL2", [P, 3 * D])
        wL2T = sb("wL2T", [P, 3, D])
        bL2 = sb("bL2", [P, D])
        th = sb("th", [P, D])
        ph = sb("ph", [P, D])
        thphT = sb("thphT", [P, 2, D])
        fc = sb("fc", [P, D])
        fcT = sb("fcT", [P, D])
        fcs = sb("fcs", [P, D])
        fcsT = sb("fcsT", [P, D])
        bn = sb("bn", [P, 4])
        stats = ohT[:, :, :, :].rearrange("p h u c -> p (h u c)")[:, 0:ITERS * 24].rearrange("p (a b) -> p a b", b=6)
        sq = sb("sq", [P, ITERS * 2])
        small = sb("small", [P, 24])
        diag = sb("diag", [P, P])
        shrow = sb("shrow", [1, D])

        PS = ctx.enter_context(nc.psum_tensor("PS", [P, 8, 512], F32))
        psflat = PS[:, :, :].rearrange("p b c -> p (b c)")

        block = ctx.enter_context(nc.Block())

        ld_edges, ld_x, ld_w = sem("ld_edges"), sem("ld_x"), sem("ld_w")
        init, init_v = sem("init"), sem("init_v")
        filled, taken = sem("filled"), sem("taken")
        vtaken = sem("vtaken")
        tbl0 = sem("tbl0")
        keys_ready = sem("keys_ready")
        rk = [sem("rk_d"), sem("rk_s")]
        rkl = [sem("rkl_d"), sem("rkl_s")]
        rkp = [sem("rkp_d"), sem("rkp_s")]
        rkq = [sem("rkq_d"), sem("rkq_s")]
        rkw = [sem("rkw_d"), sem("rkw_s")]
        pos_ready = [sem("pos_d"), sem("pos_s")]
        wt_ready = [sem("wt_d"), sem("wt_s")]
        wt_v = [sem("wt_v_d"), sem("wt_v_s")]
        sc_ring = [sem("sc_ring_d"), sem("sc_ring_s")]
        sc_done = [[sem(f"sc_done_{k}{h}") for h in range(2)] for k in "ds"]
        rec_ld = [sem("rec_ld_d"), sem("rec_ld_s")]
        unpacked = [sem("unpacked_d"), sem("unpacked_s")]

        names = ["p1", "p2", "p3", "p4"]
        g_idx = {k: sem(f"{k}_idx") for k in names + ["p5"]}
        g_got = {k: [sem(f"{k}_got{h}") for h in range(2)] for k in names + ["p5"]}
        oh_ok = {k: [sem(f"{k}_oh{h}") for h in range(2)] for k in names + ["p5", "pc"]}
        mm_ok = {k: [sem(f"{k}_mm{h}") for h in range(2)] for k in names + ["pc"]}
        add_ok = {k: sem(f"{k}_add") for k in names + ["pc"]}
        acc_zero = sem("acc_zero")
        scaled = [sem("p3_scaled0"), sem("p3_scaled1")]

        n_pass = {k: sem(f"{k}_end") for k in "ABCDEF"}
        nv = {k: sem(f"n{k}_dve") for k in "ABCDEF"}
        na = {k: sem(f"n{k}_act") for k in "ABCDEF"}
        npe = {k: sem(f"n{k}_pe") for k in "ABCDEF"}
        nst = {k: sem(f"n{k}_store") for k in "ABCE"}
        dn_v, dn_p, dn_a = sem("norm_dve"), sem("norm_pe"), sem("norm_act")
        nv2, na2, nst2 = sem("nD2_dve"), sem("nD2_act"), sem("nD2_store")
        wt_pe, wt_dve = sem("wt_pe"), sem("wt_dve")
        q_tr = [sem("p5_tr0"), sem("p5_tr1")]
        q_a = [sem("p5_a0"), sem("p5_a1")]
        q_t = [sem("p5_t0"), sem("p5_t1")]
        q_e = [sem("p5_e0"), sem("p5_e1")]
        q_sq = [sem("p5_sq0"), sem("p5_sq1")]
        q_cp = [sem("p5_cp0"), sem("p5_cp1")]
        q_st = [sem("p5_st0"), sem("p5_st1")]
        bn_v, bn_a, bn_p = sem("bn_dve"), sem("bn_act"), sem("bn_pe")
        b_ld = [sem("b_ld0"), sem("b_ld1")]
        b_r = [sem("b_r0"), sem("b_r1")]
        b_mm = [sem("b_mm0"), sem("b_mm1")]
        b_bn = [sem("b_bn0"), sem("b_bn1")]
        c_ld = [sem("c_ld0"), sem("c_ld1")]
        c_r = [sem("c_r0"), sem("c_r1")]
        c_e = [sem("c_e0"), sem("c_e1")]
        c_y = [sem("c_y0"), sem("c_y1")]
        res_st = sem("res_st")

        scale0, mu0, mfc, sh1 = small[:, 0:1], small[:, 1:2], small[:, 2:3], small[:, 3:4]

        def cols8(i, h):
            return bass.ds(i * (2 * U) + h * U, U)

        @block.sync
        def _(sp):
            sp.wait_ge(init_v, 17)
            for k, a in ((0, dst), (1, src)):
                sp.dma_start(key_i[0:EP, k, :], a[0:EP * EC].rearrange("(p c) -> p c", p=EP)).then_inc(ld_edges, 16)
                sp.dma_start(key_i[EP:P, k, 0:ER], a[EP * EC:E].rearrange("(p c) -> p c", p=1)).then_inc(ld_edges, 16)
            w = edge_weight1.rearrange("e o -> (e o)")
            sp.dma_start(wgt[0:EP, :], w[0:EP * EC].rearrange("(p c) -> p c", p=EP)).then_inc(ld_edges, 16)
            sp.dma_start(wgt[EP:P, 0:ER], w[EP * EC:E].rearrange("(p c) -> p c", p=1)).then_inc(ld_edges, 16)
            sp.dma_start(x0[:, 0:NW - 1, :], x[0:(NW - 1) * P, :].rearrange("(w p) f -> p w f", p=P)).then_inc(ld_x, 16)
            sp.dma_start(x0[0:TAIL, NW - 1, :], x[(NW - 1) * P:N, :]).then_inc(ld_x, 16)
            for t, a in ((wA[0], W1), (wA[1], W2), (wA[2], W3), (wA[3], W4), (th, theta_w), (ph, phi_w), (fc, fc1_w)):
                sp.dma_start(t[:, :], a).then_inc(ld_w, 16)
            sp.dma_start(wL1[:, :, :], L1W.rearrange("(k p) n -> p k n", p=P)).then_inc(ld_w, 16)
            sp.dma_start(wL2[:, :], L2W).then_inc(ld_w, 16)
            for t, a in ((bcol[0][:, :], b1), (bcol[1][:, :], b3), (bn[:, 0:1], bn0_g), (bn[:, 1:2], bn0_b),
                         (bn[:, 2:3], bn1_g), (bn[:, 3:4], bn1_b)):
                sp.dma_start(t, a.rearrange("(p o) -> p o", o=1)).then_inc(ld_w, 16)
            for t, a in ((brow[0], b2), (brow[1], b4), (bL1, L1b), (bL2, L2b)):
                sp.dma_start(t[:, :], a.rearrange("(o f) -> o f", o=1).to_broadcast([P, D])).then_inc(ld_w, 16)
            sp.wait_ge(init, 6)
            sp.dma_start(rec_dst.rearrange("(p t) r -> p t r", p=P), rec[0][:, :, :]).then_inc(filled, 16)
            sp.dma_start(rec_src.rearrange("(p t) r -> p t r", p=P), rec[1][:, :, :]).then_inc(filled, 16)
            sp.dma_start(table[NP:NP + P, :], zeros_e[:, 0:D]).then_inc(tbl0, 16)
            sp.wait_ge(ld_x, 32)
            sp.dma_start(table_w, x0[:, :, :]).then_inc(tbl0, 16)
            for k, r in ((0, rec_dst), (1, rec_src)):
                for h in range(2):
                    sp.wait_ge(sc_done[k][h], EC // (2 * U) * U * 16)
                sp.dma_start(rec[k][:, :, :], r.rearrange("(p t) r -> p t r", p=P)).then_inc(rec_ld[k], 16)

            def store_chunks(ph_, ready, K, sem_, src_of):
                with sp.Fori(0, NCH) as i:
                    sp.wait_ge(ready, i * K + K)
                    sp.dma_start(table_w[:, bass.ds(i * CW, CW), :], src_of(i)).then_inc(sem_, 16)

            store_chunks("A", na["A"], 3, nst["A"], lambda i: cur[:, bass.ds(i * CW, CW), :])
            store_chunks("B", nv["B"], KB, nst["B"], lambda i: cur[:, bass.ds(i * CW, CW), :])
            store_chunks("C", nv["C"], KC, nst["C"], lambda i: cur[:, bass.ds(i * CW, CW), :])
            with sp.Fori(0, NCH) as i:
                sp.wait_ge(nv["E"], i * 3 + 2)
                sp.dma_start(table_w[:, bass.ds(i * CW, CW), :], y[:, :, :]).then_inc(nst["E"], 16)
            with sp.Fori(0, ITERS) as i:
                for h in range(2):
                    sp.wait_ge(q_cp[h], i + 1)
                    sp.dma_start(e_store[i * 2 + h, :, :], el[:, h, :]).then_inc(q_st[h], 16)
            for h in range(2):
                sp.wait_ge(q_st[h], ITERS * 16)
            with sp.Fori(0, ITERS) as i:
                for h in range(2):
                    sp.wait_ge(b_r[h], i)
                    sp.dma_start(el[:, h, :], e_store[i * 2 + h, :, :]).then_inc(b_ld[h], 16)
            for h in range(2):
                sp.wait_ge(b_r[h], ITERS)
            with sp.Fori(0, ITERS) as i:
                for h in range(2):
                    sp.wait_ge(c_r[h], i)
                    sp.dma_start(el[:, h, :], e_store[i * 2 + h, :, :]).then_inc(c_ld[h], 16)
            sp.wait_ge(nv["F"], NCH * KF)
            sp.dma_start(out[0:(NW - 1) * P, :].rearrange("(w p) f -> p w f", p=P), cur[:, 0:NW - 1, :]).then_inc(res_st, 16)
            sp.dma_start(out[(NW - 1) * P:N, :], cur[0:TAIL, NW - 1, :]).then_inc(res_st, 16)
            sp.wait_ge(res_st, 32)

        @block.gpsimd
        def _(pool):
            pool.iota(wnum[:, :], pattern=[[1, NW + 1]], base=0, channel_multiplier=0,
                      allow_small_or_imprecise_dtypes=True).then_inc(init, 1)
            pool.iota(tnum[:, :], pattern=[[1, T]], base=0, channel_multiplier=0,
                      allow_small_or_imprecise_dtypes=True).then_inc(init, 1)
            pool.iota(col[:, :], pattern=[[1, P]], base=0, channel_multiplier=0,
                      allow_small_or_imprecise_dtypes=True).then_inc(init, 1)
            pool.wait_ge(init_v, 5)
            pool.affine_select(out=ident[:, :], in_=ident[:, :], compare_op=ALU.not_equal, fill=1.0,
                               base=0, pattern=[[-1, P]], channel_multiplier=1).then_inc(init, 1)
            pool.affine_select(out=upper[:, :], in_=upper[:, :], compare_op=ALU.is_gt, fill=0.0,
                               base=0, pattern=[[1, P]], channel_multiplier=-1).then_inc(init, 1)
            pool.memset(epsc[:, :], EPS).then_inc(init, 1)

            def scatter(k, r):
                pool.wait_ge(filled, 32)
                with pool.Fori(0, EC // (2 * U)) as i:
                    for h in range(2):
                        pool.wait_ge(sc_ring[k], i * 4 + (2 * h + 2))
                        pool.sem_inc(taken, 1)
                        for u in range(U):
                            pool.indirect_dma_start(
                                r, bass.IndirectOffsetOnAxis(ap=posr[:, h, u:u + 1], axis=0),
                                recr[k][:, h, u, :], None).then_inc(sc_done[k][h], 16)

            def gather(name, free, n, iters):
                with pool.Fori(0, iters) as i:
                    for h in range(2):
                        pool.wait_ge(free[h], i)
                        pool.wait_ge(g_idx[name], i * 2 + (h + 1))
                        pool.sem_inc(taken, 1)
                        for u in range(n):
                            pool.indirect_dma_start(
                                msg[:, h, u, 0:D], None, table,
                                bass.IndirectOffsetOnAxis(ap=idxr[:, h, u:u + 1], axis=0)).then_inc(g_got[name][h], 16)

            scatter(0, rec_dst)
            scatter(1, rec_src)
            pool.wait_ge(tbl0, 32)
            gather("p1", mm_ok["p1"], U, ITERS)
            pool.wait_ge(nst["A"], 16 * NCH)
            gather("p2", mm_ok["p2"], U, ITERS)
            pool.wait_ge(nst["B"], 16 * NCH)
            gather("p3", mm_ok["p3"], U, ITERS)
            pool.wait_ge(nst["C"], 16 * NCH)
            gather("p4", mm_ok["p4"], U, ITERS)
            pool.wait_ge(nst["E"], 16 * NCH)
            gather("p5", q_e, U, ITERS)

        @block.scalar
        def _(act):
            def scatter_ring(k):
                act.wait_ge(pos_ready[k], 1)
                r = (raw, raw_s)[k]
                with act.Fori(0, EC // (2 * U)) as i:
                    for h in range(2):
                        act.wait_ge(sc_done[k][h], i * (16 * U))
                        act.copy(posr[:, h, :], pos[:, k, cols8(i, h)]).then_inc(sc_ring[k], 1)
                        act.copy(recr[k][:, h, :, 0:2 + k], r[:, cols8(i, h), 0:2 + k]).then_inc(sc_ring[k], 1)

            def unpack(k):
                act.wait_ge(rec_ld[k], 16)
                act.copy(gidx[k][:, :], rec[k][:, :, 0]).then_inc(unpacked[k], 1)
                act.wait_ge(unpacked[k], 1)

            def index_ring(name, k, scale=False):
                for h in range(2):
                    act.copy(idxr[:, h, :], gidx[k][:, h * U:(h + 1) * U]).then_inc(g_idx[name], 1)
                with act.Fori(0, ITERS) as i:
                    for h in range(2):
                        act.wait_ge(g_got[name][h], i * (16 * U) + 16 * U)
                        act.copy(idxr[:, h, :], gidx[k][:, bass.ds(i * (2 * U) + (2 + h) * U, U)]).then_inc(g_idx[name], 1)
                        if scale:
                            for u in range(U):
                                act.activation(msg[:, h, u, 0:D], msg[:, h, u, 0:D], ACT.Copy,
                                               scale=rec[k][:, bass.ds(i * (2 * U) + (h * U + u), 1), 2]).then_inc(scaled[h], 1)

            scatter_ring(0)
            for h in range(2):
                act.wait_ge(sc_done[0][h], EC // 2 * 16)
            scatter_ring(1)
            act.wait_ge(sc_ring[1], EC // (2 * U) * 4)
            unpack(0)
            index_ring("p1", 0)

            def conv(p, b, last):
                with act.Fori(0, NCH) as i:
                    act.wait_ge(npe[p], i * 3 + 1)
                    act.copy(sT[:, :], psflat[:, 0:C]).then_inc(na[p], 1)
                    act.wait_ge(npe[p], i * 3 + 2)
                    act.activation(nT[:, :], psflat[:, 1024:1024 + C], ACT.Relu, bias=b[:, :]).then_inc(na[p], 1)
                    last(i)

            def relu_h1(i):
                act.wait_ge(nv["A"], i * 2 + 2)
                act.activation(cur[:, bass.ds(i * CW, CW), :], y[:, :, :], ACT.Relu).then_inc(na["A"], 1)

            def ln_sqrt(sem_a, sem_v, i, K, k):
                act.wait_ge(sem_v, i * K + k)
                act.activation(lnsd[:, :], lnmv[:, :, 1], ACT.Sqrt, bias=epsc[:, :]).then_inc(sem_a, 1)

            act.wait_ge(ld_w, 16 * 19)
            conv("A", bcol[0], relu_h1)
            act.wait_ge(na["A"], 3 * NCH)
            index_ring("p2", 0)
            conv("B", bcol[1], lambda i: ln_sqrt(na["B"], nv["B"], i, KB, LNB))
            unpack(1)
            index_ring("p3", 1, scale=True)

            def sage(p, K, last):
                with act.Fori(0, NCH) as i:
                    act.wait_ge(npe[p], i * 3 + 1)
                    act.copy(sT[:, :], psflat[:, 0:C]).then_inc(na[p], 1)
                    act.wait_ge(npe[p], i * 3 + 2)
                    act.copy(nT[:, :], psflat[:, 1024:1024 + C]).then_inc(na[p], 1)
                    last(i)

            sage("C", KC, lambda i: ln_sqrt(na["C"], nv["C"], i, KC, LNC))
            index_ring("p4", 0)

            def tanh_d(i):
                act.wait_ge(nv["D"], i * 3 + 3)
                act.activation(x0[:, bass.ds(i * CW, CW), :], y[:, :, :], ACT.Tanh).then_inc(na["D"], 1)

            sage("D", 3, tanh_d)
            act.wait_ge(dn_p, 1)
            act.activation(small[:, 4:5], psflat[:, 0:1], ACT.Sqrt).then_inc(dn_a, 1)
            with act.Fori(0, NCH) as i:
                ln_sqrt(na2, nv2, i, KD2, LND2)
            with act.Fori(0, NCH) as i:
                act.wait_ge(npe["E"], i * 3 + 1)
                act.copy(sT[:, :], psflat[:, 0:C]).then_inc(na["E"], 1)
            act.wait_ge(bn_v, 4)
            for h in range(2):
                act.wait_ge(g_got["p4"][h], ITERS * 16 * U)
                act.copy(idxr[:, h, :], gidx[0][:, h * U:(h + 1) * U]).then_inc(g_idx["p5"], 1)
            with act.Fori(0, ITERS) as i:
                for h in range(2):
                    act.wait_ge(q_e[h], i)
                    act.wait_ge(q_tr[h], i + 1)
                    act.copy(ohT[:, h, :, :], PS[:, 2 * h:2 * h + 2, :].rearrange("p b (u c) -> p (b u) c", c=P)).then_inc(q_t[h], 1)
                    act.wait_ge(q_e[h], i + 1)
                    act.wait_ge(q_st[h], i * 16)
                    e = psflat[:, (4 + 2 * h) * 512:(6 + 2 * h) * 512]
                    act.copy(el[:, h, :], e).then_inc(q_cp[h], 1)
                    act.activation(rT[:, h, :], e, ACT.Square, accum_out=sq[:, bass.ds(i * 2 + h, 1)]).then_inc(q_sq[h], 1)
                    act.wait_ge(g_got["p5"][h], i * (16 * U) + 16 * U)
                    act.copy(idxr[:, h, :], gidx[0][:, bass.ds(i * (2 * U) + (2 + h) * U, U)]).then_inc(g_idx["p5"], 1)
            act.wait_ge(bn_v, 6)
            act.activation(small[:, 5:6], small[:, 6:7], ACT.Sqrt, bias=epsc[:, :]).then_inc(bn_a, 1)
            act.wait_ge(bn_v, 8)
            act.activation(small[:, 8:9], bn[:, 1:2], ACT.Relu).then_inc(bn_a, 1)
            with act.Fori(0, ITERS) as i:
                for h in range(2):
                    act.wait_ge(b_ld[h], i * 16 + 16)
                    act.wait_ge(b_mm[h], i)
                    act.activation(rT[:, h, :], el[:, h, :], ACT.Relu, bias=bn[:, 1:2], scale=scale0).then_inc(b_r[h], 1)
            act.wait_ge(bn_v, BNV)
            act.activation(small[:, 15:16], small[:, 14:15], ACT.Sqrt, bias=epsc[:, :]).then_inc(bn_a, 1)
            for h in range(2):
                act.wait_ge(b_mm[h], ITERS)

            def c_relu(h, i):
                act.wait_ge(c_ld[h], i * 16 + 16)
                act.wait_ge(c_e[h], i)
                act.activation(rT[:, h, :], el[:, h, :], ACT.Relu, bias=bn[:, 1:2], scale=scale0).then_inc(c_r[h], 1)

            def c_turn(i, last=False):
                for h in range(2):
                    if not (last and h):
                        c_relu(1 - h, i + h)
                    act.wait_ge(c_e[h], i + 1)
                    act.wait_ge(mm_ok["pc"][h], i)
                    act.activation(msg[:, h, :, 0:D], PS[:, 2 * h:2 * h + 2, :].rearrange("p b (u c) -> p (b u) c", c=D),
                                   ACT.Relu).then_inc(c_y[h], 1)

            c_relu(0, 0)
            with act.Fori(0, ITERS - 1) as i:
                c_turn(i)
            c_turn(ITERS - 1, last=True)
            with act.Fori(0, NCH) as i:
                ln_sqrt(na["F"], nv["F"], i, KF, LNF)

        @block.tensor
        def _(pe):
            pe.wait_ge(init, 6)
            pe.wait_ge(init_v, 17)
            for k in range(2):
                pe.wait_ge(rkl[k], NW + 1)
                pe.matmul(PS[:, 6, 0:NW + 1], upper[:, :], cnt[:, :], start=True, stop=True).then_inc(rkp[k], 1)
                pe.matmul(PS[:, 7, 0:NW + 1], ones[:, :], cnt[:, :], start=True, stop=True).then_inc(rkp[k], 1)
            pe.wait_ge(ld_w, 16 * 19)
            for n in range(3):
                pe.transpose(PS[:, 0, n * P:(n + 1) * P], wL2[:, n * D:(n + 1) * D], ident[:, :]).then_inc(wt_pe, 1)
            pe.transpose(PS[:, 0, 3 * P:4 * P], th[:, :], ident[:, :]).then_inc(wt_pe, 1)
            pe.wait_ge(wt_dve, 1)
            pe.transpose(PS[:, 1, 0:P], ph[:, :], ident[:, :]).then_inc(wt_pe, 1)
            pe.transpose(PS[:, 1, P:2 * P], fc[:, :], ident[:, :]).then_inc(wt_pe, 1)

            def slot(h, u):
                return PS[:, 3 * h + u // 3, (u % 3) * D1:(u % 3 + 1) * D1]

            def segsum(name):
                with pe.Fori(0, ITERS) as i:
                    for h in range(2):
                        pe.wait_ge(oh_ok[name][h], i + 1)
                        pe.wait_ge(g_got[name][h], (i + 1) * (16 * U))
                        if name == "p3":
                            pe.wait_ge(scaled[h], i * U + U)
                        pe.wait_ge(add_ok[name], i * (2 * U))
                        for u in range(U):
                            mm = pe.matmul(slot(h, u), oh[:, h, u, :], msg[:, h, u, :], start=True, stop=True)
                        mm.then_inc(mm_ok[name][h], 1)

            def turn_chunk(to, frm):
                for j in range(CW):
                    mm = pe.transpose(psflat[:, to + j * P:to + (j + 1) * P], frm[:, j * P:(j + 1) * P], ident[:, :])
                return mm

            def conv(p, wa, wb, kv, s_step):
                with pe.Fori(0, NCH) as i:
                    pe.wait_ge(nv[p], i * kv + s_step)
                    turn_chunk(0, s_ring).then_inc(npe[p], 1)
                    pe.wait_ge(na[p], i * 3 + 1)
                    pe.matmul(psflat[:, 1024:1536], wa[:, :], sT[:, 0:512], start=True, stop=True)
                    pe.matmul(psflat[:, 1536:1024 + C], wa[:, :], sT[:, 512:C], start=True, stop=True).then_inc(npe[p], 1)
                    pe.wait_ge(na[p], i * 3 + 2)
                    for j in range(CW):
                        mm = pe.matmul(psflat[:, 2048 + j * P:2048 + (j + 1) * P], nT[:, j * P:(j + 1) * P], wb[:, :],
                                       start=True, stop=True)
                    mm.then_inc(npe[p], 1)

            def sage(p, kv, ws_x, w_n):
                with pe.Fori(0, NCH) as i:
                    pe.wait_ge(nv[p], i * kv + 2)
                    turn_chunk(0, s_ring).then_inc(npe[p], 1)
                    turn_chunk(1024, n_ring).then_inc(npe[p], 1)
                    pe.wait_ge(na[p], i * 3 + 2)
                    for j in range(CW):
                        o = psflat[:, 2048 + j * P:2048 + (j + 1) * P]
                        for n, wx in enumerate(ws_x):
                            pe.matmul(o, sT[:, j * P:(j + 1) * P], wx, start=(n == 0), stop=False)
                        mm = pe.matmul(o, nT[:, j * P:(j + 1) * P], w_n, start=False, stop=True)
                    mm.then_inc(npe[p], 1)

            segsum("p1")
            conv("A", wA[0], wA[1], 2, 1)
            segsum("p2")
            conv("B", wA[2], wA[3], KB, 1)
            segsum("p3")
            sage("C", KC, [wL1[:, 0, :]], wL1[:, 1, :])
            segsum("p4")
            sage("D", 3, [wL2T[:, 0, :], wL2T[:, 2, :]], wL2T[:, 1, :])
            pe.wait_ge(dn_v, 3)
            pe.matmul(psflat[:, 0:1], ones[:, :], small[:, 7:8], start=True, stop=True).then_inc(dn_p, 1)
            pe.wait_ge(dn_v, 4)
            with pe.Fori(0, NCH) as i:
                pe.wait_ge(nv["E"], i * 3 + 1)
                turn_chunk(0, s_ring).then_inc(npe["E"], 1)
                pe.wait_ge(na["E"], i + 1)
                for j in range(CW):
                    mm = pe.matmul(psflat[:, 1024 + j * 256:1280 + j * 256], sT[:, j * P:(j + 1) * P],
                                   thphT[:, :, :].rearrange("p a c -> p (a c)"), start=True, stop=True)
                mm.then_inc(npe["E"], 1)
                pe.wait_ge(nv["E"], i * 3 + 2)
                for j in range(CW):
                    pe.matmul(psflat[:, 3072:3073], s2a[:, j * P:(j + 1) * P], deg_dst[:, bass.ds(i * CW + j, 1)],
                              start=(j == 0), stop=False)
                    mm = pe.matmul(psflat[:, 3072:3073], y[:, j, :], deg_src[:, bass.ds(i * CW + j, 1)],
                                   start=False, stop=(j == CW - 1))
                mm.then_inc(npe["E"], 1)
            pe.wait_ge(bn_v, 3)
            pe.matmul(PS[:, 7, 0:P], ones[:, :], diag[:, :], start=True, stop=True).then_inc(bn_p, 1)
            pe.wait_ge(bn_v, 4)
            with pe.Fori(0, ITERS) as i:
                for h in range(2):
                    pe.wait_ge(oh_ok["p5"][h], i + 1)
                    pe.wait_ge(q_t[h], i)
                    for u in range(U):
                        mm = pe.transpose(PS[:, 2 * h + u // 4, (u % 4) * P:(u % 4 + 1) * P], oh[:, h, u, :], ident[:, :])
                    mm.then_inc(q_tr[h], 1)
                    pe.wait_ge(q_t[h], i + 1)
                    pe.wait_ge(q_a[h], i * U + U)
                    pe.wait_ge(g_got["p5"][h], (i + 1) * (16 * U))
                    pe.wait_ge(q_sq[h], i)
                    for u in range(U):
                        o = PS[:, 4 + 2 * h + u // 4, (u % 4) * P:(u % 4 + 1) * P]
                        pe.matmul(o, abuf[:, h, u, :], ohT[:, h, u, :], start=True, stop=False)
                        mm = pe.matmul(o, msg[:, h, u, 0:D], ident[:, :], start=False, stop=True)
                    mm.then_inc(q_e[h], 1)
            for h in range(2):
                pe.wait_ge(q_sq[h], ITERS)
            pe.wait_ge(bn_a, 2)
            pe.matmul(PS[:, 7, 0:1], fcT[:, :], small[:, 8:9], start=True, stop=True).then_inc(bn_p, 1)
            with pe.Fori(0, ITERS) as i:
                for h in range(2):
                    pe.wait_ge(b_r[h], i + 1)
                    pe.wait_ge(b_bn[h], i * 2)
                    for s in range(2):
                        mm = pe.matmul(PS[:, 2 * h + s, :], fcT[:, :], rT[:, h, s * 512:(s + 1) * 512], start=True, stop=True)
                    mm.then_inc(b_mm[h], 1)
            pe.wait_ge(bn_v, BNV + 2)
            pe.transpose(PS[:, 6, 0:P], fcs[:, :], ident[:, :]).then_inc(bn_p, 1)
            pe.transpose(PS[0:1, 6, P:2 * P], sh1, ident[:, :]).then_inc(bn_p, 1)
            pe.wait_ge(bn_v, BNV + 4)

            def c_product(h, i):
                pe.wait_ge(c_r[h], i + 1)
                pe.wait_ge(c_y[h], i)
                for u in range(U):
                    o = PS[:, 2 * h + u // 4, (u % 4) * P:(u % 4 + 1) * P]
                    pe.matmul(o, rT[:, h, u * P:(u + 1) * P], fcsT[:, :], start=True, stop=False)
                    mm = pe.matmul(o, ones[0:1, :], shrow[:, :], start=False, stop=True)
                mm.then_inc(c_e[h], 1)

            def c_turn(i, last=False):
                for h in range(2):
                    if not (last and h):
                        c_product(1 - h, i + h)
                    pe.wait_ge(c_y[h], i + 1)
                    pe.wait_ge(oh_ok["pc"][h], i + 1)
                    pe.wait_ge(add_ok["pc"], i * (2 * U))
                    for u in range(U):
                        mm = pe.matmul(PS[:, 4 + 2 * h + u // 4, (u % 4) * P:(u % 4 + 1) * P], oh[:, h, u, :],
                                       msg[:, h, u, 0:D], start=True, stop=True)
                    mm.then_inc(mm_ok["pc"][h], 1)

            c_product(0, 0)
            with pe.Fori(0, ITERS - 1) as i:
                c_turn(i)
            c_turn(ITERS - 1, last=True)

        @block.vector
        def _(dve):
            v = Count(dve, init_v)
            v.inc(dve.memset(key_i[:, :, :], NP))
            v.inc(dve.memset(wgt[:, :], 0.0))                 
            v.inc(dve.memset(ident[:, :], 0.0))
            v.inc(dve.memset(ones[:, :], 1.0))
            v.inc(dve.memset(upper[:, :], 1.0))
            v.inc(dve.memset(zeros_e[:, :], 0.0))
            for k in range(2):
                v.inc(dve.memset(rec[k][:, :, 0], float(ZROW)))
                v.inc(dve.memset(rec[k][:, :, 1], -1.0))
                v.inc(dve.memset(rec[1][:, :, 2 + k], 0.0))
            v.inc(dve.memset(msg[:, :, :, D:D1], 1.0))
            v.inc(dve.memset(x0[:, NW - 1, :], 0.0))
            v.inc(dve.memset(recr[1][:, :, :, :], 0.0))
            v.link(dve.memset(small[:, :], 0.0))
            v.link(dve.memset(small[0:TAIL, 20:21], 1.0))
            dve.wait_ge(ld_edges, 96)
            dve.wait_ge(init, 6)

            def rank(k):
                r = (raw, raw_s)[k]
                c = Count(dve, rk[k])
                lo = mask[:, 0, :]
                hi = mask[:, 1, :]
                c.inc(dve.tensor_scalar(lo, key_i[:, k, :], P - 1, None, ALU.bitwise_and))
                c.inc(dve.tensor_scalar(hi, key_i[:, k, :], 7, None, ALU.arith_shift_right))
                c.wait()
                c.inc(dve.tensor_copy(r[:, :, 1], lo))
                c.inc(dve.tensor_copy(winf[:, :], hi))
                c.inc(dve.tensor_copy(r[:, :, 0], key_i[:, 1 - k, :]))
                c.inc(dve.tensor_copy(r[:, :, 2], wgt[:, :]))
                c.wait()
                with dve.Fori(0, NW + 1) as i:
                    dve.wait_ge(rkl[k], i)
                    dve.tensor_scalar(scan[:, 0, :], winf[:, :], wnum[:, bass.ds(i, 1)], None, ALU.is_equal, ALU.add,
                                      accum_out=cnt[:, bass.ds(i, 1)]).then_inc(rkl[k], 1)
                dve.wait_ge(rkp[k], 2)
                c.link(dve.tensor_copy(tot[:, :], PS[:, 7, 0:NW + 1]))
                c.link(dve.tensor_scalar(tiles_f[:, :], tot[:, :], float(P - 1), None, ALU.add))
                c.link(dve.tensor_copy(tiles_i[:, :], tiles_f[:, :]))
                c.link(dve.tensor_scalar(tiles_i[:, :], tiles_i[:, :], 7, None, ALU.arith_shift_right))
                c.link(dve.tensor_copy(tiles_f[:, :], tiles_i[:, :]))
                c.link(dve.tensor_tensor_scan(tend[:, :], tiles_f[:, :], zeros_e[:, 0:NW + 1], 0.0, ALU.add, ALU.add))
                c.link(dve.tensor_tensor(off[:, :], tend[:, :], tiles_f[:, :], ALU.subtract))
                c.link(dve.memset(off[:, NW:NW + 1], float(T)))
                c.link(dve.tensor_scalar(off[:, :], off[:, :], float(P), -1.0, ALU.mult, ALU.add))
                c.link(dve.tensor_tensor(off[:, :], off[:, :], PS[:, 6, 0:NW + 1], ALU.add))
                with dve.Fori(0, (NW + 1) // 2) as i:
                    for h in range(2):
                        w = i * 2 + h
                        dve.wait_ge(rkq[k], i * 6 + 3 * h)
                        dve.tensor_scalar(mask[:, h, :], winf[:, :], wnum[:, bass.ds(w, 1)], None, ALU.is_equal).then_inc(rkq[k], 1)
                        dve.wait_ge(rkq[k], i * 6 + (3 * h + 1))
                        dve.tensor_tensor_scan(scan[:, h, :], mask[:, h, :], zeros_e[:, :], off[:, bass.ds(w, 1)],
                                               ALU.add, ALU.add).then_inc(rkq[k], 1)
                        dve.wait_ge(rkq[k], i * 6 + (3 * h + 2))
                        dve.sem_inc(vtaken, 1)
                        dve.copy_predicated(posf[:, :], mask[:, h, :], scan[:, h, :]).then_inc(rkq[k], 1)
                dve.wait_ge(rkq[k], 3 * (NW + 1))
                c.link(dve.tensor_copy(pos[:, k, :], posf[:, :]))
                c.inc(dve.tensor_scalar(lo, pos[:, k, :], P - 1, None, ALU.bitwise_and))
                c.link(dve.tensor_scalar(hi, pos[:, k, :], 7, None, ALU.arith_shift_right))
                c.inc(dve.tensor_copy(scan[:, 0, :], lo))
                c.link(dve.tensor_copy(scan[:, 1, :], hi))
                dve.scalar_tensor_tensor(out=pos[:, k, :], in0=scan[:, 0, :], scalar=float(TT), in1=scan[:, 1, :],
                                         op0=ALU.mult, op1=ALU.add).then_inc(pos_ready[k], 1)
                c.link(dve.memset(wtf[:, 0, :], 0.0))
                with dve.Fori(0, NW - 1) as i:
                    dve.wait_ge(rkw[k], i)
                    dve.scalar_tensor_tensor(out=wtf[:, 0, :], in0=tnum[:, :], scalar=tend[:, bass.ds(i, 1)],
                                             in1=wtf[:, 0, :], op0=ALU.is_ge, op1=ALU.add).then_inc(rkw[k], 1)
                dve.wait_ge(rkw[k], NW - 1)
                c.link(dve.tensor_copy(wtile[k][:, :], wtf[0:1, 0, :]))
                dve.wait_ge(pos_ready[k], 1)

            def windows(k, h, i):
                return nc.values_load_multi_w_load_instructions(
                    wtile[k][0:1, cols8(i, h)], engines=[mybir.EngineType.DVE], min_val=0, max_val=NW - 1)[1]

            def one_hots(name, k, h, i, free):
                dve.wait_ge(free[h], i)
                dve.tensor_tensor(oh[:, h, :, :],
                                  col[:, :].rearrange("p (o c) -> p o c", o=1).to_broadcast([P, U, P]),
                                  rec[k][:, cols8(i, h), 1:2].to_broadcast([P, U, P]),
                                  ALU.is_equal).then_inc(oh_ok[name][h], 1)

            def add_windows(name, h, i, ws, got, width):
                dve.wait_ge(mm_ok[name][h], i + 1)
                for u in range(U):
                    dve.wait_ge(add_ok[name], i * (2 * U) + (h * U + u))
                    a = acc[:, bass.ds(ws[u], 1), 0:width]
                    dve.tensor_tensor(a, a, got(h, u), ALU.add).then_inc(add_ok[name], 1)

            def slot(h, u):
                return PS[:, 3 * h + u // 3, (u % 3) * D1:(u % 3 + 1) * D1].rearrange("p (o c) -> p o c", o=1)

            def ahead(name, k, got, width):
                one_hots(name, k, 0, 0, mm_ok[name])

                def turn(i, last=False):
                    for h in range(2):
                        ws = windows(k, h, i)
                        if not (last and h):
                            one_hots(name, k, 1 - h, i + h, mm_ok[name])
                        add_windows(name, h, i, ws, got, width)

                with dve.Fori(0, ITERS - 1) as i:
                    turn(i)
                turn(ITERS - 1, last=True)

            z = Count(dve, acc_zero)

            def segsum(name, k):
                dve.wait_ge(rec_ld[k], 16)
                z.link(dve.memset(acc[:, :, :], 0.0))
                ahead(name, k, slot, D1)
                dve.wait_ge(add_ok[name], T)

            rank(0)
            rank(1)
            dve.wait_ge(ld_w, 16 * 19)
            dve.tensor_tensor(ph[:, :], ph[:, :], th[:, :], ALU.subtract).then_inc(wt_dve, 1)
            dve.wait_ge(wt_pe, 6)
            wd = Count(dve, wt_dve)
            wd.n = 1
            wd.inc(dve.tensor_copy(wL2T[:, :, :], PS[:, 0, 0:384].rearrange("p (a c) -> p a c", a=3)))
            wd.inc(dve.tensor_copy(thphT[:, 0, :], PS[:, 0, 384:512]))
            wd.inc(dve.tensor_copy(thphT[:, 1, :], PS[:, 1, 0:P]))
            wd.link(dve.tensor_copy(fcT[:, :], PS[:, 1, P:2 * P]))

            def wide(a):
                return a.rearrange("p (j o) -> p j o", o=1).to_broadcast([P, CW, D])

            def brc(a):
                return a[:, :].rearrange("p (o c) -> p o c", o=1).to_broadcast([P, CW, D])

            s3 = s_ring[:, :].rearrange("p (j c) -> p j c", j=CW)
            n3 = n_ring[:, :].rearrange("p (j c) -> p j c", j=CW)
            ps3 = psflat[:, 2048:2048 + C].rearrange("p (j c) -> p j c", j=CW)

            def ln(c, i, sem_a, a_val):
                for j in range(CW):
                    c.inc(dve.bn_stats(lnst[:, j, :], y[:, j, :]))
                c.wait()
                dve.sem_inc(vtaken, 1)
                for j in range(CW):
                    c.inc(dve.bn_aggr(lnmv[:, j, :], lnst[:, j, :]))
                dve.wait_ge(sem_a, a_val)
                c.link(dve.reciprocal(lnrs[:, :], lnsd[:, :]))
                for j in range(CW):
                    c.inc(dve.tensor_scalar(cur[:, bass.ds(i * CW + j, 1), :], y[:, j:j + 1, :], lnmv[:, j, 0:1],
                                            lnrs[:, j:j + 1], ALU.subtract, ALU.mult))
                c.wait()

            dve.wait_ge(tbl0, 32)
            segsum("p1", 0)
            dv = Count(dve, n_pass["A"])
            dv.link(dve.tensor_copy(deg_dst[:, :], acc[:, :, D]))
            with dve.Fori(0, NCH) as i:
                c = Count(dve, nv["A"], 2, i)
                ch = bass.ds(i * CW, CW)
                dve.wait_ge(npe["A"], i * 3)
                c.inc(dve.tensor_tensor(s3, x0[:, ch, :], acc[:, ch, 0:D], ALU.add))
                dve.wait_ge(npe["A"], i * 3 + 3)
                dve.wait_ge(na["A"], i * 3)
                c.inc(dve.tensor_tensor(y[:, :, :], ps3, brc(brow[0]), ALU.add))
            dve.wait_ge(na["A"], 3 * NCH)
            segsum("p2", 0)
            with dve.Fori(0, NCH) as i:
                c = Count(dve, nv["B"], KB, i)
                ch = bass.ds(i * CW, CW)
                dve.wait_ge(npe["B"], i * 3)
                c.inc(dve.tensor_tensor(s3, cur[:, ch, :], acc[:, ch, 0:D], ALU.add))
                dve.wait_ge(npe["B"], i * 3 + 3)
                c.link(dve.tensor_tensor(y[:, :, :], ps3, brc(brow[1]), ALU.add))
                c.link(dve.tensor_tensor(y[:, :, :], y[:, :, :], x0[:, ch, :], ALU.add))
                ln(c, i, na["B"], i * 3 + 3)
                assert c.n == KB
            dve.wait_ge(nv["B"], KB * NCH)

            def reciprocal_degree(cc, deg):
                cc.link(dve.tensor_scalar(rdeg[:, :], deg[:, :], 1.0, None, ALU.max))
                cc.link(dve.reciprocal(rdeg[:, :], rdeg[:, :]))

            def sage_in(c, i):
                ch = bass.ds(i * CW, CW)
                dve.wait_ge(npe[c.p], i * 3)
                c.inc(dve.tensor_copy(s3, cur[:, ch, :]))
                c.inc(dve.tensor_tensor(n3, acc[:, ch, 0:D],
                                        rdeg[:, ch].rearrange("p (j o) -> p j o", o=1).to_broadcast([P, CW, D]), ALU.mult))
                dve.wait_ge(npe[c.p], i * 3 + 3)

            segsum("p3", 1)
            dv = Count(dve, n_pass["C"])
            dv.link(dve.tensor_copy(deg_src[:, :], acc[:, :, D]))
            reciprocal_degree(dv, deg_src)
            with dve.Fori(0, NCH) as i:
                c = Count(dve, nv["C"], KC, i)
                c.p = "C"
                sage_in(c, i)
                c.link(dve.tensor_tensor(y[:, :, :], ps3, brc(bL1), ALU.add))
                c.link(dve.tensor_tensor(y[:, :, :], y[:, :, :], s3, ALU.add))
                ln(c, i, na["C"], i * 3 + 3)
                assert c.n == KC
            dve.wait_ge(nv["C"], KC * NCH)
            segsum("p4", 0)
            dv = Count(dve, n_pass["D"])
            reciprocal_degree(dv, deg_dst)
            with dve.Fori(0, NCH) as i:
                c = Count(dve, nv["D"], 3, i)
                c.p = "D"
                sage_in(c, i)
                dve.wait_ge(na["D"], i * 3)
                c.inc(dve.tensor_tensor(y[:, :, :], ps3, brc(bL2), ALU.add))
            dve.wait_ge(na["D"], 3 * NCH)
            c = Count(dve, dn_v)
            c.link(dve.tensor_scalar(x0[:, NW - 1, :], x0[:, NW - 1, :], small[:, 20:21], None, ALU.mult))
            c.link(dve.tensor_tensor(acc[:, :, 0:D], x0[:, :, :], x0[:, :, :], ALU.mult))
            c.link(dve.tensor_reduce(small[:, 7:8], acc[:, :, 0:D], AX.XY, ALU.add))
            dve.wait_ge(dn_a, 1)
            c.link(dve.reciprocal(small[:, 10:11], small[:, 4:5]))
            with dve.Fori(0, NCH) as i:
                c = Count(dve, nv2, KD2, i)
                ch = bass.ds(i * CW, CW)
                c.link(dve.scalar_tensor_tensor(out=y[:, :, :], in0=x0[:, ch, :], scalar=small[:, 10:11],
                                                in1=cur[:, ch, :], op0=ALU.mult, op1=ALU.add))
                ln(c, i, na2, i + 1)
                assert c.n == KD2
            dve.wait_ge(nv2, KD2 * NCH)
            c = Count(dve, bn_v)
            c.link(dve.memset(mu0, 0.0))
            with dve.Fori(0, NCH) as i:
                ch = bass.ds(i * CW, CW)
                dve.wait_ge(npe["E"], i * 3)
                dve.tensor_copy(s3, cur[:, ch, :]).then_inc(nv["E"], 1)
                dve.wait_ge(npe["E"], i * 3 + 2)
                dve.wait_ge(nst["E"], i * 16)
                ab = psflat[:, 1024:1024 + 2 * C].rearrange("p (j c) -> p j c", j=CW)
                dve.tensor_copy(s2a[:, :].rearrange("p (j c) -> p j c", j=CW), ab[:, :, 0:D])
                dve.tensor_copy(x0[:, ch, :], ab[:, :, 0:D])
                dve.tensor_copy(y[:, :, :], ab[:, :, D:2 * D]).then_inc(nv["E"], 1)
                dve.wait_ge(npe["E"], i * 3 + 3)
                dve.wait_ge(nv["E"], i * 3 + 2)
                dve.tensor_tensor(mu0, mu0, psflat[:, 3072:3073], ALU.add).then_inc(nv["E"], 1)
            dve.wait_ge(nv["E"], 3 * NCH)
            c.link(dve.tensor_scalar(mfc, mu0, 1.0 / E, None, ALU.mult))
            c.inc(dve.tensor_scalar(diag[:, :], ident[:, :], mfc, None, ALU.mult))
            dve.wait_ge(bn_p, 1)
            c.link(dve.tensor_tensor(x0[:, :, :], x0[:, :, :],
                                     PS[:, 7, 0:P].rearrange("p (o c) -> p o c", o=1).to_broadcast([P, NW, D]),
                                     ALU.subtract))
            with dve.Fori(0, ITERS) as i:
                for h in range(2):
                    ws = windows(0, h, i)
                    one_hots("p5", 0, h, i, q_tr)
                    dve.wait_ge(q_e[h], i)
                    for u in range(U):
                        dve.tensor_copy(abuf[:, h, u:u + 1, :], x0[:, bass.ds(ws[u], 1), :]).then_inc(q_a[h], 1)
            for h in range(2):
                dve.wait_ge(q_sq[h], ITERS)
            c.link(dve.tensor_reduce(small[:, 11:12], sq[:, :], AX.X, ALU.add))
            c.link(dve.tensor_scalar(small[:, 6:7], small[:, 11:12], 1.0 / E, None, ALU.mult))
            assert c.n == 6
            dve.wait_ge(bn_a, 1)
            c.link(dve.reciprocal(small[:, 12:13], small[:, 5:6]))
            c.link(dve.tensor_tensor(scale0, small[:, 12:13], bn[:, 0:1], ALU.mult))
            dve.wait_ge(bn_p, 2)
            c.link(dve.tensor_copy(small[:, 13:14], PS[:, 7, 0:1]))
            with dve.Fori(0, ITERS) as i:
                for h in range(2):
                    dve.wait_ge(b_mm[h], i + 1)
                    for s in range(2):
                        dve.bn_stats(stats[:, bass.ds(i * 4 + (2 * h + s), 1), :], PS[:, 2 * h + s, :]).then_inc(b_bn[h], 1)
            for h in range(2):
                dve.wait_ge(b_bn[h], 2 * ITERS)
            c.link(dve.bn_aggr(small[:, 16:18], stats[:, :, :].rearrange("p a b -> p (a b)")))
            EMPTY = SLOTS - E
            c.link(dve.tensor_tensor(small[:, 18:19], small[:, 16:17], small[:, 13:14], ALU.subtract))
            c.link(dve.scalar_tensor_tensor(out=small[:, 19:20], in0=small[:, 18:19], scalar=EMPTY / E,
                                            in1=small[:, 16:17], op0=ALU.mult, op1=ALU.add))
            c.link(dve.tensor_tensor(small[:, 18:19], small[:, 13:14], small[:, 19:20], ALU.subtract))
            c.link(dve.tensor_tensor(small[:, 18:19], small[:, 18:19], small[:, 18:19], ALU.mult))
            c.link(dve.tensor_scalar(small[:, 21:22], small[:, 17:18], SLOTS / E, None, ALU.mult))
            c.link(dve.scalar_tensor_tensor(out=small[:, 14:15], in0=small[:, 18:19], scalar=-EMPTY / SLOTS,
                                            in1=small[:, 21:22], op0=ALU.mult, op1=ALU.add))
            assert c.n == BNV, c.n
            dve.wait_ge(bn_a, 3)
            t = Count(dve, dn_v)
            t.n = 4
            t.link(dve.reciprocal(small[:, 22:23], small[:, 15:16]))
            t.link(dve.tensor_tensor(small[:, 22:23], small[:, 22:23], bn[:, 2:3], ALU.mult))
            t.link(dve.tensor_tensor(small[:, 23:24], small[:, 22:23], small[:, 19:20], ALU.mult))
            c.link(dve.tensor_scalar(fcs[:, :], fc[:, :], small[:, 22:23], None, ALU.mult))
            c.link(dve.tensor_tensor(sh1, bn[:, 3:4], small[:, 23:24], ALU.subtract))
            dve.wait_ge(bn_p, 4)
            c.link(dve.tensor_copy(fcsT[:, :], PS[:, 6, 0:P]))
            c.link(dve.tensor_copy(shrow[:, :], PS[0:1, 6, P:2 * P]))
            z.link(dve.memset(acc[:, :, :], 0.0))
            ahead("pc", 0, lambda h, u: PS[:, 4 + 2 * h + u // 4, (u % 4) * P:(u % 4 + 1) * P].rearrange("p (o c) -> p o c", o=1), D)
            dve.wait_ge(add_ok["pc"], T)
            with dve.Fori(0, NCH) as i:
                c = Count(dve, nv["F"], KF, i)
                ch = bass.ds(i * CW, CW)
                c.link(dve.tensor_tensor(n3, acc[:, ch, 0:D],
                                         rdeg[:, ch].rearrange("p (j o) -> p j o", o=1).to_broadcast([P, CW, D]), ALU.mult))
                c.link(dve.tensor_tensor(n3, n3, cur[:, ch, :], ALU.add))
                c.link(dve.scalar_tensor_tensor(out=y[:, :, :], in0=n3, scalar=0.0, in1=cur[:, ch, :],
                                                op0=ALU.max, op1=ALU.add))
                ln(c, i, na["F"], i + 1)
                assert c.n == KF


_INS = ["x", "src", "dst", "edge_weight1", "L0_gnn_W1", "L0_gnn_b1", "L0_gnn_W2", "L0_gnn_b2", "L0_gnn_W3", "L0_gnn_b3",
        "L0_gnn_W4", "L0_gnn_b4", "L1_gnn_W", "L1_gnn_b", "L2_gnn_W", "L2_gnn_b", "L3_gnn_theta_w", "L3_gnn_phi_w",
        "L3_gnn_fc1_w", "L3_gnn_bn0_g", "L3_gnn_bn0_b", "L3_gnn_bn1_g", "L3_gnn_bn1_b"]


def kernel(**inputs):
    import numpy as np
    import concourse.bacc as bacc
    from concourse import mybir as mb
    from concourse.bass_utils import run_bass_kernel_spmd

    nc = bacc.Bacc("TRN2", target_bir_lowering=False, num_devices=1)
    arrays, args = {}, []
    for name in _INS:
        a = np.ascontiguousarray(inputs[name])
        arrays[f"in_{name}"] = a
        args.append(nc.dram_tensor(f"in_{name}", a.shape, mb.dt.from_np(a.dtype), kind="ExternalInput").ap())
    shape = inputs["x"].shape
    args.append(nc.dram_tensor("result", shape, mb.dt.float32, kind="ExternalOutput").ap())
    gnn_kernel(nc, *args)
    r = run_bass_kernel_spmd(nc, [arrays], core_ids=[0])
    return np.asarray(r.results[0]["result"]).reshape(shape)
```

```python
from contextlib import ExitStack

import concourse.bass as bass
from concourse import mybir

F32 = mybir.dt.float32
I32 = mybir.dt.int32
ALU = mybir.AluOpType
ACT = mybir.ActivationFunctionType
AX = mybir.AxisListType

P = 128


class Count:

    def __init__(self, eng, sem, K=0, i=0):
        self.eng, self.sem, self.K, self.i, self.n = eng, sem, K, i, 0

    def inc(self, ins):
        ins.then_inc(self.sem, 1)
        self.n += 1
        return self.n

    def wait(self, n=None):
        self.eng.wait_ge(self.sem, self.i * self.K + (self.n if n is None else n))

    def link(self, ins):
        self.inc(ins)
        self.wait()

    def turn(self, i):
        assert self.n in (0, self.K)
        self.i, self.n = i, 0


def gnn_kernel(nc, x, src, dst, edge_weight1, W1, b1, W2, b2, W3, b3, W4, b4, L1W, L1b, L2W, L2b,
               theta_w, phi_w, fc1_w, bn0_g, bn0_b, bn1_g, bn1_b, out):
    N, D = x.shape
    E = src.shape[0]
    NW = -(-N // P)
    NP = NW * P
    ZROW = NP
    EC = 2 * 8 * (-(-E // (P * 16)))
    EP = E // EC
    ER = E - EP * EC
    assert D == P and EP == P - 1 and 0 < ER < EC
    U = 8
    T = (E + NW * (P - 1)) // P
    T = -(-T // (2 * U)) * 2 * U
    TT = T + 2 * U
    assert EC * P - E <= (TT - T) * P
    TG = TT // P
    EB = -(-E // P)
    EL = E - (EB - 1) * P
    assert TG * P == TT and NW + 1 < T // (2 * U)
    ITERS = T // (2 * U)
    SLOTS = T * P
    EPS = 1e-5
    CW = 7
    NCH = NW // CW
    assert NCH * CW == NW
    TAIL = N - (NW - 1) * P
    C = CW * P
    LN = 3 * CW + 1
    KB, LNB = 3 + LN, 3 + 2 * CW
    KC, LNC = 4 + LN, 4 + 2 * CW
    KD2, LND2 = 1 + LN, 1 + 2 * CW
    KF, LNF = 3 + LN, 3 + 2 * CW
    IV = 19
    SHL = 43
    SCI = EC // (2 * U)
    FLV, SHQ = 4, 14
    BNV = 16
    D1 = D + 1

    table = nc.dram_tensor("node_table", (NP + P, D), F32).ap()
    rec_dst = nc.dram_tensor("rec_dst", (P * TT, 2), F32).ap()
    rec_src = nc.dram_tensor("rec_src", (P * TT, 4), F32).ap()
    pairs = nc.dram_tensor("pairs", (EB, 4, P), I32).ap()
    wdram = [nc.dram_tensor(f"window_of_tile_{k}", (P, TG), I32).ap() for k in "ds"]
    e_store = nc.dram_tensor("e_store", (ITERS * 2, P, U * P), F32).ap()
    table_w = table[0:NP, :].rearrange("(w p) f -> p w f", p=P)

    ctx = ExitStack()
    with ctx:
        def sb(name, shape, dt=F32):
            return ctx.enter_context(nc.sbuf_tensor(name, shape, dt))

        def sem(name):
            return ctx.enter_context(nc.semaphore(name))

        x0 = sb("x0", [P, NW, D])
        cur = sb("cur", [P, NW, D])
        acc = sb("acc", [P, NW, D1])
        deg_dst = sb("deg_dst", [P, NW])
        deg_src = sb("deg_src", [P, NW])
        rdeg = sb("rdeg", [P, NW])
        accf = cur[:, :, :].rearrange("p a b -> p (a b)")
        sumf = acc[:, :, :].rearrange("p a b -> p (a b)")
        blk = sumf[:, 0:4 * TT].bitcast(I32).rearrange("p (j k c) -> p j k c", j=TG, k=2)
        blkf = sumf[:, 0:4 * TT].rearrange("p (j k c) -> p j k c", j=TG, k=2)
        lanes = sumf[:, 4 * TT:6 * TT].rearrange("p (k j c) -> p k j c", k=2, j=TG)
        real = sumf[:, 6 * TT:7 * TT].bitcast(I32).rearrange("p (j c) -> p j c", j=TG)
        key_i = accf[:, 0:2 * EC].bitcast(I32).rearrange("p (k c) -> p k c", k=2)
        raw = sb("raw", [P, EC, 3])
        raw_s = sb("raw_s", [P, EC, 3])
        wgt = accf[:, 2 * EC:3 * EC]
        pos = sb("pos", [P, 2, EC], I32)
        rec = [sb("rec_d_sb", [P, TT, 2]), sb("rec_s_sb", [P, TT, 4])]
        gidx = [sb("gidx_d", [P, TT], I32), sb("gidx_s", [P, TT], I32)]
        wtile = [sb("wtile_d", [1, TT], I32), sb("wtile_s", [1, TT], I32)]
        winf = accf[:, 3 * EC:4 * EC]
        scratch = sb("scratch", [P, 4, C])
        mask = scratch[:, 0:2, 0:EC].bitcast(I32)
        scan = scratch[:, 2:4, 0:EC]
        posf = accf[:, 4 * EC:5 * EC]
        zeros_e = accf[:, 5 * EC:6 * EC]
        cnt = sb("cnt", [P, NW + 1])
        tot = sb("tot", [P, NW + 1])
        tiles_i = sb("tiles_i", [P, NW + 1], I32)
        tiles_f = sb("tiles_f", [P, NW + 1])
        tend = sb("tend", [P, NW + 1])
        off = sb("off", [P, NW + 1])
        wnum = sb("wnum", [P, NW + 1])
        tnum = sb("tnum", [P, TG])
        ge = scratch[:, 0, 0:TG * (NW - 1)].rearrange("p (j w) -> p j w", j=TG)
        gex = scratch[:, 1, 0:TG * (NW - 1)].rearrange("p (j w) -> p j w", j=TG)
        nxt = scratch[:, 3, 0:EC].bitcast(I32)
        less = sb("less", [P, NW - 1])
        tcols = sb("tcols", [P, 4, TG])
        wcol = sb("wcol", [P, TG], I32)
        first_i = sb("first_i", [P, TG], I32)
        blk_i = sb("blk_i", [P, TG], I32)
        shift_i = sb("shift_i", [P, TG], I32)
        bit_i = sb("bit_i", [P, 7, TG], I32)
        flag = sb("flag", [P, 1], I32)
        posr = sb("posr", [P, 2, U], I32)
        recr = [sb("recr_d", [P, 2, U, 2]), sb("recr_s", [P, 2, U, 4])]
        idxr = sb("idxr", [P, 2, U], I32)
        msg = sb("msg", [P, 2, U, D1])
        oh = sb("oh", [P, 2, U, P])
        ohT = sb("ohT", [P, 2, U, P])
        abuf = sb("abuf", [P, 2, U, D])
        el = raw[:, :, :].rearrange("p a b -> p (a b)")[:, 0:2 * U * P].rearrange("p (h c) -> p h c", h=2)
        rT = raw_s[:, :, :].rearrange("p a b -> p (a b)")[:, 0:2 * U * P].rearrange("p (h c) -> p h c", h=2)
        s_ring, n_ring, sT, nT = (scratch[:, n, :] for n in range(4))
        s2a = n_ring
        y = sb("y", [P, CW, D])
        lnst = sb("lnst", [P, CW, 6])
        lnmv = sb("lnmv", [P, CW, 2])
        lnsd = sb("lnsd", [P, CW])
        lnrs = sb("lnrs", [P, CW])
        ident = sb("ident", [P, P])
        upper = sb("upper", [P, P])
        ones = sb("ones", [P, P])
        col = sb("col", [P, P])
        epsc = sb("epsc", [P, 1])
        wA = [sb(f"w_{n}", [P, D]) for n in range(4)]
        bcol = [sb(f"bcol_{n}", [P, 1]) for n in (0, 2)]
        brow = [sb(f"brow_{n}", [P, D]) for n in (1, 3)]
        wL1 = sb("wL1", [P, 2, D])
        bL1 = sb("bL1", [P, D])
        wL2 = sb("wL2", [P, 3 * D])
        wL2T = sb("wL2T", [P, 3, D])
        bL2 = sb("bL2", [P, D])
        th = sb("th", [P, D])
        ph = sb("ph", [P, D])
        thphT = sb("thphT", [P, 2, D])
        fc = sb("fc", [P, D])
        fcT = sb("fcT", [P, D])
        fcs = sb("fcs", [P, D])
        fcsT = sb("fcsT", [P, D])
        bn = sb("bn", [P, 4])
        stats = ohT[:, :, :, :].rearrange("p h u c -> p (h u c)")[:, 0:ITERS * 24].rearrange("p (a b) -> p a b", b=6)
        sq = sb("sq", [P, ITERS * 2])
        small = sb("small", [P, 24])
        diag = sb("diag", [P, P])
        shrow = sb("shrow", [1, D])

        PS = ctx.enter_context(nc.psum_tensor("PS", [P, 8, 512], F32))
        psflat = PS[:, :, :].rearrange("p b c -> p (b c)")

        block = ctx.enter_context(nc.Block())

        ld_edges, ld_x, ld_w = sem("ld_edges"), sem("ld_x"), sem("ld_w")
        init, init_v = sem("init"), sem("init_v")
        filled, taken = sem("filled"), sem("taken")
        vtaken = sem("vtaken")
        tbl0 = sem("tbl0")
        rk = [sem("rk_d"), sem("rk_s")]
        rkl = [sem("rkl_d"), sem("rkl_s")]
        rkp = [sem("rkp_d"), sem("rkp_s")]
        rkq = [sem("rkq_d"), sem("rkq_s")]
        fl_v, fl_p = sem("flag_dve"), sem("flag_pe")
        ld_next, pairs_ok = sem("ld_next"), sem("pairs_ok")
        wc_ok, wc_st, wt_ld = [[sem(f"{n}_{k}") for k in "ds"] for n in ("wcol", "wcol_stored", "wtile_ld")]
        sh_v, sh_got, sh_p = sem("short_dve"), sem("short_got"), sem("short_pe")
        pos_ready = [sem("pos_d"), sem("pos_s")]
        sc_ring = [sem("sc_ring_d"), sem("sc_ring_s")]
        sc_done = [[sem(f"sc_done_{k}{h}") for h in range(2)] for k in "ds"]
        rec_ld = [sem("rec_ld_d"), sem("rec_ld_s")]
        unpacked = [sem("unpacked_d"), sem("unpacked_s")]

        names = ["p1", "p2", "p3", "p4"]
        g_idx = {k: sem(f"{k}_idx") for k in names + ["p5"]}
        g_got = {k: [sem(f"{k}_got{h}") for h in range(2)] for k in names + ["p5"]}
        oh_ok = {k: [sem(f"{k}_oh{h}") for h in range(2)] for k in names + ["p5", "pc"]}
        mm_ok = {k: [sem(f"{k}_mm{h}") for h in range(2)] for k in names + ["pc"]}
        add_ok = {k: sem(f"{k}_add") for k in names + ["pc"]}
        acc_zero = sem("acc_zero")
        scaled = [sem("p3_scaled0"), sem("p3_scaled1")]

        n_pass = {k: sem(f"{k}_end") for k in "ABCDEF"}
        nv = {k: sem(f"n{k}_dve") for k in "ABCDEF"}
        na = {k: sem(f"n{k}_act") for k in "ABCDEF"}
        npe = {k: sem(f"n{k}_pe") for k in "ABCDEF"}
        nst = {k: sem(f"n{k}_store") for k in "ABCE"}
        dn_v, dn_p, dn_a = sem("norm_dve"), sem("norm_pe"), sem("norm_act")
        nv2, na2, nst2 = sem("nD2_dve"), sem("nD2_act"), sem("nD2_store")
        wt_pe, wt_dve = sem("wt_pe"), sem("wt_dve")
        q_tr = [sem("p5_tr0"), sem("p5_tr1")]
        q_a = [sem("p5_a0"), sem("p5_a1")]
        q_t = [sem("p5_t0"), sem("p5_t1")]
        q_e = [sem("p5_e0"), sem("p5_e1")]
        q_sq = [sem("p5_sq0"), sem("p5_sq1")]
        q_cp = [sem("p5_cp0"), sem("p5_cp1")]
        q_st = [sem("p5_st0"), sem("p5_st1")]
        bn_v, bn_a, bn_p = sem("bn_dve"), sem("bn_act"), sem("bn_pe")
        b_ld = [sem("b_ld0"), sem("b_ld1")]
        b_r = [sem("b_r0"), sem("b_r1")]
        b_mm = [sem("b_mm0"), sem("b_mm1")]
        b_bn = [sem("b_bn0"), sem("b_bn1")]
        c_ld = [sem("c_ld0"), sem("c_ld1")]
        c_r = [sem("c_r0"), sem("c_r1")]
        c_e = [sem("c_e0"), sem("c_e1")]
        c_y = [sem("c_y0"), sem("c_y1")]
        res_st = sem("res_st")

        scale0, mu0, mfc, sh1 = small[:, 0:1], small[:, 1:2], small[:, 2:3], small[:, 3:4]

        def cols8(i, h):
            return bass.ds(i * (2 * U) + h * U, U)

        @block.sync
        def _(sp):
            sp.wait_ge(init_v, IV)
            for k, a in ((0, dst), (1, src)):
                sp.dma_start(key_i[0:EP, k, :], a[0:EP * EC].rearrange("(p c) -> p c", p=EP)).then_inc(ld_edges, 16)
                sp.dma_start(key_i[EP:P, k, 0:ER], a[EP * EC:E].rearrange("(p c) -> p c", p=1)).then_inc(ld_edges, 16)
            sp.dma_start(nxt[0:EP, :], dst[1:EP * EC + 1].rearrange("(p c) -> p c", p=EP)).then_inc(ld_next, 16)
            sp.dma_start(nxt[EP:P, 0:ER - 1], dst[EP * EC + 1:E].rearrange("(p c) -> p c", p=1)).then_inc(ld_next, 16)
            w = edge_weight1.rearrange("e o -> (e o)")
            sp.dma_start(wgt[0:EP, :], w[0:EP * EC].rearrange("(p c) -> p c", p=EP)).then_inc(ld_edges, 16)
            sp.dma_start(wgt[EP:P, 0:ER], w[EP * EC:E].rearrange("(p c) -> p c", p=1)).then_inc(ld_edges, 16)
            sp.dma_start(pairs[EB - 2:EB, :, :].rearrange("q k c -> q (k c)"), gidx[0][0:2, 0:4 * P]).then_inc(pairs_ok, 16)
            sp.wait_ge(pairs_ok, 16)
            for k, a in ((0, src), (2, dst)):
                sp.dma_start(pairs[0:EB - 1, k, :], a[0:E - EL].rearrange("(q c) -> q c", c=P)).then_inc(pairs_ok, 16)
                sp.dma_start(pairs[0:EB - 2, k + 1, :], a[P:E - EL].rearrange("(q c) -> q c", c=P)).then_inc(pairs_ok, 16)
                sp.dma_start(pairs[EB - 1:EB, k, 0:EL], a[E - EL:E].rearrange("(q c) -> q c", q=1)).then_inc(pairs_ok, 16)
                sp.dma_start(pairs[EB - 2:EB - 1, k + 1, 0:EL], a[E - EL:E].rearrange("(q c) -> q c", q=1)).then_inc(pairs_ok, 16)
            sp.dma_start(x0[:, 0:NW - 1, :], x[0:(NW - 1) * P, :].rearrange("(w p) f -> p w f", p=P)).then_inc(ld_x, 16)
            sp.dma_start(x0[0:TAIL, NW - 1, :], x[(NW - 1) * P:N, :]).then_inc(ld_x, 16)
            for t, a in ((wA[0], W1), (wA[1], W2), (wA[2], W3), (wA[3], W4), (th, theta_w), (ph, phi_w), (fc, fc1_w)):
                sp.dma_start(t[:, :], a).then_inc(ld_w, 16)
            sp.dma_start(wL1[:, :, :], L1W.rearrange("(k p) n -> p k n", p=P)).then_inc(ld_w, 16)
            sp.dma_start(wL2[:, :], L2W).then_inc(ld_w, 16)
            for t, a in ((bcol[0][:, :], b1), (bcol[1][:, :], b3), (bn[:, 0:1], bn0_g), (bn[:, 1:2], bn0_b),
                         (bn[:, 2:3], bn1_g), (bn[:, 3:4], bn1_b)):
                sp.dma_start(t, a.rearrange("(p o) -> p o", o=1)).then_inc(ld_w, 16)
            for t, a in ((brow[0], b2), (brow[1], b4), (bL1, L1b), (bL2, L2b)):
                sp.dma_start(t[:, :], a.rearrange("(o f) -> o f", o=1).to_broadcast([P, D])).then_inc(ld_w, 16)
            sp.wait_ge(init, 6)
            sp.dma_start(rec_dst.rearrange("(p t) r -> p t r", p=P), rec[0][:, :, :]).then_inc(filled, 16)
            sp.dma_start(rec_src.rearrange("(p t) r -> p t r", p=P), rec[1][:, :, :]).then_inc(filled, 16)
            sp.dma_start(table[NP:NP + P, :], zeros_e[:, 0:D]).then_inc(tbl0, 16)
            sp.wait_ge(ld_x, 32)
            sp.dma_start(table_w, x0[:, :, :]).then_inc(tbl0, 16)

            def window_rows(k):
                sp.wait_ge(wc_ok[k], 1)
                sp.dma_start(wdram[k], wcol[:, :]).then_inc(wc_st[k], 16)
                sp.wait_ge(wc_st[k], 16)
                sp.dma_start(wtile[k][:, :], wdram[k].rearrange("(o p) j -> o (p j)", o=1)).then_inc(wt_ld[k], 16)

            def load_records(k):
                for h in range(2):
                    sp.wait_ge(sc_done[k][h], EC // 2 * 16)
                sp.dma_start(rec[k][:, :, :], (rec_dst, rec_src)[k].rearrange("(p t) r -> p t r", p=P)).then_inc(rec_ld[k], 16)

            window_rows(0)
            sp.wait_ge(fl_v, FLV)
            unsorted = sp.value_load(flag[0:1, 0:1], min_val=0, max_val=1)
            with sp.If(unsorted == 1):
                load_records(0)
            window_rows(1)

            def store_chunks(ph_, ready, K, sem_, src_of):
                with sp.Fori(0, NCH) as i:
                    sp.wait_ge(ready, i * K + K)
                    sp.dma_start(table_w[:, bass.ds(i * CW, CW), :], src_of(i)).then_inc(sem_, 16)

            store_chunks("A", na["A"], 3, nst["A"], lambda i: cur[:, bass.ds(i * CW, CW), :])
            store_chunks("B", nv["B"], KB, nst["B"], lambda i: cur[:, bass.ds(i * CW, CW), :])
            load_records(1)
            store_chunks("C", nv["C"], KC, nst["C"], lambda i: cur[:, bass.ds(i * CW, CW), :])
            with sp.Fori(0, NCH) as i:
                sp.wait_ge(nv["E"], i * 3 + 2)
                sp.dma_start(table_w[:, bass.ds(i * CW, CW), :], y[:, :, :]).then_inc(nst["E"], 16)
            with sp.Fori(0, ITERS) as i:
                for h in range(2):
                    sp.wait_ge(q_cp[h], i + 1)
                    sp.dma_start(e_store[i * 2 + h, :, :], el[:, h, :]).then_inc(q_st[h], 16)
            for h in range(2):
                sp.wait_ge(q_st[h], ITERS * 16)
            with sp.Fori(0, ITERS) as i:
                for h in range(2):
                    sp.wait_ge(b_r[h], i)
                    sp.dma_start(el[:, h, :], e_store[i * 2 + h, :, :]).then_inc(b_ld[h], 16)
            for h in range(2):
                sp.wait_ge(b_r[h], ITERS)
            with sp.Fori(0, ITERS) as i:
                for h in range(2):
                    sp.wait_ge(c_r[h], i)
                    sp.dma_start(el[:, h, :], e_store[i * 2 + h, :, :]).then_inc(c_ld[h], 16)
            sp.wait_ge(nv["F"], NCH * KF)
            sp.dma_start(out[0:(NW - 1) * P, :].rearrange("(w p) f -> p w f", p=P), cur[:, 0:NW - 1, :]).then_inc(res_st, 16)
            sp.dma_start(out[(NW - 1) * P:N, :], cur[0:TAIL, NW - 1, :]).then_inc(res_st, 16)
            sp.wait_ge(res_st, 32)

        @block.gpsimd
        def _(pool):
            pool.iota(wnum[:, :], pattern=[[1, NW + 1]], base=0, channel_multiplier=0,
                      allow_small_or_imprecise_dtypes=True).then_inc(init, 1)
            pool.iota(tnum[:, :], pattern=[[1, TG]], base=0, channel_multiplier=TG,
                      allow_small_or_imprecise_dtypes=True).then_inc(init, 1)
            pool.iota(col[:, :], pattern=[[1, P]], base=0, channel_multiplier=0,
                      allow_small_or_imprecise_dtypes=True).then_inc(init, 1)
            pool.wait_ge(init_v, 5)
            pool.affine_select(out=ident[:, :], in_=ident[:, :], compare_op=ALU.not_equal, fill=1.0,
                               base=0, pattern=[[-1, P]], channel_multiplier=1).then_inc(init, 1)
            pool.affine_select(out=upper[:, :], in_=upper[:, :], compare_op=ALU.is_gt, fill=0.0,
                               base=0, pattern=[[1, P]], channel_multiplier=-1).then_inc(init, 1)
            pool.memset(epsc[:, :], EPS).then_inc(init, 1)

            def scatter(k, r, a, b):
                with pool.Fori(a, b) as i:
                    for h in range(2):
                        pool.wait_ge(sc_done[k][h], i * (16 * U))
                        pool.tensor_copy(posr[:, h, :], pos[:, k, cols8(i, h)]).then_inc(sc_ring[k], 1)
                        pool.tensor_copy(recr[k][:, h, :, 0:2 + k], (raw, raw_s)[k][:, cols8(i, h), 0:2 + k]).then_inc(sc_ring[k], 1)
                        pool.wait_ge(sc_ring[k], i * 4 + (2 * h + 2))
                        pool.sem_inc(taken, 1)
                        for u in range(U):
                            pool.indirect_dma_start(
                                r, bass.IndirectOffsetOnAxis(ap=posr[:, h, u:u + 1], axis=0),
                                recr[k][:, h, u, :], None).then_inc(sc_done[k][h], 16)

            def gather(name, free, n, iters):
                with pool.Fori(0, iters) as i:
                    for h in range(2):
                        pool.wait_ge(free[h], i)
                        pool.wait_ge(g_idx[name], i * 2 + (h + 1))
                        pool.sem_inc(taken, 1)
                        for u in range(n):
                            pool.indirect_dma_start(
                                msg[:, h, u, 0:D], None, table,
                                bass.IndirectOffsetOnAxis(ap=idxr[:, h, u:u + 1], axis=0)).then_inc(g_got[name][h], 16)

            pool.wait_ge(filled, 32)
            pool.wait_ge(pairs_ok, 16 * 9)
            pool.wait_ge(fl_v, FLV)
            unsorted = pool.value_load(flag[0:1, 0:1], min_val=0, max_val=1)
            with pool.If(unsorted == 1):
                pool.wait_ge(pos_ready[0], 1)
                scatter(0, rec_dst, 0, SCI)
            with pool.Else():
                pool.wait_ge(sh_v, SHQ)
                for j in range(TG):
                    pool.indirect_dma_start(
                        blk[:, j, :, :].rearrange("p k c -> p (k c)"), None, pairs.rearrange("q k c -> q (k c)"),
                        bass.IndirectOffsetOnAxis(ap=blk_i[:, j:j + 1], axis=0)).then_inc(sh_got, 16)
            pool.wait_ge(tbl0, 32)
            gather("p1", mm_ok["p1"], U, ITERS)
            pool.wait_ge(pos_ready[1], 1)
            scatter(1, rec_src, 0, SCI // 2)
            pool.wait_ge(nst["A"], 16 * NCH)
            gather("p2", mm_ok["p2"], U, ITERS)
            scatter(1, rec_src, SCI // 2, SCI)
            pool.wait_ge(nst["B"], 16 * NCH)
            gather("p3", mm_ok["p3"], U, ITERS)
            pool.wait_ge(nst["C"], 16 * NCH)
            gather("p4", mm_ok["p4"], U, ITERS)
            pool.wait_ge(nst["E"], 16 * NCH)
            gather("p5", q_e, U, ITERS)

        @block.scalar
        def _(act):
            def unpack(k):
                act.wait_ge(rec_ld[k], 16)
                act.copy(gidx[k][:, :], rec[k][:, :, 0]).then_inc(unpacked[k], 1)
                act.wait_ge(unpacked[k], 1)

            def index_ring(name, k, scale=False):
                for h in range(2):
                    act.copy(idxr[:, h, :], gidx[k][:, h * U:(h + 1) * U]).then_inc(g_idx[name], 1)
                with act.Fori(0, ITERS) as i:
                    for h in range(2):
                        act.wait_ge(g_got[name][h], i * (16 * U) + 16 * U)
                        act.copy(idxr[:, h, :], gidx[k][:, bass.ds(i * (2 * U) + (2 + h) * U, U)]).then_inc(g_idx[name], 1)
                        if scale:
                            for u in range(U):
                                act.activation(msg[:, h, u, 0:D], msg[:, h, u, 0:D], ACT.Copy,
                                               scale=rec[k][:, bass.ds(i * (2 * U) + (h * U + u), 1), 2]).then_inc(scaled[h], 1)

            act.wait_ge(unpacked[0], 1)
            index_ring("p1", 0)

            def conv(p, b, last):
                with act.Fori(0, NCH) as i:
                    act.wait_ge(npe[p], i * 3 + 1)
                    act.copy(sT[:, :], psflat[:, 0:C]).then_inc(na[p], 1)
                    act.wait_ge(npe[p], i * 3 + 2)
                    act.activation(nT[:, :], psflat[:, 1024:1024 + C], ACT.Relu, bias=b[:, :]).then_inc(na[p], 1)
                    last(i)

            def relu_h1(i):
                act.wait_ge(nv["A"], i * 2 + 2)
                act.activation(cur[:, bass.ds(i * CW, CW), :], y[:, :, :], ACT.Relu).then_inc(na["A"], 1)

            def ln_sqrt(sem_a, sem_v, i, K, k):
                act.wait_ge(sem_v, i * K + k)
                act.activation(lnsd[:, :], lnmv[:, :, 1], ACT.Sqrt, bias=epsc[:, :]).then_inc(sem_a, 1)

            act.wait_ge(ld_w, 16 * 19)
            conv("A", bcol[0], relu_h1)
            act.wait_ge(na["A"], 3 * NCH)
            index_ring("p2", 0)
            conv("B", bcol[1], lambda i: ln_sqrt(na["B"], nv["B"], i, KB, LNB))
            unpack(1)
            index_ring("p3", 1, scale=True)

            def sage(p, K, last):
                with act.Fori(0, NCH) as i:
                    act.wait_ge(npe[p], i * 3 + 1)
                    act.copy(sT[:, :], psflat[:, 0:C]).then_inc(na[p], 1)
                    act.wait_ge(npe[p], i * 3 + 2)
                    act.copy(nT[:, :], psflat[:, 1024:1024 + C]).then_inc(na[p], 1)
                    last(i)

            sage("C", KC, lambda i: ln_sqrt(na["C"], nv["C"], i, KC, LNC))
            index_ring("p4", 0)

            def tanh_d(i):
                act.wait_ge(nv["D"], i * 3 + 3)
                act.activation(x0[:, bass.ds(i * CW, CW), :], y[:, :, :], ACT.Tanh).then_inc(na["D"], 1)

            sage("D", 3, tanh_d)
            act.wait_ge(dn_p, 1)
            act.activation(small[:, 4:5], psflat[:, 0:1], ACT.Sqrt).then_inc(dn_a, 1)
            with act.Fori(0, NCH) as i:
                ln_sqrt(na2, nv2, i, KD2, LND2)
            with act.Fori(0, NCH) as i:
                act.wait_ge(npe["E"], i * 3 + 1)
                act.copy(sT[:, :], psflat[:, 0:C]).then_inc(na["E"], 1)
            act.wait_ge(bn_v, 4)
            for h in range(2):
                act.wait_ge(g_got["p4"][h], ITERS * 16 * U)
                act.copy(idxr[:, h, :], gidx[0][:, h * U:(h + 1) * U]).then_inc(g_idx["p5"], 1)
            with act.Fori(0, ITERS) as i:
                for h in range(2):
                    act.wait_ge(q_e[h], i)
                    act.wait_ge(q_tr[h], i + 1)
                    act.copy(ohT[:, h, :, :], PS[:, 2 * h:2 * h + 2, :].rearrange("p b (u c) -> p (b u) c", c=P)).then_inc(q_t[h], 1)
                    act.wait_ge(q_e[h], i + 1)
                    act.wait_ge(q_st[h], i * 16)
                    e = psflat[:, (4 + 2 * h) * 512:(6 + 2 * h) * 512]
                    act.copy(el[:, h, :], e).then_inc(q_cp[h], 1)
                    act.activation(rT[:, h, :], e, ACT.Square, accum_out=sq[:, bass.ds(i * 2 + h, 1)]).then_inc(q_sq[h], 1)
                    act.wait_ge(g_got["p5"][h], i * (16 * U) + 16 * U)
                    act.copy(idxr[:, h, :], gidx[0][:, bass.ds(i * (2 * U) + (2 + h) * U, U)]).then_inc(g_idx["p5"], 1)
            act.wait_ge(bn_v, 6)
            act.activation(small[:, 5:6], small[:, 6:7], ACT.Sqrt, bias=epsc[:, :]).then_inc(bn_a, 1)
            act.wait_ge(bn_v, 8)
            act.activation(small[:, 8:9], bn[:, 1:2], ACT.Relu).then_inc(bn_a, 1)
            with act.Fori(0, ITERS) as i:
                for h in range(2):
                    act.wait_ge(b_ld[h], i * 16 + 16)
                    act.wait_ge(b_mm[h], i)
                    act.activation(rT[:, h, :], el[:, h, :], ACT.Relu, bias=bn[:, 1:2], scale=scale0).then_inc(b_r[h], 1)
            act.wait_ge(bn_v, BNV)
            act.activation(small[:, 15:16], small[:, 14:15], ACT.Sqrt, bias=epsc[:, :]).then_inc(bn_a, 1)
            for h in range(2):
                act.wait_ge(b_mm[h], ITERS)

            def c_relu(h, i):
                act.wait_ge(c_ld[h], i * 16 + 16)
                act.wait_ge(c_e[h], i)
                act.activation(rT[:, h, :], el[:, h, :], ACT.Relu, bias=bn[:, 1:2], scale=scale0).then_inc(c_r[h], 1)

            def c_turn(i, last=False):
                for h in range(2):
                    if not (last and h):
                        c_relu(1 - h, i + h)
                    act.wait_ge(c_e[h], i + 1)
                    act.wait_ge(mm_ok["pc"][h], i)
                    act.activation(msg[:, h, :, 0:D], PS[:, 2 * h:2 * h + 2, :].rearrange("p b (u c) -> p (b u) c", c=D),
                                   ACT.Relu).then_inc(c_y[h], 1)

            c_relu(0, 0)
            with act.Fori(0, ITERS - 1) as i:
                c_turn(i)
            c_turn(ITERS - 1, last=True)
            with act.Fori(0, NCH) as i:
                ln_sqrt(na["F"], nv["F"], i, KF, LNF)

        @block.tensor
        def _(pe):
            pe.wait_ge(init, 6)
            pe.wait_ge(init_v, IV)
            pe.wait_ge(fl_v, 2)
            pe.matmul(PS[:, 5, 0:1], ones[:, :], small[:, 5:6], start=True, stop=True).then_inc(fl_p, 1)

            def count_sums(k):
                pe.wait_ge(rkl[k], NW + 1)
                pe.matmul(PS[:, 6, 0:NW + 1], upper[:, :], cnt[:, :], start=True, stop=True).then_inc(rkp[k], 1)
                pe.matmul(PS[:, 7, 0:NW + 1], ones[:, :], cnt[:, :], start=True, stop=True).then_inc(rkp[k], 1)

            count_sums(0)
            pe.wait_ge(fl_v, FLV)
            unsorted = pe.value_load(flag[0:1, 0:1], min_val=0, max_val=1)
            with pe.If(unsorted == 0):
                pe.wait_ge(sh_v, SHL)
                for k in range(2):
                    for j in range(TG):
                        mm = pe.transpose(psflat[:, k * 1024 + j * P:k * 1024 + (j + 1) * P], lanes[:, k, j, :], ident[:, :])
                mm.then_inc(sh_p, 1)
            count_sums(1)
            pe.wait_ge(ld_w, 16 * 19)
            for n in range(3):
                pe.transpose(PS[:, 4, n * P:(n + 1) * P], wL2[:, n * D:(n + 1) * D], ident[:, :]).then_inc(wt_pe, 1)
            pe.transpose(PS[:, 4, 3 * P:4 * P], th[:, :], ident[:, :]).then_inc(wt_pe, 1)
            pe.wait_ge(wt_dve, 1)
            pe.transpose(PS[:, 5, 0:P], ph[:, :], ident[:, :]).then_inc(wt_pe, 1)
            pe.transpose(PS[:, 5, P:2 * P], fc[:, :], ident[:, :]).then_inc(wt_pe, 1)

            def slot(h, u):
                return PS[:, 3 * h + u // 3, (u % 3) * D1:(u % 3 + 1) * D1]

            def segsum(name):
                with pe.Fori(0, ITERS) as i:
                    for h in range(2):
                        pe.wait_ge(oh_ok[name][h], i + 1)
                        pe.wait_ge(g_got[name][h], (i + 1) * (16 * U))
                        if name == "p3":
                            pe.wait_ge(scaled[h], i * U + U)
                        pe.wait_ge(add_ok[name], i * (2 * U))
                        for u in range(U):
                            mm = pe.matmul(slot(h, u), oh[:, h, u, :], msg[:, h, u, :], start=True, stop=True)
                        mm.then_inc(mm_ok[name][h], 1)

            def turn_chunk(to, frm):
                for j in range(CW):
                    mm = pe.transpose(psflat[:, to + j * P:to + (j + 1) * P], frm[:, j * P:(j + 1) * P], ident[:, :])
                return mm

            def conv(p, wa, wb, kv, s_step):
                with pe.Fori(0, NCH) as i:
                    pe.wait_ge(nv[p], i * kv + s_step)
                    turn_chunk(0, s_ring).then_inc(npe[p], 1)
                    pe.wait_ge(na[p], i * 3 + 1)
                    pe.matmul(psflat[:, 1024:1536], wa[:, :], sT[:, 0:512], start=True, stop=True)
                    pe.matmul(psflat[:, 1536:1024 + C], wa[:, :], sT[:, 512:C], start=True, stop=True).then_inc(npe[p], 1)
                    pe.wait_ge(na[p], i * 3 + 2)
                    for j in range(CW):
                        mm = pe.matmul(psflat[:, 2048 + j * P:2048 + (j + 1) * P], nT[:, j * P:(j + 1) * P], wb[:, :],
                                       start=True, stop=True)
                    mm.then_inc(npe[p], 1)

            def sage(p, kv, ws_x, w_n):
                with pe.Fori(0, NCH) as i:
                    pe.wait_ge(nv[p], i * kv + 2)
                    turn_chunk(0, s_ring).then_inc(npe[p], 1)
                    turn_chunk(1024, n_ring).then_inc(npe[p], 1)
                    pe.wait_ge(na[p], i * 3 + 2)
                    for j in range(CW):
                        o = psflat[:, 2048 + j * P:2048 + (j + 1) * P]
                        for n, wx in enumerate(ws_x):
                            pe.matmul(o, sT[:, j * P:(j + 1) * P], wx, start=(n == 0), stop=False)
                        mm = pe.matmul(o, nT[:, j * P:(j + 1) * P], w_n, start=False, stop=True)
                    mm.then_inc(npe[p], 1)

            segsum("p1")
            conv("A", wA[0], wA[1], 2, 1)
            segsum("p2")
            conv("B", wA[2], wA[3], KB, 1)
            segsum("p3")
            sage("C", KC, [wL1[:, 0, :]], wL1[:, 1, :])
            segsum("p4")
            sage("D", 3, [wL2T[:, 0, :], wL2T[:, 2, :]], wL2T[:, 1, :])
            pe.wait_ge(dn_v, 3)
            pe.matmul(psflat[:, 0:1], ones[:, :], small[:, 7:8], start=True, stop=True).then_inc(dn_p, 1)
            pe.wait_ge(dn_v, 4)
            with pe.Fori(0, NCH) as i:
                pe.wait_ge(nv["E"], i * 3 + 1)
                turn_chunk(0, s_ring).then_inc(npe["E"], 1)
                pe.wait_ge(na["E"], i + 1)
                for j in range(CW):
                    mm = pe.matmul(psflat[:, 1024 + j * 256:1280 + j * 256], sT[:, j * P:(j + 1) * P],
                                   thphT[:, :, :].rearrange("p a c -> p (a c)"), start=True, stop=True)
                mm.then_inc(npe["E"], 1)
                pe.wait_ge(nv["E"], i * 3 + 2)
                for j in range(CW):
                    pe.matmul(psflat[:, 3072:3073], s2a[:, j * P:(j + 1) * P], deg_dst[:, bass.ds(i * CW + j, 1)],
                              start=(j == 0), stop=False)
                    mm = pe.matmul(psflat[:, 3072:3073], y[:, j, :], deg_src[:, bass.ds(i * CW + j, 1)],
                                   start=False, stop=(j == CW - 1))
                mm.then_inc(npe["E"], 1)
            pe.wait_ge(bn_v, 3)
            pe.matmul(PS[:, 7, 0:P], ones[:, :], diag[:, :], start=True, stop=True).then_inc(bn_p, 1)
            pe.wait_ge(bn_v, 4)
            with pe.Fori(0, ITERS) as i:
                for h in range(2):
                    pe.wait_ge(oh_ok["p5"][h], i + 1)
                    pe.wait_ge(q_t[h], i)
                    for u in range(U):
                        mm = pe.transpose(PS[:, 2 * h + u // 4, (u % 4) * P:(u % 4 + 1) * P], oh[:, h, u, :], ident[:, :])
                    mm.then_inc(q_tr[h], 1)
                    pe.wait_ge(q_t[h], i + 1)
                    pe.wait_ge(q_a[h], i * U + U)
                    pe.wait_ge(g_got["p5"][h], (i + 1) * (16 * U))
                    pe.wait_ge(q_sq[h], i)
                    for u in range(U):
                        o = PS[:, 4 + 2 * h + u // 4, (u % 4) * P:(u % 4 + 1) * P]
                        pe.matmul(o, abuf[:, h, u, :], ohT[:, h, u, :], start=True, stop=False)
                        mm = pe.matmul(o, msg[:, h, u, 0:D], ident[:, :], start=False, stop=True)
                    mm.then_inc(q_e[h], 1)
            for h in range(2):
                pe.wait_ge(q_sq[h], ITERS)
            pe.wait_ge(bn_a, 2)
            pe.matmul(PS[:, 7, 0:1], fcT[:, :], small[:, 8:9], start=True, stop=True).then_inc(bn_p, 1)
            with pe.Fori(0, ITERS) as i:
                for h in range(2):
                    pe.wait_ge(b_r[h], i + 1)
                    pe.wait_ge(b_bn[h], i * 2)
                    for s in range(2):
                        mm = pe.matmul(PS[:, 2 * h + s, :], fcT[:, :], rT[:, h, s * 512:(s + 1) * 512], start=True, stop=True)
                    mm.then_inc(b_mm[h], 1)
            pe.wait_ge(bn_v, BNV + 2)
            pe.transpose(PS[:, 6, 0:P], fcs[:, :], ident[:, :]).then_inc(bn_p, 1)
            pe.transpose(PS[0:1, 6, P:2 * P], sh1, ident[:, :]).then_inc(bn_p, 1)
            pe.wait_ge(bn_v, BNV + 4)

            def c_product(h, i):
                pe.wait_ge(c_r[h], i + 1)
                pe.wait_ge(c_y[h], i)
                for u in range(U):
                    o = PS[:, 2 * h + u // 4, (u % 4) * P:(u % 4 + 1) * P]
                    pe.matmul(o, rT[:, h, u * P:(u + 1) * P], fcsT[:, :], start=True, stop=False)
                    mm = pe.matmul(o, ones[0:1, :], shrow[:, :], start=False, stop=True)
                mm.then_inc(c_e[h], 1)

            def c_turn(i, last=False):
                for h in range(2):
                    if not (last and h):
                        c_product(1 - h, i + h)
                    pe.wait_ge(c_y[h], i + 1)
                    pe.wait_ge(oh_ok["pc"][h], i + 1)
                    pe.wait_ge(add_ok["pc"], i * (2 * U))
                    for u in range(U):
                        mm = pe.matmul(PS[:, 4 + 2 * h + u // 4, (u % 4) * P:(u % 4 + 1) * P], oh[:, h, u, :],
                                       msg[:, h, u, 0:D], start=True, stop=True)
                    mm.then_inc(mm_ok["pc"][h], 1)

            c_product(0, 0)
            with pe.Fori(0, ITERS - 1) as i:
                c_turn(i)
            c_turn(ITERS - 1, last=True)

        @block.vector
        def _(dve):
            v = Count(dve, init_v)
            v.inc(dve.memset(key_i[:, :, :], NP))
            v.inc(dve.memset(wgt[:, :], 0.0))                 
            v.inc(dve.memset(ident[:, :], 0.0))
            v.inc(dve.memset(ones[:, :], 1.0))
            v.inc(dve.memset(upper[:, :], 1.0))
            v.inc(dve.memset(zeros_e[:, :], 0.0))
            for k in range(2):
                v.inc(dve.memset(rec[k][:, :, 0], float(ZROW)))
                v.inc(dve.memset(rec[k][:, :, 1], -1.0))
                v.inc(dve.memset(rec[1][:, :, 2 + k], 0.0))
            v.inc(dve.memset(msg[:, :, :, D:D1], 1.0))
            v.inc(dve.memset(x0[:, NW - 1, :], 0.0))
            v.inc(dve.memset(recr[1][:, :, :, :], 0.0))
            v.inc(dve.memset(nxt, NP))
            v.inc(dve.memset(gidx[0][:, :], 0))
            v.link(dve.memset(small[:, :], 0.0))
            v.link(dve.memset(small[0:TAIL, 20:21], 1.0))
            dve.wait_ge(ld_edges, 96)
            dve.wait_ge(init, 6)

            assert v.n == IV, v.n
            f = Count(dve, fl_v)
            dve.wait_ge(ld_next, 32)
            f.link(dve.tensor_tensor(scan[:, 0, :], key_i[:, 0, :], nxt, ALU.is_gt))
            f.link(dve.tensor_reduce(small[:, 5:6], scan[:, 0, :], AX.X, ALU.add))
            dve.wait_ge(fl_p, 1)
            f.link(dve.tensor_scalar(small[:, 6:7], PS[:, 5, 0:1], 1.0, None, ALU.min))
            f.link(dve.tensor_copy(flag[:, :], small[:, 6:7]))
            assert f.n == FLV
            cc = [Count(dve, rk[k]) for k in range(2)]

            def rows(a, n):
                return a.rearrange("p (j o) -> p j o", o=1).to_broadcast([P, a.shape[1], n])

            def each(a, n):
                return a.rearrange("p (o c) -> p o c", o=1).to_broadcast([P, n, a.shape[1]])

            def count(k):
                c = cc[k]
                hi = mask[:, 1, :]
                c.link(dve.tensor_scalar(hi, key_i[:, k, :], 7, None, ALU.arith_shift_right))
                c.link(dve.tensor_copy(winf[:, :], hi))
                with dve.Fori(0, NW + 1) as i:
                    dve.wait_ge(rkl[k], i)
                    dve.tensor_scalar(scan[:, 0, :], winf[:, :], wnum[:, bass.ds(i, 1)], None, ALU.is_equal, ALU.add,
                                      accum_out=cnt[:, bass.ds(i, 1)]).then_inc(rkl[k], 1)
                dve.wait_ge(rkp[k], 2)
                c.link(dve.tensor_copy(tot[:, :], PS[:, 7, 0:NW + 1]))
                c.link(dve.tensor_scalar(tiles_f[:, :], tot[:, :], float(P - 1), None, ALU.add))
                c.link(dve.tensor_copy(tiles_i[:, :], tiles_f[:, :]))
                c.link(dve.tensor_scalar(tiles_i[:, :], tiles_i[:, :], 7, None, ALU.arith_shift_right))
                c.link(dve.tensor_copy(tiles_f[:, :], tiles_i[:, :]))
                c.link(dve.tensor_tensor_scan(tend[:, :], tiles_f[:, :], zeros_e[:, 0:NW + 1], 0.0, ALU.add, ALU.add))
                c.link(dve.tensor_tensor(off[:, :], tend[:, :], tiles_f[:, :], ALU.subtract))
                c.link(dve.memset(off[:, NW:NW + 1], float(T)))
                c.link(dve.tensor_scalar(off[:, :], off[:, :], float(P), -1.0, ALU.mult, ALU.add))
                c.link(dve.tensor_tensor(off[:, :], off[:, :], PS[:, 6, 0:NW + 1], ALU.add))
                if k:
                    dve.wait_ge(wc_st[0], 16)
                c.link(dve.tensor_tensor(ge, rows(tnum[:, :], NW - 1), each(tend[:, 0:NW - 1], TG), ALU.is_ge))
                c.link(dve.tensor_reduce(tcols[:, 0, :], ge, AX.X, ALU.add))
                dve.tensor_copy(wcol[:, :], tcols[:, 0, :]).then_inc(wc_ok[k], 1)

            def records(k):
                c, r = cc[k], (raw, raw_s)[k]
                lo = mask[:, 0, :]
                c.link(dve.tensor_scalar(lo, key_i[:, k, :], P - 1, None, ALU.bitwise_and))
                c.inc(dve.tensor_copy(r[:, :, 1], lo))
                c.inc(dve.tensor_copy(r[:, :, 0], key_i[:, 1 - k, :]))
                c.inc(dve.tensor_copy(r[:, :, 2], wgt[:, :]))
                c.wait()

            def place_mask(k, i):
                dve.wait_ge(rkq[k], i * 3)
                dve.tensor_scalar(mask[:, 0, :], winf[:, :], wnum[:, bass.ds(i, 1)], None, ALU.is_equal).then_inc(rkq[k], 1)

            def place_scan(k, i):
                dve.wait_ge(rkq[k], i * 3 + 1)
                dve.tensor_tensor_scan(scan[:, 0, :], mask[:, 0, :], zeros_e[:, :], off[:, bass.ds(i, 1)],
                                       ALU.add, ALU.add).then_inc(rkq[k], 1)

            def place_take(k, i):
                dve.wait_ge(rkq[k], i * 3 + 2)
                dve.sem_inc(vtaken, 1)
                dve.copy_predicated(posf[:, :], mask[:, 0, :], scan[:, 0, :]).then_inc(rkq[k], 1)

            def place_end(k):
                c = cc[k]
                lo, hi = mask[:, 0, :], mask[:, 1, :]
                dve.wait_ge(rkq[k], 3 * (NW + 1))
                c.link(dve.tensor_copy(pos[:, k, :], posf[:, :]))
                c.inc(dve.tensor_scalar(lo, pos[:, k, :], P - 1, None, ALU.bitwise_and))
                c.link(dve.tensor_scalar(hi, pos[:, k, :], 7, None, ALU.arith_shift_right))
                c.inc(dve.tensor_copy(scan[:, 0, :], lo))
                c.link(dve.tensor_copy(scan[:, 1, :], hi))
                dve.scalar_tensor_tensor(out=pos[:, k, :], in0=scan[:, 0, :], scalar=float(TT), in1=scan[:, 1, :],
                                         op0=ALU.mult, op1=ALU.add).then_inc(pos_ready[k], 1)
                dve.wait_ge(pos_ready[k], 1)

            def long_way():
                records(0)
                with dve.Fori(0, NW + 1) as i:
                    place_mask(0, i)
                    place_scan(0, i)
                    place_take(0, i)
                place_end(0)
                dve.wait_ge(rec_ld[0], 16)

            def short_way():
                c = Count(dve, sh_v)
                c.link(dve.scalar_tensor_tensor(out=less[:, :], in0=tiles_f[:, 0:NW - 1], scalar=-float(P),
                                                in1=tot[:, 0:NW - 1], op0=ALU.mult, op1=ALU.add))
                c.link(dve.tensor_tensor(gex, ge, each(less[:, :], TG), ALU.mult))
                c.link(dve.tensor_reduce(tcols[:, 1, :], gex, AX.X, ALU.add))
                c.link(dve.scalar_tensor_tensor(out=tcols[:, 1, :], in0=tnum[:, :], scalar=float(P), in1=tcols[:, 1, :],
                                                op0=ALU.mult, op1=ALU.add))
                c.link(dve.tensor_tensor(gex, ge, each(tot[:, 1:NW], TG), ALU.mult))
                c.link(dve.tensor_reduce(tcols[:, 2, :], gex, AX.X, ALU.add))
                c.link(dve.tensor_scalar(tcols[:, 2, :], tcols[:, 2, :], tot[:, 0:1], None, ALU.add))
                c.link(dve.tensor_tensor(tcols[:, 3, :], tcols[:, 2, :], tcols[:, 1, :], ALU.subtract))
                c.link(dve.tensor_copy(first_i[:, :], tcols[:, 1, :]))
                c.link(dve.tensor_scalar(blk_i[:, :], first_i[:, :], 7, None, ALU.arith_shift_right))
                c.link(dve.tensor_copy(tcols[:, 2, :], blk_i[:, :]))
                c.link(dve.tensor_scalar(tcols[:, 2, :], tcols[:, 2, :], float(EB - 1), None, ALU.min))
                c.link(dve.tensor_scalar(shift_i[:, :], first_i[:, :], P - 1, None, ALU.bitwise_and))
                c.link(dve.tensor_copy(blk_i[:, :], tcols[:, 2, :]))
                assert c.n == SHQ
                for b in range(7):
                    c.inc(dve.tensor_scalar(bit_i[:, b, :], shift_i[:, :], 1 << b, None, ALU.bitwise_and))
                c.inc(dve.tensor_tensor(real, each(col[:, :], TG), rows(tcols[:, 3, :], P), ALU.is_lt))
                c.inc(dve.memset(lanes[:, 0, :, :], float(ZROW)))
                c.link(dve.memset(lanes[:, 1, :, :], -1.0))
                dve.wait_ge(sh_got, 16 * TG)
                for b in range(6, -1, -1):
                    w = P - 1 + (1 << b)
                    for k in range(2):
                        c.inc(dve.copy_predicated(blk[:, :, k, 0:w], rows(bit_i[:, b, :], w), blk[:, :, k, 1 << b:w + (1 << b)]))
                    c.wait()
                c.link(dve.tensor_scalar(blk[:, :, 1, 0:P], blk[:, :, 1, 0:P], P - 1, None, ALU.bitwise_and))
                for k in range(2):
                    c.link(dve.tensor_copy(blkf[:, :, k, P:2 * P], blk[:, :, k, 0:P]))
                for k in range(2):
                    c.link(dve.copy_predicated(lanes[:, k, :, :], real, blkf[:, :, k, P:2 * P]))
                assert c.n == SHL, c.n
                dve.wait_ge(sh_p, 1)
                dve.wait_ge(filled, 32)
                for k in range(2):
                    c.link(dve.tensor_copy(rec[0][:, :, k].rearrange("l (p j) -> l j p", j=TG),
                                           psflat[:, k * 1024:k * 1024 + TT].rearrange("l (j p) -> l j p", j=TG)))

            def windows(k, h, i):
                return nc.values_load_multi_w_load_instructions(
                    wtile[k][0:1, cols8(i, h)], engines=[mybir.EngineType.DVE], min_val=0, max_val=NW - 1)[1]

            def one_hots(name, k, h, i, free):
                dve.wait_ge(free[h], i)
                dve.tensor_tensor(oh[:, h, :, :],
                                  col[:, :].rearrange("p (o c) -> p o c", o=1).to_broadcast([P, U, P]),
                                  rec[k][:, cols8(i, h), 1:2].to_broadcast([P, U, P]),
                                  ALU.is_equal).then_inc(oh_ok[name][h], 1)

            def add_windows(name, h, i, ws, got, width):
                dve.wait_ge(mm_ok[name][h], i + 1)
                for u in range(U):
                    dve.wait_ge(add_ok[name], i * (2 * U) + (h * U + u))
                    a = acc[:, bass.ds(ws[u], 1), 0:width]
                    dve.tensor_tensor(a, a, got(h, u), ALU.add).then_inc(add_ok[name], 1)

            def slot(h, u):
                return PS[:, 3 * h + u // 3, (u % 3) * D1:(u % 3 + 1) * D1].rearrange("p (o c) -> p o c", o=1)

            def ahead(name, k, got, width):
                one_hots(name, k, 0, 0, mm_ok[name])

                def turn(i, last=False, rank=False):
                    if rank:
                        place_mask(1, i)
                    for h in range(2):
                        ws = windows(k, h, i)
                        if not (last and h):
                            one_hots(name, k, 1 - h, i + h, mm_ok[name])
                        add_windows(name, h, i, ws, got, width)
                        if rank:
                            (place_scan, place_take)[h](1, i)

                if name == "p1":
                    with dve.Fori(0, NW + 1) as i:
                        turn(i, rank=True)
                with dve.Fori(NW + 1 if name == "p1" else 0, ITERS - 1) as i:
                    turn(i)
                turn(ITERS - 1, last=True)

            z = Count(dve, acc_zero)

            def segsum(name, k):
                if k:
                    dve.wait_ge(rec_ld[k], 16)
                dve.wait_ge(wt_ld[k], 16)
                z.link(dve.memset(acc[:, :, :], 0.0))
                ahead(name, k, slot, D1)
                dve.wait_ge(add_ok[name], T)

            count(0)
            unsorted = dve.value_load(flag[0:1, 0:1], min_val=0, max_val=1)
            with dve.If(unsorted == 1):
                long_way()
            with dve.Else():
                short_way()
            dve.tensor_copy(gidx[0][:, :], rec[0][:, :, 0]).then_inc(unpacked[0], 1)
            dve.wait_ge(unpacked[0], 1)
            count(1)
            records(1)
            dve.wait_ge(ld_w, 16 * 19)
            dve.tensor_tensor(ph[:, :], ph[:, :], th[:, :], ALU.subtract).then_inc(wt_dve, 1)
            dve.wait_ge(wt_pe, 6)
            wd = Count(dve, wt_dve)
            wd.n = 1
            wd.inc(dve.tensor_copy(wL2T[:, :, :], PS[:, 4, 0:384].rearrange("p (a c) -> p a c", a=3)))
            wd.inc(dve.tensor_copy(thphT[:, 0, :], PS[:, 4, 384:512]))
            wd.inc(dve.tensor_copy(thphT[:, 1, :], PS[:, 5, 0:P]))
            wd.link(dve.tensor_copy(fcT[:, :], PS[:, 5, P:2 * P]))

            def wide(a):
                return a.rearrange("p (j o) -> p j o", o=1).to_broadcast([P, CW, D])

            def brc(a):
                return a[:, :].rearrange("p (o c) -> p o c", o=1).to_broadcast([P, CW, D])

            s3 = s_ring[:, :].rearrange("p (j c) -> p j c", j=CW)
            n3 = n_ring[:, :].rearrange("p (j c) -> p j c", j=CW)
            ps3 = psflat[:, 2048:2048 + C].rearrange("p (j c) -> p j c", j=CW)

            def ln(c, i, sem_a, a_val):
                for j in range(CW):
                    c.inc(dve.bn_stats(lnst[:, j, :], y[:, j, :]))
                c.wait()
                dve.sem_inc(vtaken, 1)
                for j in range(CW):
                    c.inc(dve.bn_aggr(lnmv[:, j, :], lnst[:, j, :]))
                dve.wait_ge(sem_a, a_val)
                c.link(dve.reciprocal(lnrs[:, :], lnsd[:, :]))
                for j in range(CW):
                    c.inc(dve.tensor_scalar(cur[:, bass.ds(i * CW + j, 1), :], y[:, j:j + 1, :], lnmv[:, j, 0:1],
                                            lnrs[:, j:j + 1], ALU.subtract, ALU.mult))
                c.wait()

            dve.wait_ge(tbl0, 32)
            segsum("p1", 0)
            place_end(1)
            dv = Count(dve, n_pass["A"])
            dv.link(dve.tensor_copy(deg_dst[:, :], acc[:, :, D]))
            with dve.Fori(0, NCH) as i:
                c = Count(dve, nv["A"], 2, i)
                ch = bass.ds(i * CW, CW)
                dve.wait_ge(npe["A"], i * 3)
                c.inc(dve.tensor_tensor(s3, x0[:, ch, :], acc[:, ch, 0:D], ALU.add))
                dve.wait_ge(npe["A"], i * 3 + 3)
                dve.wait_ge(na["A"], i * 3)
                c.inc(dve.tensor_tensor(y[:, :, :], ps3, brc(brow[0]), ALU.add))
            dve.wait_ge(na["A"], 3 * NCH)
            segsum("p2", 0)
            with dve.Fori(0, NCH) as i:
                c = Count(dve, nv["B"], KB, i)
                ch = bass.ds(i * CW, CW)
                dve.wait_ge(npe["B"], i * 3)
                c.inc(dve.tensor_tensor(s3, cur[:, ch, :], acc[:, ch, 0:D], ALU.add))
                dve.wait_ge(npe["B"], i * 3 + 3)
                c.link(dve.tensor_tensor(y[:, :, :], ps3, brc(brow[1]), ALU.add))
                c.link(dve.tensor_tensor(y[:, :, :], y[:, :, :], x0[:, ch, :], ALU.add))
                ln(c, i, na["B"], i * 3 + 3)
                assert c.n == KB
            dve.wait_ge(nv["B"], KB * NCH)

            def reciprocal_degree(cc, deg):
                cc.link(dve.tensor_scalar(rdeg[:, :], deg[:, :], 1.0, None, ALU.max))
                cc.link(dve.reciprocal(rdeg[:, :], rdeg[:, :]))

            def sage_in(c, i):
                ch = bass.ds(i * CW, CW)
                dve.wait_ge(npe[c.p], i * 3)
                c.inc(dve.tensor_copy(s3, cur[:, ch, :]))
                c.inc(dve.tensor_tensor(n3, acc[:, ch, 0:D],
                                        rdeg[:, ch].rearrange("p (j o) -> p j o", o=1).to_broadcast([P, CW, D]), ALU.mult))
                dve.wait_ge(npe[c.p], i * 3 + 3)

            segsum("p3", 1)
            dv = Count(dve, n_pass["C"])
            dv.link(dve.tensor_copy(deg_src[:, :], acc[:, :, D]))
            reciprocal_degree(dv, deg_src)
            with dve.Fori(0, NCH) as i:
                c = Count(dve, nv["C"], KC, i)
                c.p = "C"
                sage_in(c, i)
                c.link(dve.tensor_tensor(y[:, :, :], ps3, brc(bL1), ALU.add))
                c.link(dve.tensor_tensor(y[:, :, :], y[:, :, :], s3, ALU.add))
                ln(c, i, na["C"], i * 3 + 3)
                assert c.n == KC
            dve.wait_ge(nv["C"], KC * NCH)
            segsum("p4", 0)
            dv = Count(dve, n_pass["D"])
            reciprocal_degree(dv, deg_dst)
            with dve.Fori(0, NCH) as i:
                c = Count(dve, nv["D"], 3, i)
                c.p = "D"
                sage_in(c, i)
                dve.wait_ge(na["D"], i * 3)
                c.inc(dve.tensor_tensor(y[:, :, :], ps3, brc(bL2), ALU.add))
            dve.wait_ge(na["D"], 3 * NCH)
            c = Count(dve, dn_v)
            c.link(dve.tensor_scalar(x0[:, NW - 1, :], x0[:, NW - 1, :], small[:, 20:21], None, ALU.mult))
            c.link(dve.tensor_tensor(acc[:, :, 0:D], x0[:, :, :], x0[:, :, :], ALU.mult))
            c.link(dve.tensor_reduce(small[:, 7:8], acc[:, :, 0:D], AX.XY, ALU.add))
            dve.wait_ge(dn_a, 1)
            c.link(dve.reciprocal(small[:, 10:11], small[:, 4:5]))
            with dve.Fori(0, NCH) as i:
                c = Count(dve, nv2, KD2, i)
                ch = bass.ds(i * CW, CW)
                c.link(dve.scalar_tensor_tensor(out=y[:, :, :], in0=x0[:, ch, :], scalar=small[:, 10:11],
                                                in1=cur[:, ch, :], op0=ALU.mult, op1=ALU.add))
                ln(c, i, na2, i + 1)
                assert c.n == KD2
            dve.wait_ge(nv2, KD2 * NCH)
            c = Count(dve, bn_v)
            c.link(dve.memset(mu0, 0.0))
            with dve.Fori(0, NCH) as i:
                ch = bass.ds(i * CW, CW)
                dve.wait_ge(npe["E"], i * 3)
                dve.tensor_copy(s3, cur[:, ch, :]).then_inc(nv["E"], 1)
                dve.wait_ge(npe["E"], i * 3 + 2)
                dve.wait_ge(nst["E"], i * 16)
                ab = psflat[:, 1024:1024 + 2 * C].rearrange("p (j c) -> p j c", j=CW)
                dve.tensor_copy(s2a[:, :].rearrange("p (j c) -> p j c", j=CW), ab[:, :, 0:D])
                dve.tensor_copy(x0[:, ch, :], ab[:, :, 0:D])
                dve.tensor_copy(y[:, :, :], ab[:, :, D:2 * D]).then_inc(nv["E"], 1)
                dve.wait_ge(npe["E"], i * 3 + 3)
                dve.wait_ge(nv["E"], i * 3 + 2)
                dve.tensor_tensor(mu0, mu0, psflat[:, 3072:3073], ALU.add).then_inc(nv["E"], 1)
            dve.wait_ge(nv["E"], 3 * NCH)
            c.link(dve.tensor_scalar(mfc, mu0, 1.0 / E, None, ALU.mult))
            c.inc(dve.tensor_scalar(diag[:, :], ident[:, :], mfc, None, ALU.mult))
            dve.wait_ge(bn_p, 1)
            c.link(dve.tensor_tensor(x0[:, :, :], x0[:, :, :],
                                     PS[:, 7, 0:P].rearrange("p (o c) -> p o c", o=1).to_broadcast([P, NW, D]),
                                     ALU.subtract))
            with dve.Fori(0, ITERS) as i:
                for h in range(2):
                    ws = windows(0, h, i)
                    one_hots("p5", 0, h, i, q_tr)
                    dve.wait_ge(q_e[h], i)
                    for u in range(U):
                        dve.tensor_copy(abuf[:, h, u:u + 1, :], x0[:, bass.ds(ws[u], 1), :]).then_inc(q_a[h], 1)
            for h in range(2):
                dve.wait_ge(q_sq[h], ITERS)
            c.link(dve.tensor_reduce(small[:, 11:12], sq[:, :], AX.X, ALU.add))
            c.link(dve.tensor_scalar(small[:, 6:7], small[:, 11:12], 1.0 / E, None, ALU.mult))
            assert c.n == 6
            dve.wait_ge(bn_a, 1)
            c.link(dve.reciprocal(small[:, 12:13], small[:, 5:6]))
            c.link(dve.tensor_tensor(scale0, small[:, 12:13], bn[:, 0:1], ALU.mult))
            dve.wait_ge(bn_p, 2)
            c.link(dve.tensor_copy(small[:, 13:14], PS[:, 7, 0:1]))
            with dve.Fori(0, ITERS) as i:
                for h in range(2):
                    dve.wait_ge(b_mm[h], i + 1)
                    for s in range(2):
                        dve.bn_stats(stats[:, bass.ds(i * 4 + (2 * h + s), 1), :], PS[:, 2 * h + s, :]).then_inc(b_bn[h], 1)
            for h in range(2):
                dve.wait_ge(b_bn[h], 2 * ITERS)
            c.link(dve.bn_aggr(small[:, 16:18], stats[:, :, :].rearrange("p a b -> p (a b)")))
            EMPTY = SLOTS - E
            c.link(dve.tensor_tensor(small[:, 18:19], small[:, 16:17], small[:, 13:14], ALU.subtract))
            c.link(dve.scalar_tensor_tensor(out=small[:, 19:20], in0=small[:, 18:19], scalar=EMPTY / E,
                                            in1=small[:, 16:17], op0=ALU.mult, op1=ALU.add))
            c.link(dve.tensor_tensor(small[:, 18:19], small[:, 13:14], small[:, 19:20], ALU.subtract))
            c.link(dve.tensor_tensor(small[:, 18:19], small[:, 18:19], small[:, 18:19], ALU.mult))
            c.link(dve.tensor_scalar(small[:, 21:22], small[:, 17:18], SLOTS / E, None, ALU.mult))
            c.link(dve.scalar_tensor_tensor(out=small[:, 14:15], in0=small[:, 18:19], scalar=-EMPTY / SLOTS,
                                            in1=small[:, 21:22], op0=ALU.mult, op1=ALU.add))
            assert c.n == BNV, c.n
            dve.wait_ge(bn_a, 3)
            t = Count(dve, dn_v)
            t.n = 4
            t.link(dve.reciprocal(small[:, 22:23], small[:, 15:16]))
            t.link(dve.tensor_tensor(small[:, 22:23], small[:, 22:23], bn[:, 2:3], ALU.mult))
            t.link(dve.tensor_tensor(small[:, 23:24], small[:, 22:23], small[:, 19:20], ALU.mult))
            c.link(dve.tensor_scalar(fcs[:, :], fc[:, :], small[:, 22:23], None, ALU.mult))
            c.link(dve.tensor_tensor(sh1, bn[:, 3:4], small[:, 23:24], ALU.subtract))
            dve.wait_ge(bn_p, 4)
            c.link(dve.tensor_copy(fcsT[:, :], PS[:, 6, 0:P]))
            c.link(dve.tensor_copy(shrow[:, :], PS[0:1, 6, P:2 * P]))
            z.link(dve.memset(acc[:, :, :], 0.0))
            ahead("pc", 0, lambda h, u: PS[:, 4 + 2 * h + u // 4, (u % 4) * P:(u % 4 + 1) * P].rearrange("p (o c) -> p o c", o=1), D)
            dve.wait_ge(add_ok["pc"], T)
            with dve.Fori(0, NCH) as i:
                c = Count(dve, nv["F"], KF, i)
                ch = bass.ds(i * CW, CW)
                c.link(dve.tensor_tensor(n3, acc[:, ch, 0:D],
                                         rdeg[:, ch].rearrange("p (j o) -> p j o", o=1).to_broadcast([P, CW, D]), ALU.mult))
                c.link(dve.tensor_tensor(n3, n3, cur[:, ch, :], ALU.add))
                c.link(dve.scalar_tensor_tensor(out=y[:, :, :], in0=n3, scalar=0.0, in1=cur[:, ch, :],
                                                op0=ALU.max, op1=ALU.add))
                ln(c, i, na["F"], i + 1)
                assert c.n == KF


_INS = ["x", "src", "dst", "edge_weight1", "L0_gnn_W1", "L0_gnn_b1", "L0_gnn_W2", "L0_gnn_b2", "L0_gnn_W3", "L0_gnn_b3",
        "L0_gnn_W4", "L0_gnn_b4", "L1_gnn_W", "L1_gnn_b", "L2_gnn_W", "L2_gnn_b", "L3_gnn_theta_w", "L3_gnn_phi_w",
        "L3_gnn_fc1_w", "L3_gnn_bn0_g", "L3_gnn_bn0_b", "L3_gnn_bn1_g", "L3_gnn_bn1_b"]


def kernel(**inputs):
    import numpy as np
    import concourse.bacc as bacc
    from concourse import mybir as mb
    from concourse.bass_utils import run_bass_kernel_spmd

    nc = bacc.Bacc("TRN2", target_bir_lowering=False, num_devices=1)
    arrays, args = {}, []
    for name in _INS:
        a = np.ascontiguousarray(inputs[name])
        arrays[f"in_{name}"] = a
        args.append(nc.dram_tensor(f"in_{name}", a.shape, mb.dt.from_np(a.dtype), kind="ExternalInput").ap())
    shape = inputs["x"].shape
    args.append(nc.dram_tensor("result", shape, mb.dt.float32, kind="ExternalOutput").ap())
    gnn_kernel(nc, *args)
    r = run_bass_kernel_spmd(nc, [arrays], core_ids=[0])
    return np.asarray(r.results[0]["result"]).reshape(shape)
```

```python
from contextlib import ExitStack

import concourse.bass as bass
from concourse import mybir

F32 = mybir.dt.float32
BF16 = mybir.dt.bfloat16
I32 = mybir.dt.int32
ALU = mybir.AluOpType
ACT = mybir.ActivationFunctionType
AX = mybir.AxisListType

P = 128


class Count:

    def __init__(self, eng, sem, K=0, i=0):
        self.eng, self.sem, self.K, self.i, self.n = eng, sem, K, i, 0

    def inc(self, ins):
        ins.then_inc(self.sem, 1)
        self.n += 1
        return self.n

    def wait(self, n=None):
        self.eng.wait_ge(self.sem, self.i * self.K + (self.n if n is None else n))

    def link(self, ins):
        self.inc(ins)
        self.wait()

    def turn(self, i):
        assert self.n in (0, self.K)
        self.i, self.n = i, 0


def gnn_kernel(nc, x, src, dst, edge_weight1, W1, b1, W2, b2, W3, b3, W4, b4, L1W, L1b, L2W, L2b,
               theta_w, phi_w, fc1_w, bn0_g, bn0_b, bn1_g, bn1_b, out):
    N, D = x.shape
    E = src.shape[0]
    NW = -(-N // P)
    NP = NW * P
    ZROW = NP
    EC = 2 * 8 * (-(-E // (P * 16)))
    EP = E // EC
    ER = E - EP * EC
    assert D == P and EP == P - 1 and 0 < ER < EC
    U = 8
    T = (E + NW * (P - 1)) // P
    T = -(-T // (2 * U)) * 2 * U
    TT = T + 2 * U
    assert EC * P - E <= (TT - T) * P
    TG = TT // P
    EB = -(-E // P)
    EL = E - (EB - 1) * P
    assert TG * P == TT and NW + 1 < T // (2 * U)
    ITERS = T // (2 * U)
    J = ITERS // 2
    assert ITERS % 2 == 1
    SLOTS = T * P
    EPS = 1e-5
    CW = 7
    NCH = NW // CW
    assert NCH * CW == NW
    TAIL = N - (NW - 1) * P
    C = CW * P
    LN = 3 * CW + 1
    KB, LNB = 3 + LN, 3 + 2 * CW
    KC, LNC = 1 + LN, 1 + 2 * CW
    KD2, LND2 = 2 + LN, 1 + 2 * CW
    KF, LNF = 4 + LN, 4 + 2 * CW
    CN = (5, 4)
    HC = (NW + 1) // 2
    SG = (NW + 1 - HC, 2 * (NW + 1) - HC)
    IV = 21
    SHL = 43
    SCI = EC // (2 * U)
    FLV, SHQ = 4, 14
    BNV = 16
    D1 = D + 1

    table = nc.dram_tensor("node_table", (NP + P, D), F32).ap()
    rec_dst = nc.dram_tensor("rec_dst", (P * TT, 2), F32).ap()
    rec_src = nc.dram_tensor("rec_src", (P * TT, 4), F32).ap()
    pairs = nc.dram_tensor("pairs", (EB, 4, P), I32).ap()
    wdram = [nc.dram_tensor(f"window_of_tile_{k}", (P, TG), I32).ap() for k in "ds"]
    e_store = nc.dram_tensor("e_store", (ITERS * 2, P, U * P), F32).ap()
    table_w = table[0:NP, :].rearrange("(w p) f -> p w f", p=P)

    ctx = ExitStack()
    with ctx:
        def sb(name, shape, dt=F32):
            return ctx.enter_context(nc.sbuf_tensor(name, shape, dt))

        def sem(name):
            return ctx.enter_context(nc.semaphore(name))

        x0 = sb("x0", [P, NW, D])
        cur = sb("cur", [P, NW, D])
        acc = sb("acc", [P, NW, D1])
        deg_dst = sb("deg_dst", [P, NW])
        deg_src = sb("deg_src", [P, NW])
        rdeg = sb("rdeg", [P, NW])
        accf = cur[:, :, :].rearrange("p a b -> p (a b)")
        sumf = acc[:, :, :].rearrange("p a b -> p (a b)")
        blk = sumf[:, 0:4 * TT].bitcast(I32).rearrange("p (j k c) -> p j k c", j=TG, k=2)
        blkf = sumf[:, 0:4 * TT].rearrange("p (j k c) -> p j k c", j=TG, k=2)
        lanes = sumf[:, 4 * TT:6 * TT].rearrange("p (k j c) -> p k j c", k=2, j=TG)
        real = sumf[:, 6 * TT:7 * TT].bitcast(I32).rearrange("p (j c) -> p j c", j=TG)
        key_i = accf[:, 0:2 * EC].bitcast(I32).rearrange("p (k c) -> p k c", k=2)
        raw = sb("raw", [P, EC, 3])
        raw_s = sb("raw_s", [P, EC, 3])
        wgt = accf[:, 2 * EC:3 * EC]
        pos = sb("pos", [P, 2, EC], I32)
        rec = [sb("rec_d_sb", [P, TT, 2]), sb("rec_s_sb", [P, TT, 4])]
        gidx = [sb("gidx_d", [P, TT], I32), sb("gidx_s", [P, TT], I32)]
        wtile = [sb("wtile_d", [1, TT], I32), sb("wtile_s", [1, TT], I32)]
        scratch = sb("scratch", [P, 4, C])
        mask = scratch[:, 0:2, 0:EC].bitcast(I32)
        scan = scratch[:, 2:4, 0:EC]
        posf = accf[:, 4 * EC:5 * EC]
        zeros_e = accf[:, 5 * EC:6 * EC]
        cnt = sb("cnt", [P, NW + 1])
        tot = sb("tot", [P, NW + 1])
        tiles_i = sb("tiles_i", [P, NW + 1], I32)
        tiles_f = sb("tiles_f", [P, NW + 1])
        tend = sb("tend", [P, NW + 1])
        off = sb("off", [P, NW + 1])
        wnum = sb("wnum", [P, NW + 1])
        tnum = sb("tnum", [P, TG])
        ge = scratch[:, 0, 0:TG * (NW - 1)].rearrange("p (j w) -> p j w", j=TG)
        gex = scratch[:, 1, 0:TG * (NW - 1)].rearrange("p (j w) -> p j w", j=TG)
        nxt = scratch[:, 3, 0:EC].bitcast(I32)
        less = sb("less", [P, NW - 1])
        tcols = sb("tcols", [P, 4, TG])
        wcol = sb("wcol", [P, TG], I32)
        first_i = sb("first_i", [P, TG], I32)
        blk_i = sb("blk_i", [P, TG], I32)
        shift_i = sb("shift_i", [P, TG], I32)
        bit_i = sb("bit_i", [P, 7, TG], I32)
        flag = sb("flag", [P, 1], I32)
        posr = sb("posr", [P, 2, U], I32)
        recr = [sb("recr_d", [P, 2, U, 2]), sb("recr_s", [P, 2, U, 4])]
        idxr = sb("idxr", [P, 2, U], I32)
        msg = sb("msg", [P, 2, U, D1])
        oh = sb("oh", [P, 2, U, P])
        ohT = sb("ohT", [P, 2, U, P])
        abuf = sb("abuf", [P, 2, U, D])
        abuff = abuf[:, :, :, :].rearrange("p h u c -> p (h u c)")
        winf = [accf[:, 3 * EC:4 * EC], abuff[:, 0:EC]]
        signs = abuff[:, EC:2 * EC]
        whalf = sb("whalf", [P, NW + 1])
        sgn = sb("sgn", [P, 2, NW + 2])
        el = raw[:, :, :].rearrange("p a b -> p (a b)")[:, 0:2 * U * P].rearrange("p (h c) -> p h c", h=2)
        rT = raw_s[:, :, :].rearrange("p a b -> p (a b)")[:, 0:2 * U * P].rearrange("p (h c) -> p h c", h=2)
        s_ring, n_ring, sT, nT = (scratch[:, n, :] for n in range(4))
        s2a = n_ring
        y = sb("y", [P, CW, D])
        lnst = sb("lnst", [P, CW, 6])
        lnmv = sb("lnmv", [P, CW, 2])
        lnsd = sb("lnsd", [P, CW])
        lnrs = sb("lnrs", [P, CW])
        ident = sb("ident", [P, P])
        upper = sb("upper", [P, P])
        ones = sb("ones", [P, P])
        col = sb("col", [P, P])
        epsc = sb("epsc", [P, 1])
        wA = [sb(f"w_{n}", [P, D]) for n in range(4)]
        bcol = [sb(f"bcol_{n}", [P, 1]) for n in (0, 2)]
        brow = [sb(f"brow_{n}", [P, D]) for n in (1, 3)]
        wL1 = sb("wL1", [P, 2, D])
        bL1 = sb("bL1", [P, D])
        wL2 = sb("wL2", [P, 3 * D])
        wL2T = sb("wL2T", [P, 3, D])
        bL2 = sb("bL2", [P, D])
        th = sb("th", [P, D])
        ph = sb("ph", [P, D])
        thphT = sb("thphT", [P, 2, D])
        fc = sb("fc", [P, D])
        fcT = sb("fcT", [P, D])
        fcs = sb("fcs", [P, D])
        fcsT = sb("fcsT", [P, D])
        bn = sb("bn", [P, 4])
        stats = msg[:, :, :, :].rearrange("p h u c -> p (h u c)")[:, 0:ITERS * 24].rearrange("p (a b) -> p a b", b=6)
        sq = sb("sq", [P, ITERS * 2])
        dsum = sb("dsum", [P, NCH])
        small = sb("small", [P, 28])
        diag = sb("diag", [P, P])
        shrow = sb("shrow", [3, 4 * D], BF16)
        shcol = sb("shcol", [P, 2], BF16)
        ones3 = sb("ones3", [3, P], BF16)
        acc2 = x0
        ev = abuf[:, 0, :, :]
        eb = [el, ohT[:, :, :, :].rearrange("p h u c -> p h (u c)")]
        b_ring = oh[:, 0, :, :].rearrange("p u c -> p (u c)")[:, 0:C]

        PS = ctx.enter_context(nc.psum_tensor("PS", [P, 8, 512], F32))
        psflat = PS[:, :, :].rearrange("p b c -> p (b c)")

        block = ctx.enter_context(nc.Block())

        ld_edges, ld_x, ld_w = sem("ld_edges"), sem("ld_x"), sem("ld_w")
        iota_ready, presets_done = sem("init"), sem("init_v")
        filled, taken = sem("filled"), sem("taken")
        vtaken = sem("vtaken")
        table_filled = sem("tbl0")
        win_steps = [sem("rk_d"), sem("rk_s")]
        dst_counted, signs_done = sem("rk_counted"), sem("rk_signs")
        counts_summed = [sem("rkp_d"), sem("rkp_s")]
        place_steps = [sem("rkq_d"), sem("rkq_s")]
        flag_v, flag_p = sem("flag_dve"), sem("flag_pe")
        ld_next, pairs_ok = sem("ld_next"), sem("pairs_ok")
        tilewin_ready, tilewin_stored, tilewin_loaded = [[sem(f"{n}_{k}") for k in "ds"] for n in ("wcol", "wcol_stored", "wtile_ld")]
        short_steps, blocks_got, lanes_turned = sem("short_dve"), sem("short_got"), sem("short_pe")
        pos_ready = [sem("pos_d"), sem("pos_s")]
        rec_ringed = [sem("sc_ring_d"), sem("sc_ring_s")]
        rec_sent = [[sem(f"sc_done_{k}{h}") for h in range(2)] for k in "ds"]
        rec_loaded = [sem("rec_ld_d"), sem("rec_ld_s")]
        unpacked = [sem("unpacked_d"), sem("unpacked_s")]

        names = ["p1", "p2", "p3", "p4"]
        idx_ready = {k: sem(f"{k}_idx") for k in names + ["p5"]}
        rows_got = {k: [sem(f"{k}_got{h}") for h in range(2)] for k in names + ["p5"]}
        onehots_ready = {k: [sem(f"{k}_oh{h}") for h in range(2)] for k in names + ["p5", "pc"]}
        sums_ready = {k: [sem(f"{k}_mm{h}") for h in range(2)] for k in names + ["pc"]}
        sums_added = {k: sem(f"{k}_add") for k in names + ["pc"]}
        acc_zero = sem("acc_zero")
        scaled = [sem("p3_scaled0"), sem("p3_scaled1")]

        n_pass = {k: sem(f"{k}_end") for k in "ACD"}
        node_v = {k: sem(f"n{k}_dve") for k in "ABCF"}
        node_a = {k: sem(f"n{k}_act") for k in "ABCDF"}
        node_p = {k: sem(f"n{k}_pe") for k in "AB"}
        table_stored = {k: sem(f"n{k}_store") for k in "ABCE"}
        norm_v, norm_p, norm_a, norm_squared = sem("norm_dve"), sem("norm_pe"), sem("norm_act"), sem("norm_squares")
        x3_steps, x3_sqrt = sem("nD2_dve"), sem("nD2_act")
        sage_in, sage_turned, sage_copied, sage_biased, sage_product = [sem(f"nCD_{n}") for n in ("in", "turned", "copied", "y", "product")]
        chunks_before = {"C": 0, "D": NCH}
        x3_turned, x3_copied, ab_product, ab_split, mean_added = [sem(f"nE_{n}") for n in ("turned", "copied", "product", "split", "mean")]
        acc2_zero, acc2_added, sums_evicted = sem("acc2_zero"), sem("pc_add2"), sem("pc_evicted")
        weights_turned, weights_copied = sem("wt_pe"), sem("wt_dve")
        oh_turned = [sem("p5_tr0"), sem("p5_tr1")]
        a_copied = [sem("p5_a0"), sem("p5_a1")]
        ohT_ready = [sem("p5_t0"), sem("p5_t1")]
        e_summed = [sem("p5_e0"), sem("p5_e1")]
        e_squared = [sem("p5_sq0"), sem("p5_sq1")]
        e_copied = [sem("p5_cp0"), sem("p5_cp1")]
        e_stored = [sem("p5_st0"), sem("p5_st1")]
        bn_v, bn_a, bn_p = sem("bn_dve"), sem("bn_act"), sem("bn_pe")
        e_loaded = [[sem(f"b_ld{par}{h}") for h in range(2)] for par in range(2)]
        r_ready = [sem("b_r0"), sem("b_r1")]
        y_product = [sem("b_mm0"), sem("b_mm1")]
        y_stats = [sem("b_bn0"), sem("b_bn1")]
        y_relu = [sem("c_y0"), sem("c_y1")]
        res_st = sem("res_st")
        H0 = 1
        started = [sage_biased, mean_added, norm_squared, acc2_added, sums_evicted, table_stored["E"], node_a["A"], node_a["B"], node_a["D"], node_p["A"], node_p["B"]]
        started += place_steps + list(sums_added.values())
        for pair in list(sums_ready.values()) + [oh_turned, e_summed, e_stored, ohT_ready, e_squared, y_stats, y_relu]:
            started += pair

        scale0, mu0, mfc, sh1 = small[:, 0:1], small[:, 1:2], small[:, 2:3], small[:, 3:4]

        def cols8(i, h):
            return bass.ds(i * (2 * U) + h * U, U)

        @block.sync
        def _(sp):
            sp.wait_ge(presets_done, IV)
            for k, a in ((0, dst), (1, src)):
                sp.dma_start(key_i[0:EP, k, :], a[0:EP * EC].rearrange("(p c) -> p c", p=EP)).then_inc(ld_edges, 16)
                sp.dma_start(key_i[EP:P, k, 0:ER], a[EP * EC:E].rearrange("(p c) -> p c", p=1)).then_inc(ld_edges, 16)
            sp.dma_start(nxt[0:EP, :], dst[1:EP * EC + 1].rearrange("(p c) -> p c", p=EP)).then_inc(ld_next, 16)
            sp.dma_start(nxt[EP:P, 0:ER - 1], dst[EP * EC + 1:E].rearrange("(p c) -> p c", p=1)).then_inc(ld_next, 16)
            w = edge_weight1.rearrange("e o -> (e o)")
            sp.dma_start(wgt[0:EP, :], w[0:EP * EC].rearrange("(p c) -> p c", p=EP)).then_inc(ld_edges, 16)
            sp.dma_start(wgt[EP:P, 0:ER], w[EP * EC:E].rearrange("(p c) -> p c", p=1)).then_inc(ld_edges, 16)
            sp.dma_start(pairs[EB - 2:EB, :, :].rearrange("q k c -> q (k c)"), gidx[0][0:2, 0:4 * P]).then_inc(pairs_ok, 16)
            sp.wait_ge(pairs_ok, 16)
            for k, a in ((0, src), (2, dst)):
                sp.dma_start(pairs[0:EB - 1, k, :], a[0:E - EL].rearrange("(q c) -> q c", c=P)).then_inc(pairs_ok, 16)
                sp.dma_start(pairs[0:EB - 2, k + 1, :], a[P:E - EL].rearrange("(q c) -> q c", c=P)).then_inc(pairs_ok, 16)
                sp.dma_start(pairs[EB - 1:EB, k, 0:EL], a[E - EL:E].rearrange("(q c) -> q c", q=1)).then_inc(pairs_ok, 16)
                sp.dma_start(pairs[EB - 2:EB - 1, k + 1, 0:EL], a[E - EL:E].rearrange("(q c) -> q c", q=1)).then_inc(pairs_ok, 16)
            sp.dma_start(x0[:, 0:NW - 1, :], x[0:(NW - 1) * P, :].rearrange("(w p) f -> p w f", p=P)).then_inc(ld_x, 16)
            sp.dma_start(x0[0:TAIL, NW - 1, :], x[(NW - 1) * P:N, :]).then_inc(ld_x, 16)
            for t, a in ((wA[0], W1), (wA[1], W2), (wA[2], W3), (wA[3], W4), (th, theta_w), (ph, phi_w), (fc, fc1_w)):
                sp.dma_start(t[:, :], a).then_inc(ld_w, 16)
            sp.dma_start(wL1[:, :, :], L1W.rearrange("(k p) n -> p k n", p=P)).then_inc(ld_w, 16)
            sp.dma_start(wL2[:, :], L2W).then_inc(ld_w, 16)
            for t, a in ((bcol[0][:, :], b1), (bcol[1][:, :], b3), (bn[:, 0:1], bn0_g), (bn[:, 1:2], bn0_b),
                         (bn[:, 2:3], bn1_g), (bn[:, 3:4], bn1_b)):
                sp.dma_start(t, a.rearrange("(p o) -> p o", o=1)).then_inc(ld_w, 16)
            for t, a in ((brow[0], b2), (brow[1], b4), (bL1, L1b), (bL2, L2b)):
                sp.dma_start(t[:, :], a.rearrange("(o f) -> o f", o=1).to_broadcast([P, D])).then_inc(ld_w, 16)
            sp.wait_ge(iota_ready, 6)
            sp.dma_start(rec_dst.rearrange("(p t) r -> p t r", p=P), rec[0][:, :, :]).then_inc(filled, 16)
            sp.dma_start(rec_src.rearrange("(p t) r -> p t r", p=P), rec[1][:, :, :]).then_inc(filled, 16)
            sp.dma_start(table[NP:NP + P, :], zeros_e[:, 0:D]).then_inc(table_filled, 16)
            sp.wait_ge(ld_x, 32)
            sp.dma_start(table_w, x0[:, :, :]).then_inc(table_filled, 16)

            def window_rows(k):
                sp.wait_ge(tilewin_ready[k], 1)
                sp.dma_start(wdram[k], wcol[:, :]).then_inc(tilewin_stored[k], 16)
                sp.wait_ge(tilewin_stored[k], 16)
                sp.dma_start(wtile[k][:, :], wdram[k].rearrange("(o p) j -> o (p j)", o=1)).then_inc(tilewin_loaded[k], 16)

            def load_records(k):
                for h in range(2):
                    sp.wait_ge(rec_sent[k][h], EC // 2 * 16)
                sp.dma_start(rec[k][:, :, :], (rec_dst, rec_src)[k].rearrange("(p t) r -> p t r", p=P)).then_inc(rec_loaded[k], 16)

            window_rows(0)
            sp.wait_ge(flag_v, FLV)
            unsorted = sp.value_load(flag[0:1, 0:1], min_val=0, max_val=1)
            with sp.If(unsorted == 1):
                load_records(0)
            window_rows(1)

            def store_chunks(ready, K, before, sem_, src_of):
                with sp.Fori(0, NCH) as i:
                    sp.wait_ge(ready, i * K + (K + before))
                    sp.dma_start(table_w[:, bass.ds(i * CW, CW), :], src_of(i)).then_inc(sem_, 16)

            store_chunks(node_a["A"], 3, H0, table_stored["A"], lambda i: cur[:, bass.ds(i * CW, CW), :])
            store_chunks(node_v["B"], KB, 0, table_stored["B"], lambda i: cur[:, bass.ds(i * CW, CW), :])
            load_records(1)
            store_chunks(node_v["C"], KC, 0, table_stored["C"], lambda i: cur[:, bass.ds(i * CW, CW), :])
            with sp.Fori(0, NCH) as i:
                sp.wait_ge(ab_split, i * 3 + 3)
                sp.dma_start(table_w[:, bass.ds(i * CW, CW), :], b_ring.rearrange("p (j c) -> p j c", j=CW)).then_inc(table_stored["E"], 16)
            with sp.Fori(0, ITERS) as i:
                for h in range(2):
                    sp.wait_ge(e_copied[h], i + 1)
                    sp.dma_start(e_store[i * 2 + h, :, :], el[:, h, :]).then_inc(e_stored[h], 16)
            for h in range(2):
                sp.wait_ge(e_stored[h], ITERS * 16 + H0)
                sp.wait_ge(e_summed[h], ITERS + H0)

            def load_e(j, par, start):
                for h in range(2):
                    if type(j) is not int or j > 0:
                        sp.wait_ge(r_ready[h], j * 2 + (par - 1))
                    sp.dma_start(eb[par][:, h, :], e_store[j * 4 + (2 * (par - start) + h), :, :]).then_inc(e_loaded[par][h], 16)

            load_e(0, 0, 0)
            load_e(0, 1, 0)
            with sp.Fori(1, J) as j:
                load_e(j, 0, 0)
                load_e(j, 1, 0)
            load_e(J, 0, 0)
            load_e(J, 1, ITERS)
            with sp.Fori(J + 1, ITERS) as j:
                load_e(j, 0, ITERS)
                load_e(j, 1, ITERS)
            sp.wait_ge(node_v["F"], NCH * KF)
            sp.dma_start(out[0:(NW - 1) * P, :].rearrange("(w p) f -> p w f", p=P), cur[:, 0:NW - 1, :]).then_inc(res_st, 16)
            sp.dma_start(out[(NW - 1) * P:N, :], cur[0:TAIL, NW - 1, :]).then_inc(res_st, 16)
            sp.wait_ge(res_st, 32)

        @block.gpsimd
        def _(pool):
            pool.iota(wnum[:, :], pattern=[[1, NW + 1]], base=0, channel_multiplier=0,
                      allow_small_or_imprecise_dtypes=True).then_inc(iota_ready, 1)
            pool.iota(tnum[:, :], pattern=[[1, TG]], base=0, channel_multiplier=TG,
                      allow_small_or_imprecise_dtypes=True).then_inc(iota_ready, 1)
            pool.iota(col[:, :], pattern=[[1, P]], base=0, channel_multiplier=0,
                      allow_small_or_imprecise_dtypes=True).then_inc(iota_ready, 1)
            pool.wait_ge(presets_done, 5)
            pool.affine_select(out=ident[:, :], in_=ident[:, :], compare_op=ALU.not_equal, fill=1.0,
                               base=0, pattern=[[-1, P]], channel_multiplier=1).then_inc(iota_ready, 1)
            pool.affine_select(out=upper[:, :], in_=upper[:, :], compare_op=ALU.is_gt, fill=0.0,
                               base=0, pattern=[[1, P]], channel_multiplier=-1).then_inc(iota_ready, 1)
            pool.memset(epsc[:, :], EPS).then_inc(iota_ready, 1)

            def scatter(k, r, a, b):
                def turn(i):
                    for h in range(2):
                        if type(i) is not int:
                            pool.wait_ge(rec_sent[k][h], i * (16 * U))
                        pool.tensor_copy(posr[:, h, :], pos[:, k, cols8(i, h)]).then_inc(rec_ringed[k], 1)
                        pool.tensor_copy(recr[k][:, h, :, 0:2 + k], (raw, raw_s)[k][:, cols8(i, h), 0:2 + k]).then_inc(rec_ringed[k], 1)
                        pool.wait_ge(rec_ringed[k], i * 4 + (2 * h + 2))
                        pool.sem_inc(taken, 1)
                        for u in range(U):
                            pool.indirect_dma_start(
                                r, bass.IndirectOffsetOnAxis(ap=posr[:, h, u:u + 1], axis=0),
                                recr[k][:, h, u, :], None).then_inc(rec_sent[k][h], 16)

                if a == 0:
                    turn(0)
                with pool.Fori(max(a, 1), b) as i:
                    turn(i)

            def gather(name, free, n, iters):
                with pool.Fori(0, iters) as i:
                    for h in range(2):
                        pool.wait_ge(free[h], i + H0)
                        pool.wait_ge(idx_ready[name], i * 2 + (h + 1))
                        pool.sem_inc(taken, 1)
                        for u in range(n):
                            pool.indirect_dma_start(
                                msg[:, h, u, 0:D], None, table,
                                bass.IndirectOffsetOnAxis(ap=idxr[:, h, u:u + 1], axis=0)).then_inc(rows_got[name][h], 16)

            pool.wait_ge(filled, 32)
            pool.wait_ge(pairs_ok, 16 * 9)
            pool.wait_ge(flag_v, FLV)
            unsorted = pool.value_load(flag[0:1, 0:1], min_val=0, max_val=1)
            with pool.If(unsorted == 1):
                pool.wait_ge(pos_ready[0], 1)
                scatter(0, rec_dst, 0, SCI)
            with pool.Else():
                pool.wait_ge(short_steps, SHQ)
                for j in range(TG):
                    pool.indirect_dma_start(
                        blk[:, j, :, :].rearrange("p k c -> p (k c)"), None, pairs.rearrange("q k c -> q (k c)"),
                        bass.IndirectOffsetOnAxis(ap=blk_i[:, j:j + 1], axis=0)).then_inc(blocks_got, 16)
            pool.wait_ge(table_filled, 32)
            gather("p1", sums_ready["p1"], U, ITERS)
            pool.wait_ge(pos_ready[1], 1)
            scatter(1, rec_src, 0, SCI // 2)
            pool.wait_ge(table_stored["A"], 16 * NCH)
            gather("p2", sums_ready["p2"], U, ITERS)
            scatter(1, rec_src, SCI // 2, SCI)
            pool.wait_ge(table_stored["B"], 16 * NCH)
            gather("p3", sums_ready["p3"], U, ITERS)
            pool.wait_ge(table_stored["C"], 16 * NCH)
            gather("p4", sums_ready["p4"], U, ITERS)
            pool.wait_ge(table_stored["E"], 16 * NCH + H0)
            gather("p5", e_summed, U, ITERS)
            for h in range(2):
                pool.wait_ge(a_copied[h], ITERS * U)
            pool.memset(acc2[:, :, :], 0.0).then_inc(acc2_zero, 1)
            pool.wait_ge(acc2_zero, 1)
            with pool.Fori(0, ITERS) as i:
                ws = nc.values_load_multi_w_load_instructions(
                    wtile[0][0:1, cols8(i, 1)], engines=[mybir.EngineType.Pool], min_val=0, max_val=NW - 1)[1]
                pool.wait_ge(sums_evicted, i + 1 + H0)
                for u in range(U):
                    pool.wait_ge(acc2_added, i * U + u + H0)
                    pool.sem_inc(taken, 1)
                    a = acc2[:, bass.ds(ws[u], 1), :]
                    pool.tensor_tensor(a, a, ev[:, u:u + 1, :], ALU.add).then_inc(acc2_added, 1)

        @block.scalar
        def _(act):
            def signs_of(k, i, before):
                if before is not None:
                    act.wait_ge(signs_done, before)
                w = whalf[:, i:i + 1] if type(i) is int else whalf[:, bass.ds(i, 1)]
                o = sgn[:, k, i:i + 1] if type(i) is int else sgn[:, k, bass.ds(i, 1)]
                act.activation(signs, winf[k][:, :], ACT.Sign, bias=w, accum_out=o).then_inc(signs_done, 1)

            act.wait_ge(presets_done, IV)
            act.wait_ge(win_steps[0], 3)
            signs_of(0, HC, None)
            with act.Fori(HC + 1, NW + 1) as i:
                signs_of(0, i, i - HC)
            act.wait_ge(win_steps[1], 2)
            with act.Fori(0, NW + 1) as i:
                signs_of(1, i, i + SG[0])

            def unpack(k):
                act.wait_ge(rec_loaded[k], 16)
                act.copy(gidx[k][:, :], rec[k][:, :, 0]).then_inc(unpacked[k], 1)
                act.wait_ge(unpacked[k], 1)

            def index_ring(name, k, scale=False):
                for h in range(2):
                    act.copy(idxr[:, h, :], gidx[k][:, h * U:(h + 1) * U]).then_inc(idx_ready[name], 1)
                with act.Fori(0, ITERS) as i:
                    for h in range(2):
                        act.wait_ge(rows_got[name][h], i * (16 * U) + 16 * U)
                        act.copy(idxr[:, h, :], gidx[k][:, bass.ds(i * (2 * U) + (2 + h) * U, U)]).then_inc(idx_ready[name], 1)
                        if scale:
                            for u in range(U):
                                act.activation(msg[:, h, u, 0:D], msg[:, h, u, 0:D], ACT.Copy,
                                               scale=rec[k][:, bass.ds(i * (2 * U) + (h * U + u), 1), 2]).then_inc(scaled[h], 1)

            act.wait_ge(unpacked[0], 1)
            index_ring("p1", 0)

            def conv(p, b, last):
                with act.Fori(0, NCH) as i:
                    act.wait_ge(node_p[p], i * 3 + 1 + H0)
                    act.copy(sT[:, :], psflat[:, 0:C]).then_inc(node_a[p], 1)
                    act.wait_ge(node_p[p], i * 3 + 2 + H0)
                    act.activation(nT[:, :], psflat[:, 1024:1024 + C], ACT.Relu, bias=b[:, :]).then_inc(node_a[p], 1)
                    last(i)

            def relu_h1(i):
                act.wait_ge(node_v["A"], i * 2 + 2)
                act.activation(cur[:, bass.ds(i * CW, CW), :], y[:, :, :], ACT.Relu).then_inc(node_a["A"], 1)

            def ln_sqrt(sem_a, sem_v, i, K, k):
                act.wait_ge(sem_v, i * K + k)
                act.activation(lnsd[:, :], lnmv[:, :, 1], ACT.Sqrt, bias=epsc[:, :]).then_inc(sem_a, 1)

            act.wait_ge(ld_w, 16 * 19)
            conv("A", bcol[0], relu_h1)
            act.wait_ge(node_a["A"], 3 * NCH + H0)
            index_ring("p2", 0)
            conv("B", bcol[1], lambda i: ln_sqrt(node_a["B"], node_v["B"], i, KB, LNB))
            unpack(1)
            index_ring("p3", 1, scale=True)

            def sage(p, last):
                def copy(i):
                    act.wait_ge(sage_turned, i * 2 + (2 * chunks_before[p] + 2))
                    act.copy(sT[:, :], psflat[:, 0:C]).then_inc(sage_copied, 1)
                    act.copy(nT[:, :], psflat[:, 1024:1024 + C]).then_inc(sage_copied, 1)

                copy(0)
                with act.Fori(0, NCH - 1) as i:
                    copy(i + 1)
                    last(i)
                last(NCH - 1)

            sage("C", lambda i: ln_sqrt(node_a["C"], node_v["C"], i, KC, LNC))
            index_ring("p4", 0)

            def tanh_d(i):
                act.wait_ge(sage_biased, i + (NCH + 1) + H0)
                act.activation(x0[:, bass.ds(i * CW, CW), :], y[:, :, :], ACT.Tanh).then_inc(node_a["D"], 1)
                act.wait_ge(node_a["D"], i + 1 + H0)
                if type(i) is int:
                    act.wait_ge(norm_v, 1)
                act.wait_ge(norm_squared, i + H0)
                act.activation(oh[:, 0, 0:CW, :], x0[:, bass.ds(i * CW, CW), :], ACT.Square,
                               accum_out=dsum[:, bass.ds(i, 1)]).then_inc(norm_squared, 1)

            sage("D", tanh_d)
            for h in range(2):
                act.wait_ge(rows_got["p4"][h], ITERS * 16 * U)
                act.copy(idxr[:, h, :], gidx[0][:, h * U:(h + 1) * U]).then_inc(idx_ready["p5"], 1)
            act.wait_ge(norm_p, 1)
            act.activation(small[:, 4:5], psflat[:, 0:1], ACT.Sqrt).then_inc(norm_a, 1)

            def copy_x3(i):
                act.wait_ge(x3_turned, i + 1)
                act.copy(sT[:, :], psflat[:, 0:C]).then_inc(x3_copied, 1)

            def split_chunk(i):
                ab = psflat[:, 1024:1024 + 2 * C].rearrange("p (j c) -> p j c", j=CW)
                act.wait_ge(ab_product, i + 1)
                act.wait_ge(mean_added, i + H0)
                act.wait_ge(table_stored["E"], i * 16 + H0)
                act.copy(s2a[:, :].rearrange("p (j c) -> p j c", j=CW), ab[:, :, 0:D]).then_inc(ab_split, 1)
                act.copy(x0[:, bass.ds(i * CW, CW), :], ab[:, :, 0:D]).then_inc(ab_split, 1)
                act.copy(b_ring.rearrange("p (j c) -> p j c", j=CW), ab[:, :, D:2 * D]).then_inc(ab_split, 1)

            ln_sqrt(x3_sqrt, x3_steps, 0, KD2, LND2)
            copy_x3(0)
            ln_sqrt(x3_sqrt, x3_steps, 1, KD2, LND2)
            with act.Fori(1, NCH - 1) as i:
                split_chunk(i - 1)
                copy_x3(i)
                ln_sqrt(x3_sqrt, x3_steps, i + 1, KD2, LND2)
            split_chunk(NCH - 2)
            copy_x3(NCH - 1)
            split_chunk(NCH - 1)
            act.wait_ge(bn_v, 4)
            with act.Fori(0, ITERS) as i:
                for h in range(2):
                    act.wait_ge(e_summed[h], i + H0)
                    act.wait_ge(oh_turned[h], i + 1 + H0)
                    act.copy(ohT[:, h, :, :], PS[:, 2 * h:2 * h + 2, :].rearrange("p b (u c) -> p (b u) c", c=P)).then_inc(ohT_ready[h], 1)
                    act.wait_ge(e_summed[h], i + 1 + H0)
                    act.wait_ge(e_stored[h], i * 16 + H0)
                    e = psflat[:, (4 + 2 * h) * 512:(6 + 2 * h) * 512]
                    act.copy(el[:, h, :], e).then_inc(e_copied[h], 1)
                    act.activation(rT[:, h, :], e, ACT.Square, accum_out=sq[:, bass.ds(i * 2 + h, 1)]).then_inc(e_squared[h], 1)
                    act.wait_ge(rows_got["p5"][h], i * (16 * U) + 16 * U)
                    act.copy(idxr[:, h, :], gidx[0][:, bass.ds(i * (2 * U) + (2 + h) * U, U)]).then_inc(idx_ready["p5"], 1)
            act.wait_ge(bn_v, 6)
            act.activation(small[:, 5:6], small[:, 6:7], ACT.Sqrt, bias=epsc[:, :]).then_inc(bn_a, 1)
            act.wait_ge(bn_v, 8)
            act.activation(small[:, 8:9], bn[:, 1:2], ACT.Relu).then_inc(bn_a, 1)

            def relu_e(h, j, par):
                act.wait_ge(e_loaded[par][h], j * 16 + 16)
                if type(j) is not int or j + par > 0:
                    act.wait_ge(y_product[h], j * 2 + par)
                act.activation(rT[:, h, :], eb[par][:, h, :], ACT.Relu, bias=bn[:, 1:2], scale=scale0).then_inc(r_ready[h], 1)

            for par in range(2):
                for h in range(2):
                    relu_e(h, 0, par)
            with act.Fori(1, J) as j:
                for par in range(2):
                    for h in range(2):
                        relu_e(h, j, par)
            for h in range(2):
                relu_e(h, J, 0)
            act.wait_ge(bn_v, BNV)
            act.activation(small[:, 15:16], small[:, 14:15], ACT.Sqrt, bias=epsc[:, :]).then_inc(bn_a, 1)

            def c_evict(i):
                act.wait_ge(sums_ready["pc"][1], i + 1 + H0)
                if type(i) is not int or i > 0:
                    act.wait_ge(acc2_added, i * U + H0)
                act.copy(ev, PS[:, 6:8, :].rearrange("p b (u c) -> p (b u) c", c=D)).then_inc(sums_evicted, 1)

            def c_turn(j, par, first=False, last=False):
                i = j * 2 + (par - ITERS)
                for h in range(2):
                    if h == 0:
                        relu_e(1, j, par)
                    elif not last:
                        relu_e(0, j if par == 0 else j + 1, 1 - par)
                    act.wait_ge(y_product[h], j * 2 + (par + 1))
                    if not first:
                        act.wait_ge(sums_ready["pc"][h], i + H0)
                    act.activation(msg[:, h, :, 0:D], PS[:, 2 * h:2 * h + 2, :].rearrange("p b (u c) -> p (b u) c", c=D),
                                   ACT.Relu).then_inc(y_relu[h], 1)
                    if not h and not first:
                        c_evict(i - 1)

            relu_e(0, J, 1)
            c_turn(J, 1, first=True)
            with act.Fori(J + 1, ITERS - 1) as j:
                c_turn(j, 0)
                c_turn(j, 1)
            c_turn(ITERS - 1, 0)
            c_turn(ITERS - 1, 1, last=True)
            c_evict(ITERS - 1)
            with act.Fori(0, NCH) as i:
                ln_sqrt(node_a["F"], node_v["F"], i, KF, LNF)

        @block.tensor
        def _(pe):
            for s in started:
                pe.sem_inc(s, H0)
            pe.wait_ge(iota_ready, 6)
            pe.wait_ge(presets_done, IV)
            pe.wait_ge(flag_v, 2)
            pe.matmul(PS[:, 5, 0:1], ones[:, :], small[:, 5:6], start=True, stop=True).then_inc(flag_p, 1)

            def count_sums(k):
                if k == 0:
                    pe.wait_ge(dst_counted, HC)
                pe.wait_ge(win_steps[k], CN[k])
                pe.matmul(PS[:, 6, 0:NW + 1], upper[:, :], cnt[:, :], start=True, stop=True).then_inc(counts_summed[k], 1)
                pe.matmul(PS[:, 7, 0:NW + 1], ones[:, :], cnt[:, :], start=True, stop=True).then_inc(counts_summed[k], 1)

            count_sums(0)
            pe.wait_ge(flag_v, FLV)
            unsorted = pe.value_load(flag[0:1, 0:1], min_val=0, max_val=1)
            with pe.If(unsorted == 0):
                pe.wait_ge(short_steps, SHL)
                for k in range(2):
                    for j in range(TG):
                        mm = pe.transpose(psflat[:, k * 1024 + j * P:k * 1024 + (j + 1) * P], lanes[:, k, j, :], ident[:, :])
                mm.then_inc(lanes_turned, 1)
            count_sums(1)
            pe.wait_ge(ld_w, 16 * 19)
            for n in range(3):
                pe.transpose(PS[:, 4, n * P:(n + 1) * P], wL2[:, n * D:(n + 1) * D], ident[:, :]).then_inc(weights_turned, 1)
            pe.transpose(PS[:, 4, 3 * P:4 * P], th[:, :], ident[:, :]).then_inc(weights_turned, 1)
            pe.wait_ge(weights_copied, 1)
            pe.transpose(PS[:, 5, 0:P], ph[:, :], ident[:, :]).then_inc(weights_turned, 1)
            pe.transpose(PS[:, 5, P:2 * P], fc[:, :], ident[:, :]).then_inc(weights_turned, 1)

            def slot(h, u):
                return PS[:, 3 * h + u // 3, (u % 3) * D1:(u % 3 + 1) * D1]

            def segsum(name):
                with pe.Fori(0, ITERS) as i:
                    for h in range(2):
                        pe.wait_ge(onehots_ready[name][h], i + 1)
                        pe.wait_ge(rows_got[name][h], (i + 1) * (16 * U))
                        if name == "p3":
                            pe.wait_ge(scaled[h], i * U + U)
                        pe.wait_ge(sums_added[name], i * (2 * U) + H0)
                        for u in range(U):
                            mm = pe.matmul(slot(h, u), oh[:, h, u, :], msg[:, h, u, :], start=True, stop=True)
                        mm.then_inc(sums_ready[name][h], 1)

            def turn_chunk(to, frm):
                for j in range(CW):
                    mm = pe.transpose(psflat[:, to + j * P:to + (j + 1) * P], frm[:, j * P:(j + 1) * P], ident[:, :])
                return mm

            def conv(p, wa, wb, kv, s_step):
                with pe.Fori(0, NCH) as i:
                    pe.wait_ge(node_v[p], i * kv + s_step)
                    turn_chunk(0, s_ring).then_inc(node_p[p], 1)
                    pe.wait_ge(node_a[p], i * 3 + 1 + H0)
                    pe.matmul(psflat[:, 1024:1536], wa[:, :], sT[:, 0:512], start=True, stop=True)
                    pe.matmul(psflat[:, 1536:1024 + C], wa[:, :], sT[:, 512:C], start=True, stop=True).then_inc(node_p[p], 1)
                    pe.wait_ge(node_a[p], i * 3 + 2 + H0)
                    for j in range(CW):
                        mm = pe.matmul(psflat[:, 2048 + j * P:2048 + (j + 1) * P], nT[:, j * P:(j + 1) * P], wb[:, :],
                                       start=True, stop=True)
                    mm.then_inc(node_p[p], 1)

            def sage(p, ws_x, w_n):
                def turn(i):
                    pe.wait_ge(sage_in, i * 2 + (2 * chunks_before[p] + 2))
                    turn_chunk(0, s_ring).then_inc(sage_turned, 1)
                    turn_chunk(1024, n_ring).then_inc(sage_turned, 1)

                def product(i):
                    pe.wait_ge(sage_copied, i * 2 + (2 * chunks_before[p] + 2))
                    pe.wait_ge(sage_biased, i + chunks_before[p] + H0)
                    for j in range(CW):
                        o = psflat[:, 2048 + j * P:2048 + (j + 1) * P]
                        for n, wx in enumerate(ws_x):
                            pe.matmul(o, sT[:, j * P:(j + 1) * P], wx, start=(n == 0), stop=False)
                        mm = pe.matmul(o, nT[:, j * P:(j + 1) * P], w_n, start=False, stop=True)
                    mm.then_inc(sage_product, 1)

                turn(0)
                with pe.Fori(0, NCH - 1) as i:
                    product(i)
                    turn(i + 1)
                product(NCH - 1)

            segsum("p1")
            conv("A", wA[0], wA[1], 2, 1)
            segsum("p2")
            conv("B", wA[2], wA[3], KB, 1)
            segsum("p3")
            sage("C", [wL1[:, 0, :]], wL1[:, 1, :])
            segsum("p4")
            sage("D", [wL2T[:, 0, :], wL2T[:, 2, :]], wL2T[:, 1, :])
            pe.wait_ge(norm_v, 2)
            pe.matmul(psflat[:, 0:1], ones[:, :], small[:, 7:8], start=True, stop=True).then_inc(norm_p, 1)
            pe.wait_ge(norm_v, 3)

            def e_turn(i):
                pe.wait_ge(x3_steps, i * KD2 + KD2)
                turn_chunk(0, s_ring).then_inc(x3_turned, 1)

            def e_product(i):
                pe.wait_ge(x3_copied, i + 1)
                for j in range(CW):
                    mm = pe.matmul(psflat[:, 1024 + j * 256:1280 + j * 256], sT[:, j * P:(j + 1) * P],
                                   thphT[:, :, :].rearrange("p a c -> p (a c)"), start=True, stop=True)
                mm.then_inc(ab_product, 1)

            def e_mean(i, first=False, last=False):
                pe.wait_ge(ab_split, i * 3 + 3)
                for j in range(CW):
                    pe.matmul(psflat[:, 3072:3073], s2a[:, j * P:(j + 1) * P], deg_dst[:, bass.ds(i * CW + j, 1)],
                              start=(first and j == 0), stop=False, skip_group_check=True)
                    mm = pe.matmul(psflat[:, 3072:3073], b_ring[:, j * P:(j + 1) * P], deg_src[:, bass.ds(i * CW + j, 1)],
                                   start=False, stop=(last and j == CW - 1), skip_group_check=True)
                mm.then_inc(mean_added, 1)

            e_turn(0)
            e_product(0)
            e_turn(1)
            e_mean(0, first=True)
            e_product(1)
            with pe.Fori(2, NCH) as i:
                e_turn(i)
                e_mean(i - 1)
                e_product(i)
            e_mean(NCH - 1, last=True)
            pe.wait_ge(bn_v, 3)
            pe.matmul(PS[:, 7, 0:P], ones[:, :], diag[:, :], start=True, stop=True).then_inc(bn_p, 1)
            pe.wait_ge(bn_v, 4)
            with pe.Fori(0, ITERS) as i:
                for h in range(2):
                    pe.wait_ge(onehots_ready["p5"][h], i + 1)
                    pe.wait_ge(ohT_ready[h], i + H0)
                    for u in range(U):
                        mm = pe.transpose(PS[:, 2 * h + u // 4, (u % 4) * P:(u % 4 + 1) * P], oh[:, h, u, :], ident[:, :])
                    mm.then_inc(oh_turned[h], 1)
                    pe.wait_ge(ohT_ready[h], i + 1 + H0)
                    pe.wait_ge(a_copied[h], i * U + U)
                    pe.wait_ge(rows_got["p5"][h], (i + 1) * (16 * U))
                    pe.wait_ge(e_squared[h], i + H0)
                    for u in range(U):
                        o = PS[:, 4 + 2 * h + u // 4, (u % 4) * P:(u % 4 + 1) * P]
                        pe.matmul(o, abuf[:, h, u, :], ohT[:, h, u, :], start=True, stop=False)
                        mm = pe.matmul(o, msg[:, h, u, 0:D], ident[:, :], start=False, stop=True)
                    mm.then_inc(e_summed[h], 1)
            for h in range(2):
                pe.wait_ge(e_squared[h], ITERS + H0)
            pe.wait_ge(bn_a, 2)
            pe.matmul(PS[:, 7, 0:1], fcT[:, :], small[:, 8:9], start=True, stop=True).then_inc(bn_p, 1)
            with pe.Fori(0, ITERS) as i:
                for h in range(2):
                    pe.wait_ge(r_ready[h], i + 1)
                    pe.wait_ge(y_stats[h], i * 2 + H0)
                    for s in range(2):
                        mm = pe.matmul(PS[:, 2 * h + s, :], fcT[:, :], rT[:, h, s * 512:(s + 1) * 512], start=True, stop=True)
                    mm.then_inc(y_product[h], 1)
            pe.wait_ge(bn_v, BNV + 2)
            pe.transpose(PS[:, 6, 0:P], fcs[:, :], ident[:, :]).then_inc(bn_p, 1)
            pe.transpose(PS[0:3, 6, P:2 * P], small[:, 24:27], ident[:, :]).then_inc(bn_p, 1)
            pe.wait_ge(bn_v, BNV + 4)

            def c_product(h, i):
                pe.wait_ge(r_ready[h], i + (ITERS + 1))
                pe.wait_ge(y_relu[h], i + H0)
                for q in range(2):
                    pe.matmul(PS[:, 2 * h + q, :], ones3[:, :], shrow[:, :], start=True, stop=False, skip_group_check=True)
                for u in range(U):
                    mm = pe.matmul(PS[:, 2 * h + u // 4, (u % 4) * P:(u % 4 + 1) * P], rT[:, h, u * P:(u + 1) * P],
                                   fcsT[:, :], start=False, stop=True, skip_group_check=True)
                mm.then_inc(y_product[h], 1)

            def c_turn(i, last=False):
                for h in range(2):
                    if not (last and h):
                        c_product(1 - h, i + h)
                    pe.wait_ge(y_relu[h], i + 1 + H0)
                    pe.wait_ge(onehots_ready["pc"][h], i + 1)
                    pe.wait_ge(sums_evicted if h else sums_added["pc"], (i if h else i * U) + H0)
                    for u in range(U):
                        mm = pe.matmul(PS[:, 4 + 2 * h + u // 4, (u % 4) * P:(u % 4 + 1) * P], oh[:, h, u, :],
                                       msg[:, h, u, 0:D], start=True, stop=True)
                    mm.then_inc(sums_ready["pc"][h], 1)

            c_product(0, 0)
            with pe.Fori(0, ITERS - 1) as i:
                c_turn(i)
            c_turn(ITERS - 1, last=True)

        @block.vector
        def _(dve):
            v = Count(dve, presets_done)
            v.inc(dve.memset(key_i[:, :, :], NP))
            v.inc(dve.memset(wgt[:, :], 0.0))
            v.inc(dve.memset(ident[:, :], 0.0))
            v.inc(dve.memset(ones[:, :], 1.0))
            v.inc(dve.memset(upper[:, :], 1.0))
            v.inc(dve.memset(zeros_e[:, :], 0.0))
            for k in range(2):
                v.inc(dve.memset(rec[k][:, :, 0], float(ZROW)))
                v.inc(dve.memset(rec[k][:, :, 1], -1.0))
                v.inc(dve.memset(rec[1][:, :, 2 + k], 0.0))
            v.inc(dve.memset(msg[:, :, :, D:D1], 1.0))
            v.inc(dve.memset(x0[:, NW - 1, :], 0.0))
            v.inc(dve.memset(recr[1][:, :, :, :], 0.0))
            v.inc(dve.memset(nxt, NP))
            v.inc(dve.memset(ones3[:, :], 1.0))
            v.inc(dve.memset(sgn[:, :, NW + 1], -float(EC)))
            v.inc(dve.memset(gidx[0][:, :], 0))
            v.link(dve.memset(small[:, :], 0.0))
            v.link(dve.memset(small[0:TAIL, 20:21], 1.0))
            dve.wait_ge(ld_edges, 96)
            dve.wait_ge(iota_ready, 6)

            assert v.n == IV, v.n
            cc = [Count(dve, win_steps[k]) for k in range(2)]
            cc[0].link(dve.tensor_scalar(whalf[:, :], wnum[:, :], -1.0, 0.5, ALU.mult, ALU.add))
            for k in range(2):
                cc[k].link(dve.tensor_scalar(mask[:, 1, :], key_i[:, k, :], 7, None, ALU.arith_shift_right))
                cc[k].link(dve.tensor_copy(winf[k][:, :], mask[:, 1, :]))
            f = Count(dve, flag_v)
            dve.wait_ge(ld_next, 32)
            f.link(dve.tensor_tensor(scan[:, 0, :], key_i[:, 0, :], nxt, ALU.is_gt))
            f.link(dve.tensor_reduce(small[:, 5:6], scan[:, 0, :], AX.X, ALU.add))
            dve.wait_ge(flag_p, 1)
            f.link(dve.tensor_scalar(small[:, 6:7], PS[:, 5, 0:1], 1.0, None, ALU.min))
            f.link(dve.tensor_copy(flag[:, :], small[:, 6:7]))
            assert f.n == FLV

            def rows(a, n):
                return a.rearrange("p (j o) -> p j o", o=1).to_broadcast([P, a.shape[1], n])

            def each(a, n):
                return a.rearrange("p (o c) -> p o c", o=1).to_broadcast([P, n, a.shape[1]])

            def count(k):
                c = cc[k]
                if k == 0:
                    dve.tensor_scalar(scan[:, 0, :], winf[0][:, :], wnum[:, 0:1], None, ALU.is_equal, ALU.add,
                                      accum_out=cnt[:, 0:1]).then_inc(dst_counted, 1)
                    with dve.Fori(1, HC) as i:
                        dve.wait_ge(dst_counted, i)
                        dve.tensor_scalar(scan[:, 0, :], winf[0][:, :], wnum[:, bass.ds(i, 1)], None, ALU.is_equal, ALU.add,
                                          accum_out=cnt[:, bass.ds(i, 1)]).then_inc(dst_counted, 1)
                a = (HC, 0)[k]
                dve.wait_ge(signs_done, SG[k])
                c.link(dve.tensor_tensor(cnt[:, a:NW + 1], sgn[:, k, a:NW + 1], sgn[:, k, a + 1:NW + 2], ALU.subtract))
                c.link(dve.tensor_scalar(cnt[:, a:NW + 1], cnt[:, a:NW + 1], 0.5, None, ALU.mult))
                assert c.n == CN[k]
                dve.wait_ge(counts_summed[k], 2)
                c.link(dve.tensor_copy(tot[:, :], PS[:, 7, 0:NW + 1]))
                c.link(dve.tensor_scalar(tiles_f[:, :], tot[:, :], float(P - 1), None, ALU.add))
                c.link(dve.tensor_copy(tiles_i[:, :], tiles_f[:, :]))
                c.link(dve.tensor_scalar(tiles_i[:, :], tiles_i[:, :], 7, None, ALU.arith_shift_right))
                c.link(dve.tensor_copy(tiles_f[:, :], tiles_i[:, :]))
                c.link(dve.tensor_tensor_scan(tend[:, :], tiles_f[:, :], zeros_e[:, 0:NW + 1], 0.0, ALU.add, ALU.add))
                c.link(dve.tensor_tensor(off[:, :], tend[:, :], tiles_f[:, :], ALU.subtract))
                c.link(dve.memset(off[:, NW:NW + 1], float(T)))
                c.link(dve.tensor_scalar(off[:, :], off[:, :], float(P), -1.0, ALU.mult, ALU.add))
                c.link(dve.tensor_tensor(off[:, :], off[:, :], PS[:, 6, 0:NW + 1], ALU.add))
                if k:
                    dve.wait_ge(tilewin_stored[0], 16)
                c.link(dve.tensor_tensor(ge, rows(tnum[:, :], NW - 1), each(tend[:, 0:NW - 1], TG), ALU.is_ge))
                c.link(dve.tensor_reduce(tcols[:, 0, :], ge, AX.X, ALU.add))
                dve.tensor_copy(wcol[:, :], tcols[:, 0, :]).then_inc(tilewin_ready[k], 1)

            def records(k):
                c, r = cc[k], (raw, raw_s)[k]
                lo = mask[:, 0, :]
                c.link(dve.tensor_scalar(lo, key_i[:, k, :], P - 1, None, ALU.bitwise_and))
                c.inc(dve.tensor_copy(r[:, :, 1], lo))
                c.inc(dve.tensor_copy(r[:, :, 0], key_i[:, 1 - k, :]))
                c.inc(dve.tensor_copy(r[:, :, 2], wgt[:, :]))
                c.wait()

            def place_mask(k, i):
                dve.wait_ge(place_steps[k], i * 3 + H0)
                dve.tensor_scalar(mask[:, 0, :], winf[k][:, :], wnum[:, bass.ds(i, 1)], None, ALU.is_equal).then_inc(place_steps[k], 1)

            def place_scan(k, i):
                dve.wait_ge(place_steps[k], i * 3 + 1 + H0)
                dve.tensor_tensor_scan(scan[:, 0, :], mask[:, 0, :], zeros_e[:, :], off[:, bass.ds(i, 1)],
                                       ALU.add, ALU.add).then_inc(place_steps[k], 1)

            def place_take(k, i):
                dve.wait_ge(place_steps[k], i * 3 + 2 + H0)
                dve.sem_inc(vtaken, 1)
                dve.copy_predicated(posf[:, :], mask[:, 0, :], scan[:, 0, :]).then_inc(place_steps[k], 1)

            def place_end(k):
                c = cc[k]
                lo, hi = mask[:, 0, :], mask[:, 1, :]
                dve.wait_ge(place_steps[k], 3 * (NW + 1) + H0)
                c.link(dve.tensor_copy(pos[:, k, :], posf[:, :]))
                c.inc(dve.tensor_scalar(lo, pos[:, k, :], P - 1, None, ALU.bitwise_and))
                c.link(dve.tensor_scalar(hi, pos[:, k, :], 7, None, ALU.arith_shift_right))
                c.inc(dve.tensor_copy(scan[:, 0, :], lo))
                c.link(dve.tensor_copy(scan[:, 1, :], hi))
                dve.scalar_tensor_tensor(out=pos[:, k, :], in0=scan[:, 0, :], scalar=float(TT), in1=scan[:, 1, :],
                                         op0=ALU.mult, op1=ALU.add).then_inc(pos_ready[k], 1)
                dve.wait_ge(pos_ready[k], 1)

            def long_way():
                records(0)
                with dve.Fori(0, NW + 1) as i:
                    place_mask(0, i)
                    place_scan(0, i)
                    place_take(0, i)
                place_end(0)
                dve.wait_ge(rec_loaded[0], 16)

            def short_way():
                c = Count(dve, short_steps)
                c.link(dve.scalar_tensor_tensor(out=less[:, :], in0=tiles_f[:, 0:NW - 1], scalar=-float(P),
                                                in1=tot[:, 0:NW - 1], op0=ALU.mult, op1=ALU.add))
                c.link(dve.tensor_tensor(gex, ge, each(less[:, :], TG), ALU.mult))
                c.link(dve.tensor_reduce(tcols[:, 1, :], gex, AX.X, ALU.add))
                c.link(dve.scalar_tensor_tensor(out=tcols[:, 1, :], in0=tnum[:, :], scalar=float(P), in1=tcols[:, 1, :],
                                                op0=ALU.mult, op1=ALU.add))
                c.link(dve.tensor_tensor(gex, ge, each(tot[:, 1:NW], TG), ALU.mult))
                c.link(dve.tensor_reduce(tcols[:, 2, :], gex, AX.X, ALU.add))
                c.link(dve.tensor_scalar(tcols[:, 2, :], tcols[:, 2, :], tot[:, 0:1], None, ALU.add))
                c.link(dve.tensor_tensor(tcols[:, 3, :], tcols[:, 2, :], tcols[:, 1, :], ALU.subtract))
                c.link(dve.tensor_copy(first_i[:, :], tcols[:, 1, :]))
                c.link(dve.tensor_scalar(blk_i[:, :], first_i[:, :], 7, None, ALU.arith_shift_right))
                c.link(dve.tensor_copy(tcols[:, 2, :], blk_i[:, :]))
                c.link(dve.tensor_scalar(tcols[:, 2, :], tcols[:, 2, :], float(EB - 1), None, ALU.min))
                c.link(dve.tensor_scalar(shift_i[:, :], first_i[:, :], P - 1, None, ALU.bitwise_and))
                c.link(dve.tensor_copy(blk_i[:, :], tcols[:, 2, :]))
                assert c.n == SHQ
                for b in range(7):
                    c.inc(dve.tensor_scalar(bit_i[:, b, :], shift_i[:, :], 1 << b, None, ALU.bitwise_and))
                c.inc(dve.tensor_tensor(real, each(col[:, :], TG), rows(tcols[:, 3, :], P), ALU.is_lt))
                c.inc(dve.memset(lanes[:, 0, :, :], float(ZROW)))
                c.link(dve.memset(lanes[:, 1, :, :], -1.0))
                dve.wait_ge(blocks_got, 16 * TG)
                for b in range(6, -1, -1):
                    w = P - 1 + (1 << b)
                    for k in range(2):
                        c.inc(dve.copy_predicated(blk[:, :, k, 0:w], rows(bit_i[:, b, :], w), blk[:, :, k, 1 << b:w + (1 << b)]))
                    c.wait()
                c.link(dve.tensor_scalar(blk[:, :, 1, 0:P], blk[:, :, 1, 0:P], P - 1, None, ALU.bitwise_and))
                for k in range(2):
                    c.link(dve.tensor_copy(blkf[:, :, k, P:2 * P], blk[:, :, k, 0:P]))
                for k in range(2):
                    c.link(dve.copy_predicated(lanes[:, k, :, :], real, blkf[:, :, k, P:2 * P]))
                assert c.n == SHL, c.n
                dve.wait_ge(lanes_turned, 1)
                dve.wait_ge(filled, 32)
                for k in range(2):
                    c.link(dve.tensor_copy(rec[0][:, :, k].rearrange("l (p j) -> l j p", j=TG),
                                           psflat[:, k * 1024:k * 1024 + TT].rearrange("l (j p) -> l j p", j=TG)))

            def windows(k, h, i):
                return nc.values_load_multi_w_load_instructions(
                    wtile[k][0:1, cols8(i, h)], engines=[mybir.EngineType.DVE], min_val=0, max_val=NW - 1)[1]

            def one_hots(name, k, h, i, free):
                dve.wait_ge(free[h], i + H0)
                dve.tensor_tensor(oh[:, h, :, :],
                                  col[:, :].rearrange("p (o c) -> p o c", o=1).to_broadcast([P, U, P]),
                                  rec[k][:, cols8(i, h), 1:2].to_broadcast([P, U, P]),
                                  ALU.is_equal).then_inc(onehots_ready[name][h], 1)

            def add_windows(name, h, i, ws, got, width):
                dve.wait_ge(sums_ready[name][h], i + 1 + H0)
                for u in range(U):
                    dve.wait_ge(sums_added[name], i * (2 * U) + (h * U + u) + H0)
                    a = acc[:, bass.ds(ws[u], 1), 0:width]
                    dve.tensor_tensor(a, a, got(h, u), ALU.add).then_inc(sums_added[name], 1)

            def slot(h, u):
                return PS[:, 3 * h + u // 3, (u % 3) * D1:(u % 3 + 1) * D1].rearrange("p (o c) -> p o c", o=1)

            def ahead(name, k, got, width):
                one_hots(name, k, 0, 0, sums_ready[name])

                def turn(i, last=False, rank=False):
                    if rank:
                        place_mask(1, i)
                    for h in range(2):
                        ws = windows(k, h, i)
                        if not (last and h):
                            one_hots(name, k, 1 - h, i + h, sums_ready[name])
                        add_windows(name, h, i, ws, got, width)
                        if rank:
                            (place_scan, place_take)[h](1, i)

                if name == "p1":
                    with dve.Fori(0, NW + 1) as i:
                        turn(i, rank=True)
                with dve.Fori(NW + 1 if name == "p1" else 0, ITERS - 1) as i:
                    turn(i)
                turn(ITERS - 1, last=True)

            z = Count(dve, acc_zero)

            def segsum(name, k):
                if k:
                    dve.wait_ge(rec_loaded[k], 16)
                dve.wait_ge(tilewin_loaded[k], 16)
                z.link(dve.memset(acc[:, :, :], 0.0))
                ahead(name, k, slot, D1)
                dve.wait_ge(sums_added[name], T + H0)

            count(0)
            unsorted = dve.value_load(flag[0:1, 0:1], min_val=0, max_val=1)
            with dve.If(unsorted == 1):
                long_way()
            with dve.Else():
                short_way()
            dve.tensor_copy(gidx[0][:, :], rec[0][:, :, 0]).then_inc(unpacked[0], 1)
            dve.wait_ge(unpacked[0], 1)
            count(1)
            records(1)
            dve.wait_ge(ld_w, 16 * 19)
            dve.tensor_tensor(ph[:, :], ph[:, :], th[:, :], ALU.subtract).then_inc(weights_copied, 1)
            dve.wait_ge(weights_turned, 6)
            wd = Count(dve, weights_copied)
            wd.n = 1
            wd.inc(dve.tensor_copy(wL2T[:, :, :], PS[:, 4, 0:384].rearrange("p (a c) -> p a c", a=3)))
            wd.inc(dve.tensor_copy(thphT[:, 0, :], PS[:, 4, 384:512]))
            wd.inc(dve.tensor_copy(thphT[:, 1, :], PS[:, 5, 0:P]))
            wd.link(dve.tensor_copy(fcT[:, :], PS[:, 5, P:2 * P]))

            def wide(a):
                return a.rearrange("p (j o) -> p j o", o=1).to_broadcast([P, CW, D])

            def brc(a):
                return a[:, :].rearrange("p (o c) -> p o c", o=1).to_broadcast([P, CW, D])

            s3 = s_ring[:, :].rearrange("p (j c) -> p j c", j=CW)
            n3 = n_ring[:, :].rearrange("p (j c) -> p j c", j=CW)
            ps3 = psflat[:, 2048:2048 + C].rearrange("p (j c) -> p j c", j=CW)

            def ln(c, i, sem_a, a_val):
                for j in range(CW):
                    c.inc(dve.bn_stats(lnst[:, j, :], y[:, j, :]))
                c.wait()
                dve.sem_inc(vtaken, 1)
                for j in range(CW):
                    c.inc(dve.bn_aggr(lnmv[:, j, :], lnst[:, j, :]))
                dve.wait_ge(sem_a, a_val)
                c.link(dve.reciprocal(lnrs[:, :], lnsd[:, :]))
                for j in range(CW):
                    c.inc(dve.tensor_scalar(cur[:, bass.ds(i * CW + j, 1), :], y[:, j:j + 1, :], lnmv[:, j, 0:1],
                                            lnrs[:, j:j + 1], ALU.subtract, ALU.mult))
                c.wait()

            dve.wait_ge(table_filled, 32)
            segsum("p1", 0)
            place_end(1)
            dv = Count(dve, n_pass["A"])
            dv.link(dve.tensor_copy(deg_dst[:, :], acc[:, :, D]))
            with dve.Fori(0, NCH) as i:
                c = Count(dve, node_v["A"], 2, i)
                ch = bass.ds(i * CW, CW)
                dve.wait_ge(node_p["A"], i * 3 + H0)
                c.inc(dve.tensor_tensor(s3, x0[:, ch, :], acc[:, ch, 0:D], ALU.add))
                dve.wait_ge(node_p["A"], i * 3 + 3 + H0)
                dve.wait_ge(node_a["A"], i * 3 + H0)
                c.inc(dve.tensor_tensor(y[:, :, :], ps3, brc(brow[0]), ALU.add))
            dve.wait_ge(node_a["A"], 3 * NCH + H0)
            segsum("p2", 0)
            with dve.Fori(0, NCH) as i:
                c = Count(dve, node_v["B"], KB, i)
                ch = bass.ds(i * CW, CW)
                dve.wait_ge(node_p["B"], i * 3 + H0)
                c.inc(dve.tensor_tensor(s3, cur[:, ch, :], acc[:, ch, 0:D], ALU.add))
                dve.wait_ge(node_p["B"], i * 3 + 3 + H0)
                c.link(dve.tensor_tensor(y[:, :, :], ps3, brc(brow[1]), ALU.add))
                c.link(dve.tensor_tensor(y[:, :, :], y[:, :, :], x0[:, ch, :], ALU.add))
                ln(c, i, node_a["B"], i * 3 + (3 + H0))
                assert c.n == KB
            dve.wait_ge(node_v["B"], KB * NCH)

            def reciprocal_degree(cc, deg):
                cc.link(dve.tensor_scalar(rdeg[:, :], deg[:, :], 1.0, None, ALU.max))
                cc.link(dve.reciprocal(rdeg[:, :], rdeg[:, :]))

            def sage(p, out_of):
                def inputs(i):
                    ch = bass.ds(i * CW, CW)
                    dve.wait_ge(sage_turned, i * 2 + 2 * chunks_before[p])
                    dve.sem_inc(vtaken, 1)
                    dve.tensor_copy(s3, cur[:, ch, :]).then_inc(sage_in, 1)
                    dve.tensor_tensor(n3, acc[:, ch, 0:D],
                                      rdeg[:, ch].rearrange("p (j o) -> p j o", o=1).to_broadcast([P, CW, D]),
                                      ALU.mult).then_inc(sage_in, 1)

                def outputs(i):
                    dve.wait_ge(sage_product, i + (chunks_before[p] + 1))
                    out_of(i)

                inputs(0)
                with dve.Fori(0, NCH - 1) as i:
                    inputs(i + 1)
                    outputs(i)
                outputs(NCH - 1)

            segsum("p3", 1)
            dv = Count(dve, n_pass["C"])
            dv.link(dve.tensor_copy(deg_src[:, :], acc[:, :, D]))
            reciprocal_degree(dv, deg_src)

            def out_c(i):
                c = Count(dve, node_v["C"], KC, i)
                dve.tensor_tensor(y[:, :, :], ps3, brc(bL1), ALU.add).then_inc(sage_biased, 1)
                dve.wait_ge(sage_biased, i + 1 + H0)
                c.link(dve.tensor_tensor(y[:, :, :], y[:, :, :], cur[:, bass.ds(i * CW, CW), :], ALU.add))
                ln(c, i, node_a["C"], i + 1)
                assert c.n == KC

            sage("C", out_c)
            dve.wait_ge(node_v["C"], KC * NCH)
            segsum("p4", 0)
            dv = Count(dve, n_pass["D"])
            reciprocal_degree(dv, deg_dst)

            def out_d(i):
                dve.wait_ge(node_a["D"], i + H0)
                dve.tensor_tensor(y[:, :, :], ps3, brc(bL2), ALU.add).then_inc(sage_biased, 1)

            sage("D", out_d)
            dve.wait_ge(node_a["D"], NCH + H0)
            c = Count(dve, norm_v)
            c.link(dve.tensor_scalar(x0[:, NW - 1, :], x0[:, NW - 1, :], small[:, 20:21], None, ALU.mult))
            dve.wait_ge(norm_squared, NCH + H0)
            c.link(dve.tensor_reduce(small[:, 7:8], dsum[:, :], AX.X, ALU.add))
            dve.wait_ge(norm_a, 1)
            c.link(dve.reciprocal(small[:, 10:11], small[:, 4:5]))

            def x3_chunk(i):
                c = Count(dve, x3_steps, KD2, i)
                ch = bass.ds(i * CW, CW)
                c.link(dve.scalar_tensor_tensor(out=y[:, :, :], in0=x0[:, ch, :], scalar=small[:, 10:11],
                                                in1=cur[:, ch, :], op0=ALU.mult, op1=ALU.add))
                ln(c, i, x3_sqrt, i + 1)
                dve.wait_ge(x3_turned, i)
                dve.sem_inc(vtaken, 1)
                c.inc(dve.tensor_copy(s3, cur[:, ch, :]))
                assert c.n == KD2

            x3_chunk(0)
            with dve.Fori(1, NCH) as i:
                x3_chunk(i)
            z.link(dve.memset(acc[:, :, :], 0.0))
            c = Count(dve, bn_v)
            dve.wait_ge(mean_added, NCH + H0)
            c.link(dve.tensor_copy(mu0, psflat[:, 3072:3073]))
            dve.wait_ge(ab_split, 3 * NCH)
            dve.wait_ge(table_stored["E"], 16 * NCH + H0)
            c.link(dve.tensor_scalar(mfc, mu0, 1.0 / E, None, ALU.mult))
            c.inc(dve.tensor_scalar(diag[:, :], ident[:, :], mfc, None, ALU.mult))
            dve.wait_ge(bn_p, 1)
            c.link(dve.tensor_tensor(x0[:, :, :], x0[:, :, :],
                                     PS[:, 7, 0:P].rearrange("p (o c) -> p o c", o=1).to_broadcast([P, NW, D]),
                                     ALU.subtract))
            with dve.Fori(0, ITERS) as i:
                for h in range(2):
                    ws = windows(0, h, i)
                    one_hots("p5", 0, h, i, oh_turned)
                    dve.wait_ge(e_summed[h], i + H0)
                    for u in range(U):
                        dve.tensor_copy(abuf[:, h, u:u + 1, :], x0[:, bass.ds(ws[u], 1), :]).then_inc(a_copied[h], 1)
            for h in range(2):
                dve.wait_ge(e_squared[h], ITERS + H0)
            c.link(dve.tensor_reduce(small[:, 11:12], sq[:, :], AX.X, ALU.add))
            c.link(dve.tensor_scalar(small[:, 6:7], small[:, 11:12], 1.0 / E, None, ALU.mult))
            assert c.n == 6
            dve.wait_ge(bn_a, 1)
            c.link(dve.reciprocal(small[:, 12:13], small[:, 5:6]))
            c.link(dve.tensor_tensor(scale0, small[:, 12:13], bn[:, 0:1], ALU.mult))
            dve.wait_ge(bn_p, 2)
            c.link(dve.tensor_copy(small[:, 13:14], PS[:, 7, 0:1]))
            with dve.Fori(0, ITERS) as i:
                for h in range(2):
                    dve.wait_ge(y_product[h], i + 1)
                    for s in range(2):
                        dve.bn_stats(stats[:, bass.ds(i * 4 + (2 * h + s), 1), :], PS[:, 2 * h + s, :]).then_inc(y_stats[h], 1)
            for h in range(2):
                dve.wait_ge(y_stats[h], 2 * ITERS + H0)
            c.link(dve.bn_aggr(small[:, 16:18], stats[:, :, :].rearrange("p a b -> p (a b)")))
            EMPTY = SLOTS - E
            c.link(dve.tensor_tensor(small[:, 18:19], small[:, 16:17], small[:, 13:14], ALU.subtract))
            c.link(dve.scalar_tensor_tensor(out=small[:, 19:20], in0=small[:, 18:19], scalar=EMPTY / E,
                                            in1=small[:, 16:17], op0=ALU.mult, op1=ALU.add))
            c.link(dve.tensor_tensor(small[:, 18:19], small[:, 13:14], small[:, 19:20], ALU.subtract))
            c.link(dve.tensor_tensor(small[:, 18:19], small[:, 18:19], small[:, 18:19], ALU.mult))
            c.link(dve.tensor_scalar(small[:, 21:22], small[:, 17:18], SLOTS / E, None, ALU.mult))
            c.link(dve.scalar_tensor_tensor(out=small[:, 14:15], in0=small[:, 18:19], scalar=-EMPTY / SLOTS,
                                            in1=small[:, 21:22], op0=ALU.mult, op1=ALU.add))
            assert c.n == BNV, c.n
            dve.wait_ge(bn_a, 3)
            t = Count(dve, norm_v)
            t.n = 3
            t.link(dve.reciprocal(small[:, 22:23], small[:, 15:16]))
            t.link(dve.tensor_tensor(small[:, 22:23], small[:, 22:23], bn[:, 2:3], ALU.mult))
            t.link(dve.tensor_tensor(small[:, 23:24], small[:, 22:23], small[:, 19:20], ALU.mult))
            c.link(dve.tensor_scalar(fcs[:, :], fc[:, :], small[:, 22:23], None, ALU.mult))
            t.link(dve.tensor_tensor(sh1, bn[:, 3:4], small[:, 23:24], ALU.subtract))
            t.link(dve.tensor_copy(shcol[:, 0:1], sh1))
            t.link(dve.tensor_copy(small[:, 24:25], shcol[:, 0:1]))
            t.link(dve.tensor_tensor(small[:, 27:28], sh1, small[:, 24:25], ALU.subtract))
            t.link(dve.tensor_copy(shcol[:, 1:2], small[:, 27:28]))
            t.link(dve.tensor_copy(small[:, 25:26], shcol[:, 1:2]))
            c.link(dve.tensor_tensor(small[:, 26:27], small[:, 27:28], small[:, 25:26], ALU.subtract))
            dve.wait_ge(bn_p, 4)
            c.link(dve.tensor_copy(fcsT[:, :], PS[:, 6, 0:P]))
            c.link(dve.tensor_copy(shrow[:, :].rearrange("p (n c) -> p n c", n=4),
                                   PS[0:3, 6, P:2 * P].rearrange("p (o c) -> p o c", o=1).to_broadcast([3, 4, D])))
            def pc_turn(i, last=False):
                one_hots("pc", 0, 1, i, sums_ready["pc"])
                ws = windows(0, 0, i)
                dve.wait_ge(sums_ready["pc"][0], i + 1 + H0)
                for u in range(U):
                    dve.wait_ge(sums_added["pc"], i * U + u + H0)
                    a = acc[:, bass.ds(ws[u], 1), 0:D]
                    g = PS[:, 4 + u // 4, (u % 4) * P:(u % 4 + 1) * P].rearrange("p (o c) -> p o c", o=1)
                    dve.tensor_tensor(a, a, g, ALU.add).then_inc(sums_added["pc"], 1)
                if not last:
                    one_hots("pc", 0, 0, i + 1, sums_ready["pc"])

            one_hots("pc", 0, 0, 0, sums_ready["pc"])
            with dve.Fori(0, ITERS - 1) as i:
                pc_turn(i)
            pc_turn(ITERS - 1, last=True)
            dve.wait_ge(sums_added["pc"], ITERS * U + H0)
            dve.wait_ge(acc2_added, ITERS * U + H0)
            with dve.Fori(0, NCH) as i:
                c = Count(dve, node_v["F"], KF, i)
                ch = bass.ds(i * CW, CW)
                c.link(dve.tensor_tensor(n3, acc[:, ch, 0:D], acc2[:, ch, :], ALU.add))
                c.link(dve.tensor_tensor(n3, n3,
                                         rdeg[:, ch].rearrange("p (j o) -> p j o", o=1).to_broadcast([P, CW, D]), ALU.mult))
                c.link(dve.tensor_tensor(n3, n3, cur[:, ch, :], ALU.add))
                c.link(dve.scalar_tensor_tensor(out=y[:, :, :], in0=n3, scalar=0.0, in1=cur[:, ch, :],
                                                op0=ALU.max, op1=ALU.add))
                ln(c, i, node_a["F"], i + 1)
                assert c.n == KF


_INS = ["x", "src", "dst", "edge_weight1", "L0_gnn_W1", "L0_gnn_b1", "L0_gnn_W2", "L0_gnn_b2", "L0_gnn_W3", "L0_gnn_b3",
        "L0_gnn_W4", "L0_gnn_b4", "L1_gnn_W", "L1_gnn_b", "L2_gnn_W", "L2_gnn_b", "L3_gnn_theta_w", "L3_gnn_phi_w",
        "L3_gnn_fc1_w", "L3_gnn_bn0_g", "L3_gnn_bn0_b", "L3_gnn_bn1_g", "L3_gnn_bn1_b"]


def kernel(**inputs):
    import numpy as np
    import concourse.bacc as bacc
    from concourse import mybir as mb
    from concourse.bass_utils import run_bass_kernel_spmd

    nc = bacc.Bacc("TRN2", target_bir_lowering=False, num_devices=1)
    arrays, args = {}, []
    for name in _INS:
        a = np.ascontiguousarray(inputs[name])
        arrays[f"in_{name}"] = a
        args.append(nc.dram_tensor(f"in_{name}", a.shape, mb.dt.from_np(a.dtype), kind="ExternalInput").ap())
    shape = inputs["x"].shape
    args.append(nc.dram_tensor("result", shape, mb.dt.float32, kind="ExternalOutput").ap())
    gnn_kernel(nc, *args)
    r = run_bass_kernel_spmd(nc, [arrays], core_ids=[0])
    return np.asarray(r.results[0]["result"]).reshape(shape)
```
